# Optimizing a Trainium2 kernel written in Bass

```python
import numpy as np
import jax
import jax.numpy as jnp

def _softmax(x, axis=-1):
    return jax.nn.softmax(x, axis=axis)

def _gelu(x):
    return jax.nn.gelu(x, approximate=True)

def _silu(x):
    return jax.nn.silu(x)

def _sigmoid(x):
    return jax.nn.sigmoid(x)

def _layernorm(x, axis=-1, eps=1e-05):
    m = jnp.mean(x, axis=axis, keepdims=True)
    v = jnp.var(x, axis=axis, keepdims=True)
    return (x - m) / jnp.sqrt(v + eps)

def _scatter_add(tgt, idx, src, axis=0):
    return tgt.at[idx].add(src)

def _segment_sum(src, seg, n):
    return jax.ops.segment_sum(src, seg, n)
kernel_name = 'mk_sandwich_d1_jaxref_r4_37f604'

def setup_inputs(seed: int=0):
    np.random.seed(seed)
    _w = jnp.asarray

    def _L0_attn_setup():
        import jax, jax.numpy as jnp
        import numpy as np
        B, S, D = (8, 512, 256)
        key = jax.random.key(seed)
        x = jax.random.normal(key, (B, S, D), dtype=jnp.float32)
        return {'x': x}
    _L0_attn_in = _L0_attn_setup()

    def _L0_ffn_setup():
        import jax, jax.numpy as jnp
        import numpy as np
        DIM = 256
        DEPTH = 2
        HEADS = 8
        DIM_HEAD = 64
        WINDOW = 128
        INNER = HEADS * DIM_HEAD
        HID = int(DIM * 4 * 2 / 3)
        B, N = (2, 2048)
        QK_SCALE = 8.0

        def shift_token(t):
            t1, t2 = jnp.split(t, 2, axis=-1)
            t2 = jnp.pad(t2, ((0, 0), (1, 0), (0, 0)))[:, :-1]
            return jnp.concatenate([t1, t2], axis=-1)

        def l2norm(t):
            return t / jnp.clip(jnp.linalg.norm(t, axis=-1, keepdims=True), 1e-12)

        def rotate_half(x):
            x1, x2 = jnp.split(x, 2, axis=-1)
            return jnp.concatenate([-x2, x1], axis=-1)

        def rotary_xpos(q, k):
            n = q.shape[-2]
            half_idx = jnp.arange(0, DIM_HEAD, 2, dtype=jnp.float32)
            inv_freq = 1.0 / 10000.0 ** (half_idx / DIM_HEAD)
            t = jnp.arange(n, dtype=jnp.float32)
            freqs = t[:, None] * inv_freq[None, :]
            freqs = jnp.concatenate([freqs, freqs], axis=-1)
            base = (half_idx + 0.4 * DIM_HEAD) / (1.4 * DIM_HEAD)
            power = (t - n // 2) / float(WINDOW // 2)
            scale = base[None, :] ** power[:, None]
            scale = jnp.concatenate([scale, scale], axis=-1)
            cos, sin = (jnp.cos(freqs), jnp.sin(freqs))
            q = q * cos * scale + rotate_half(q) * sin * scale
            k = k * cos / scale + rotate_half(k) * sin / scale
            return (q, k)

        def local_attention(q, k, v):
            b, h, n, d = q.shape
            w = n // WINDOW
            bq = q.reshape(b, h, w, WINDOW, d) * QK_SCALE
            bk = k.reshape(b, h, w, WINDOW, d)
            bv = v.reshape(b, h, w, WINDOW, d)

            def look_around(t):
                p = jnp.pad(t, ((0, 0), (0, 0), (1, 0), (0, 0), (0, 0)))
                return jnp.concatenate([p[:, :, :w], p[:, :, 1:]], axis=3)
            bk, bv = (look_around(bk), look_around(bv))
            bt = jnp.arange(n).reshape(w, WINDOW)
            btp = jnp.pad(bt, ((1, 0), (0, 0)), constant_values=-1)
            btk = jnp.concatenate([btp[:w], btp[1:]], axis=1)
            sim = jnp.einsum('bhwid,bhwjd->bhwij', bq, bk)
            i = bt[:, :, None]
            j = btk[:, None, :]
            mask = (i < j) | (i > j + WINDOW) | (j == -1)
            sim = jnp.where(mask, -jnp.finfo(sim.dtype).max, sim)
            attn = jax.nn.softmax(sim, axis=-1)
            out = jnp.einsum('bhwij,bhwjd->bhwid', attn, bv)
            return out.reshape(b, h, n, d)

        def _layer(x, wqkv, qs, ksc, wo, lg, lb, w1, b1, w2, b2):
            b, n, _ = x.shape
            h = shift_token(x)
            qkv = h @ wqkv
            q, k, v = jnp.split(qkv, 3, axis=-1)
            to_heads = lambda t: t.reshape(b, n, HEADS, DIM_HEAD).transpose(0, 2, 1, 3)
            q, k, v = (to_heads(q), to_heads(k), to_heads(v))
            q = l2norm(q) * qs
            k = l2norm(k) * ksc
            q, k = rotary_xpos(q, k)
            o = local_attention(q, k, v)
            o = o.transpose(0, 2, 1, 3).reshape(b, n, INNER)
            x = x + o @ wo
            h = shift_token(x)
            mu = h.mean(-1, keepdims=True)
            var = h.var(-1, keepdims=True)
            h = (h - mu) / jnp.sqrt(var + 1e-05) * lg + lb
            h = h @ w1 + b1
            a, g = jnp.split(h, 2, axis=-1)
            h = a * jax.nn.gelu(g, approximate=False)
            x = x + h @ w2 + b2
            return x
        key = jax.random.key(seed)
        ks = jax.random.split(key, 6)
        return {'x': jax.random.normal(ks[0], (B, N, DIM), jnp.float32), 'wqkv': jax.random.normal(ks[1], (DEPTH, DIM, 3 * INNER), jnp.float32) * 0.02, 'q_scale': jnp.ones((DEPTH, DIM_HEAD), jnp.float32), 'k_scale': jnp.ones((DEPTH, DIM_HEAD), jnp.float32), 'wo': jax.random.normal(ks[2], (DEPTH, INNER, DIM), jnp.float32) * 0.02, 'ln_g': jnp.ones((DEPTH, DIM), jnp.float32), 'ln_b': jnp.zeros((DEPTH, DIM), jnp.float32), 'w1': jax.random.normal(ks[3], (DEPTH, DIM, 2 * HID), jnp.float32) * 0.02, 'b1': jnp.zeros((DEPTH, 2 * HID), jnp.float32), 'w2': jax.random.normal(ks[4], (DEPTH, HID, DIM), jnp.float32) * 0.02, 'b2': jnp.zeros((DEPTH, DIM), jnp.float32)}
    _L0_ffn_in = _L0_ffn_setup()
    _d = {'L0_attn_x': _L0_attn_in['x'], 'L0_ffn_wqkv': _L0_ffn_in['wqkv'], 'L0_ffn_q_scale': _L0_ffn_in['q_scale'], 'L0_ffn_k_scale': _L0_ffn_in['k_scale'], 'L0_ffn_wo': _L0_ffn_in['wo'], 'L0_ffn_ln_g': _L0_ffn_in['ln_g'], 'L0_ffn_ln_b': _L0_ffn_in['ln_b'], 'L0_ffn_w1': _L0_ffn_in['w1'], 'L0_ffn_b1': _L0_ffn_in['b1'], 'L0_ffn_w2': _L0_ffn_in['w2'], 'L0_ffn_b2': _L0_ffn_in['b2']}
    _x0 = _d['L0_attn_x']
    _d['L0_attn_x'] = jax.random.normal(jax.random.fold_in(jax.random.key(seed), 1), (4, 2048, 256), dtype=_x0.dtype)
    del _x0
    return _d

def reference(L0_attn_x, L0_ffn_wqkv, L0_ffn_q_scale, L0_ffn_k_scale, L0_ffn_wo, L0_ffn_ln_g, L0_ffn_ln_b, L0_ffn_w1, L0_ffn_b1, L0_ffn_w2, L0_ffn_b2):

    def _L0_attn_ref(x):
        import jax, jax.numpy as jnp
        import numpy as np
        B, S, D = (8, 512, 256)
        scores = jnp.einsum('bid,bjd->bij', x, x)
        attn = jax.nn.softmax(scores, axis=1)
        context = jnp.einsum('bij,bjd->bid', attn, x)
        return context

    def _L0_ffn_ref(x, wqkv, q_scale, k_scale, wo, ln_g, ln_b, w1, b1, w2, b2):
        import jax, jax.numpy as jnp
        import numpy as np
        DIM = 256
        DEPTH = 2
        HEADS = 8
        DIM_HEAD = 64
        WINDOW = 128
        INNER = HEADS * DIM_HEAD
        HID = int(DIM * 4 * 2 / 3)
        B, N = (2, 2048)
        QK_SCALE = 8.0

        def shift_token(t):
            t1, t2 = jnp.split(t, 2, axis=-1)
            t2 = jnp.pad(t2, ((0, 0), (1, 0), (0, 0)))[:, :-1]
            return jnp.concatenate([t1, t2], axis=-1)

        def l2norm(t):
            return t / jnp.clip(jnp.linalg.norm(t, axis=-1, keepdims=True), 1e-12)

        def rotate_half(x):
            x1, x2 = jnp.split(x, 2, axis=-1)
            return jnp.concatenate([-x2, x1], axis=-1)

        def rotary_xpos(q, k):
            n = q.shape[-2]
            half_idx = jnp.arange(0, DIM_HEAD, 2, dtype=jnp.float32)
            inv_freq = 1.0 / 10000.0 ** (half_idx / DIM_HEAD)
            t = jnp.arange(n, dtype=jnp.float32)
            freqs = t[:, None] * inv_freq[None, :]
            freqs = jnp.concatenate([freqs, freqs], axis=-1)
            base = (half_idx + 0.4 * DIM_HEAD) / (1.4 * DIM_HEAD)
            power = (t - n // 2) / float(WINDOW // 2)
            scale = base[None, :] ** power[:, None]
            scale = jnp.concatenate([scale, scale], axis=-1)
            cos, sin = (jnp.cos(freqs), jnp.sin(freqs))
            q = q * cos * scale + rotate_half(q) * sin * scale
            k = k * cos / scale + rotate_half(k) * sin / scale
            return (q, k)

        def local_attention(q, k, v):
            b, h, n, d = q.shape
            w = n // WINDOW
            bq = q.reshape(b, h, w, WINDOW, d) * QK_SCALE
            bk = k.reshape(b, h, w, WINDOW, d)
            bv = v.reshape(b, h, w, WINDOW, d)

            def look_around(t):
                p = jnp.pad(t, ((0, 0), (0, 0), (1, 0), (0, 0), (0, 0)))
                return jnp.concatenate([p[:, :, :w], p[:, :, 1:]], axis=3)
            bk, bv = (look_around(bk), look_around(bv))
            bt = jnp.arange(n).reshape(w, WINDOW)
            btp = jnp.pad(bt, ((1, 0), (0, 0)), constant_values=-1)
            btk = jnp.concatenate([btp[:w], btp[1:]], axis=1)
            sim = jnp.einsum('bhwid,bhwjd->bhwij', bq, bk)
            i = bt[:, :, None]
            j = btk[:, None, :]
            mask = (i < j) | (i > j + WINDOW) | (j == -1)
            sim = jnp.where(mask, -jnp.finfo(sim.dtype).max, sim)
            attn = jax.nn.softmax(sim, axis=-1)
            out = jnp.einsum('bhwij,bhwjd->bhwid', attn, bv)
            return out.reshape(b, h, n, d)

        def _layer(x, wqkv, qs, ksc, wo, lg, lb, w1, b1, w2, b2):
            b, n, _ = x.shape
            h = shift_token(x)
            qkv = h @ wqkv
            q, k, v = jnp.split(qkv, 3, axis=-1)
            to_heads = lambda t: t.reshape(b, n, HEADS, DIM_HEAD).transpose(0, 2, 1, 3)
            q, k, v = (to_heads(q), to_heads(k), to_heads(v))
            q = l2norm(q) * qs
            k = l2norm(k) * ksc
            q, k = rotary_xpos(q, k)
            o = local_attention(q, k, v)
            o = o.transpose(0, 2, 1, 3).reshape(b, n, INNER)
            x = x + o @ wo
            h = shift_token(x)
            mu = h.mean(-1, keepdims=True)
            var = h.var(-1, keepdims=True)
            h = (h - mu) / jnp.sqrt(var + 1e-05) * lg + lb
            h = h @ w1 + b1
            a, g = jnp.split(h, 2, axis=-1)
            h = a * jax.nn.gelu(g, approximate=False)
            x = x + h @ w2 + b2
            return x
        for l in range(DEPTH):
            x = _layer(x, wqkv[l], q_scale[l], k_scale[l], wo[l], ln_g[l], ln_b[l], w1[l], b1[l], w2[l], b2[l])
        return x
    x = L0_attn_x
    x = x + _layernorm(_L0_attn_ref(_layernorm(x, axis=-1)), axis=-1)
    x = x + _layernorm(_L0_ffn_ref(_layernorm(x, axis=-1), L0_ffn_wqkv, L0_ffn_q_scale, L0_ffn_k_scale, L0_ffn_wo, L0_ffn_ln_g, L0_ffn_ln_b, L0_ffn_w1, L0_ffn_b1, L0_ffn_w2, L0_ffn_b2), axis=-1)
    return x

_drawn_inputs = setup_inputs


def setup_inputs(seed=0):
    import zlib

    import numpy as np

    out = dict(_drawn_inputs(seed))
    spreads = {'L0_ffn_q_scale': (1.0, 0.6),
     'L0_ffn_k_scale': (1.0, 0.6),
     'L0_ffn_ln_g': (1.0, 0.6),
     'L0_ffn_ln_b': (0.0, 0.8),
     'L0_ffn_b1': (0.0, 0.8),
     'L0_ffn_b2': (0.0, 0.454)}
    factors = {'L0_ffn_wqkv': 5.398, 'L0_ffn_wo': 5.306, 'L0_ffn_w1': 3.491, 'L0_ffn_w2': 3.477}
    for name, (base, spread) in spreads.items():
        noise = np.random.default_rng([zlib.crc32(name.encode()), seed]).standard_normal(out[name].shape)
        drawn = base * np.exp(spread * noise) if base else spread * noise
        out[name] = jnp.asarray(drawn.astype(out[name].dtype))
    for name, factor in factors.items():
        out[name] = (out[name] * factor).astype(out[name].dtype)
    return out
```

```python
from contextlib import ExitStack

import numpy as np

import concourse.bass as bass
import concourse.mybir as mybir

F32, F32R = mybir.dt.float32, mybir.dt.float32r
F16, BF16, I32 = mybir.dt.float16, mybir.dt.bfloat16, mybir.dt.int32
ALU = mybir.AluOpType
ACT = mybir.ActivationFunctionType
AX = mybir.AxisListType
RED_MAX = bass.bass_isa.ReduceOp.max
ds = bass.ds

P = 128
B, S, D = 4, 2048, 256
KD = D // P
WPB = S // P
NW = B * WPB
LAYERS, HEADS, DH = 2, 8, 64
INNER = HEADS * DH
HP = HEADS // 2
HID = int(D * 4 * 2 / 3)
HC = -(-HID // P)
HPAD = HC * P
EPS = 1e-5
QK_SCALE = 8.0
MASKED, ABOVE_ALL = 1e30, 3e38
EVEN_MASK, ODD_MASK = 3, 4
XS_SCALE = 2.0 ** 9
W1_TOP = 2.0 ** 13
NT = LAYERS * NW
BLOCKS_PER_BATCH = WPB + 1
XS_BLOCKS = (NT + NW) + (NT + NW) // WPB
XP_BLOCKS = NT + NT // WPB
SLOTS = 4
LAST_SLOT = NT + 4
FIRST_GROUP = 2
LAST_GROUP = NT // SLOTS - 1
W1_BANKS = (0, 1, 3, 4, 5, 6)


def wait(eng, sem, count):
    if not (isinstance(count, int) and count <= 0):
        eng.wait_ge(sem, count)


def wait_apart(eng, sem, count, passed):
    if not (isinstance(count, int) and count <= 0):
        eng.wait_ge(sem, count)
        eng.sem_inc(passed, 1)


def stream_block(t):
    return t + t // WPB + 1


def phase_a(nc, x_in, ident_in, x2_dram, xs_dram, xp_dram):
    x_v = x_in.rearrange("b (w p) d -> p (b w) d", p=P)
    x2_v = x2_dram.rearrange("(w p) d -> p w d", p=P)
    xs_v = xs_dram.rearrange("(w p) d -> p w d", p=P)
    chunks = S // 512
    e_full_start = 2
    ctx_free_start = 4
    e_lo_start = 1
    xs_lo_start = 1
    xs_full_start = 2
    with ExitStack() as ctx:
        def sb(name, shape, dt=F32):
            return ctx.enter_context(nc.sbuf_tensor("a_" + name, shape, dt))

        def sem(name):
            return ctx.enter_context(nc.semaphore("a_" + name))

        ident_f = sb("ident_f", [P, P])
        ident = sb("ident", [P, P], F16)
        xn = sb("xn", [P, WPB, D])
        xn_hl = sb("xn_hl", [P, 2, 2, D], F16)
        xnT = sb("xnT", [P, 2, KD, S], F16)
        E = sb("E", [P, 2, WPB, S], F16)
        e32 = sb("e32", [P, S])
        xs32 = sb("xs32", [P, D])
        xs = sb("xs", [P, 2, WPB, D], F16)
        negmax = sb("negmax", [P, 2])
        colsum = sb("colsum", [P, 2])
        colsum_s = sb("colsum_s", [P, 2])
        inv_sum = sb("inv_sum", [P, 2])
        st_n, mv_n, var_n, rstd_n = sb("st_n", [P, 6]), sb("mv_n", [P, 2]), sb("var_n", [P, 1]), sb("rstd_n", [P, 1])
        st_c, mv_c, var_c = sb("st_c", [P, 6]), sb("mv_c", [P, 2]), sb("var_c", [P, 1])
        pow_c, rstd_c = sb("pow_c", [P, 1]), sb("rstd_c", [P, 1])
        st_x, mv_x, var_x, rstd_x = sb("st_x", [P, 6]), sb("mv_x", [P, 2]), sb("var_x", [P, 1]), sb("rstd_x", [P, 1])
        mhalf = sb("mhalf", [P, 1])
        unscale = sb("unscale", [P, 1])
        x_res = sb("x_res", [P, 2, D])
        ln_c = sb("ln_c", [P, D])
        x2 = sb("x2", [P, 2, D])
        xo = sb("xo", [P, 2, D])
        zeros = sb("zeros", [3 * B, D])
        ps = ctx.enter_context(nc.psum_tensor("a_ps", [P, 8, 512], F32))
        ps_tr = [ps[:, 4 + i, 0:256].bitcast(F16).rearrange("p (h k n) -> p h k n", h=2, k=KD) for i in range(2)]

        consts_in, consts, pool_consts, x_loaded = sem("consts_in"), sem("consts"), sem("pool_consts"), sem("x_loaded")
        stn, mvn, varn_ready, rstdn_ready, xn_ready, xn_hi, xn_lo = (sem(n) for n in (
            "stn", "mvn", "varn_ready", "rstdn_ready", "xn_ready", "xn_hi", "xn_lo"))
        trans_done, xnT_ready = sem("trans_done"), sem("xnT_ready")
        scores_done, max_ready, e_hi, e_full, e_lo = (sem(n) for n in (
            "scores_done", "max_ready", "e_hi", "e_full", "e_lo"))
        sum_scaled, inv_ready, xs_full, xs_hi, xs_lo = (sem(n) for n in (
            "sum_scaled", "inv_ready", "xs_full", "xs_hi", "xs_lo"))
        ctx_done, stc, mvc, varc_ready, powc, rstdc_ready, ctx_free = (sem(n) for n in (
            "ctx_done", "stc", "mvc", "varc_ready", "powc", "rstdc_ready", "ctx_free"))
        x2_ready, stx, mvx, varx_ready, rstdx_ready, xo_ready = (sem(n) for n in (
            "x2_ready", "stx", "mvx", "varx_ready", "rstdx_ready", "xo_ready"))
        res_in = [sem(f"res_in{i}") for i in range(2)]
        x2_out = [sem(f"x2_out{i}") for i in range(2)]
        xo_out = [sem(f"xo_out{i}") for i in range(2)]
        zero_rows = sem("zero_rows")
        passed_dve, passed_pe = sem("passed_dve"), sem("passed_pe")
        block = ctx.enter_context(nc.Block())

        @block.sync
        def _(sp):
            sp.dma_start(ident_f[:], ident_in).then_inc(consts_in, 16)
            sp.dma_start(xn[:], x_v[:, 0:WPB, :]).then_inc(x_loaded, 16)
            for u in range(2):
                sp.sem_inc(x2_out[u], 16)
                sp.sem_inc(xo_out[u], 16)
            sp.sem_inc(e_full, e_full_start)
            sp.sem_inc(ctx_free, ctx_free_start)
            sp.sem_inc(e_lo, e_lo_start)
            sp.sem_inc(xs_lo, xs_lo_start)
            sp.sem_inc(xs_full, xs_full_start)
            sp.wait_ge(pool_consts, 1)
            rows = BLOCKS_PER_BATCH * P
            sp.dma_start(xs_dram.rearrange("(q r) d -> q r d", r=rows)[:, P - 1, :], zeros[:]).then_inc(zero_rows, 16)
            sp.dma_start(xp_dram.rearrange("(q r) d -> q r d", r=rows)[:, P - 1, :], zeros[0:2 * B, :]).then_inc(zero_rows, 16)
            for u in range(2):
                sp.dma_start(x_res[:, u, :], x_v[:, u, :]).then_inc(res_in[u], 16)
            with sp.Fori(0, B) as b:
                sp.wait_ge(xs_full, xs_full_start + (b + 1) * WPB)
                sp.dma_start(xn[:], x_v[:, ds(((b + 1) % B) * WPB, WPB), :]).then_inc(x_loaded, 16)
                with sp.Fori(0, WPB // 2) as h:
                    for u in range(2):
                        g = b * WPB + 2 * h + u
                        sp.wait_ge(xo_ready, g + 1)
                        sp.dma_start(x2_v[:, ds(g, 1), :], x2[:, u, :]).then_inc(x2_out[u], 16)
                        sp.dma_start(xs_v[:, ds(stream_block(g), 1), :], xo[:, u, :]).then_inc(xo_out[u], 16)
                        sp.dma_start(x_res[:, u, :], x_v[:, ds((g + 2) % NW, 1), :]).then_inc(res_in[u], 16)
            for u in range(2):
                sp.wait_ge(x2_out[u], 16 * (NW // 2 + 1))
                sp.wait_ge(xo_out[u], 16 * (NW // 2 + 1))
                sp.wait_ge(res_in[u], 16 * (NW // 2 + 1))
            sp.wait_ge(zero_rows, 32)
            sp.wait_ge(x_loaded, 16 * (B + 1))

        @block.gpsimd
        def _(pool):
            nc.gpsimd.memset(mhalf[:], -0.5)
            nc.gpsimd.memset(unscale[:], 1.0 / XS_SCALE)
            nc.gpsimd.memset(zeros[:], 0.0).then_inc(pool_consts, 1)
            pool.wait_ge(pool_consts, 1)

            def prep(n, u):
                pool.wait_ge(varn_ready, n + 1)
                nc.gpsimd.tensor_tensor(rstd_n[:], var_n[:], mhalf[:], ALU.pow).then_inc(rstdn_ready, 1)
                pool.wait_ge(xn_hi, n + 1)
                nc.gpsimd.tensor_tensor(xn_hl[:, u, 1, :], xn[:, ds(n % WPB, 1), :], xn_hl[:, u, 0, :], ALU.subtract).then_inc(xn_lo, 1)

            with pool.Fori(0, WPB // 2) as h:
                for u in range(2):
                    prep(2 * h + u, u)
            with pool.Fori(0, B) as b:
                with pool.Fori(0, WPB // 2) as h:
                    for u in range(2):
                        j = 2 * h + u
                        g = b * WPB + j
                        pool.wait_ge(inv_ready, g + 1)
                        pool.wait_ge(xs_lo, xs_lo_start + g)
                        nc.gpsimd.tensor_tensor(xs32[:], xn[:, ds(j, 1), :], inv_sum[:, u:u + 1].to_broadcast([P, D]), ALU.mult).then_inc(xs_full, 1)
                        pool.wait_ge(xs_full, xs_full_start + g + 1)
                        nc.gpsimd.tensor_copy(xs[:, 0, ds(j, 1), :], xs32[:]).then_inc(xs_hi, 1)
                        pool.wait_ge(xs_hi, g + 1)
                        nc.gpsimd.tensor_tensor(xs[:, 1, ds(j, 1), :], xs32[:], xs[:, 0, ds(j, 1), :], ALU.subtract).then_inc(xs_lo, 1)
                with pool.Fori(0, WPB // 2) as h:
                    for u in range(2):
                        g = b * WPB + 2 * h + u
                        pool.wait_ge(varc_ready, g + 1)
                        nc.gpsimd.tensor_tensor(pow_c[:], var_c[:], mhalf[:], ALU.pow).then_inc(powc, 1)
                        pool.wait_ge(powc, g + 1)
                        nc.gpsimd.tensor_tensor(rstd_c[:], pow_c[:], unscale[:], ALU.mult).then_inc(rstdc_ready, 1)
                        prep(g + WPB, u)
                        pool.wait_ge(varx_ready, g + 1)
                        nc.gpsimd.tensor_tensor(rstd_x[:], var_x[:], mhalf[:], ALU.pow).then_inc(rstdx_ready, 1)

        @block.vector
        def _(dve):
            dve.wait_ge(consts_in, 16)
            nc.vector.tensor_copy(ident[:], ident_f[:]).then_inc(consts, 1)

            def prep_stats(n):
                tile = xn[:, ds(n % WPB, 1), :]
                nc.vector.bn_stats(st_n[:], tile).then_inc(stn, 1)
                wait_apart(dve, stn, n + 1, passed_dve)
                nc.vector.bn_aggr(mv_n[:], st_n[:]).then_inc(mvn, 1)
                dve.wait_ge(mvn, n + 1)
                nc.vector.tensor_scalar(var_n[:], mv_n[:, 1:2], EPS, None, ALU.add).then_inc(varn_ready, 1)

            def prep_norm(n, u):
                tile = xn[:, ds(n % WPB, 1), :]
                dve.wait_ge(rstdn_ready, n + 1)
                nc.vector.tensor_scalar(tile, tile, mv_n[:, 0:1], rstd_n[:], ALU.subtract, ALU.mult).then_inc(xn_ready, 1)
                dve.wait_ge(xn_ready, n + 1)
                wait(dve, trans_done, n - 1)
                nc.vector.tensor_scalar(xn_hl[:, u, 0, :], tile, 1.0, None, ALU.mult).then_inc(xn_hi, 1)

            dve.wait_ge(x_loaded, 16)
            for n in range(2):
                prep_stats(n)
                prep_norm(n, n)
            with dve.Fori(1, WPB // 2) as h:
                for u in range(2):
                    prep_stats(2 * h + u)
                    prep_norm(2 * h + u, u)

            with dve.Fori(0, B) as b:
                def row_max(j):
                    g = b * WPB + j
                    u = j % 2
                    dve.wait_ge(scores_done, g + 1)
                    nc.vector.tensor_reduce(negmax[:, ds(u, 1)], ps[:, ds(4 * u, chunks), :].rearrange("p c n -> p (c n)"),
                                            AX.X, ALU.max, negate=True).then_inc(max_ready, 1)

                def low_part(j):
                    g = b * WPB + j
                    u = j % 2
                    dve.wait_ge(e_full, e_full_start + g + 1)
                    nc.vector.tensor_scalar(colsum_s[:, ds(u, 1)], colsum[:, ds(u, 1)], 1.0 / XS_SCALE, None, ALU.mult).then_inc(sum_scaled, 1)
                    nc.vector.tensor_tensor(E[:, 1, ds(j, 1), :], e32[:], E[:, 0, ds(j, 1), :], ALU.subtract).then_inc(e_lo, 1)
                    dve.wait_ge(sum_scaled, g + 1)
                    dve.wait_ge(xs_full, xs_full_start + g - 1)
                    nc.vector.reciprocal(inv_sum[:, ds(u, 1)], colsum_s[:, ds(u, 1)]).then_inc(inv_ready, 1)

                row_max(0)
                with dve.Fori(1, WPB) as j:
                    row_max(j)
                    low_part(j - 1)
                low_part(WPB - 1)
                wait_apart(dve, x_loaded, 16 * (b + 2), passed_dve)
                with dve.Fori(0, WPB // 4) as h:
                    for u4 in range(4):
                        i = 4 * h + u4
                        u = u4 % 2
                        g = b * WPB + i
                        n = g + WPB
                        bank = ps[:, u4, 0:D]
                        dve.wait_ge(ctx_done, g + 1)
                        nc.vector.bn_stats(st_c[:], bank).then_inc(stc, 1)
                        wait_apart(dve, stc, g + 1, passed_dve)
                        nc.vector.bn_aggr(mv_c[:], st_c[:]).then_inc(mvc, 1)
                        dve.wait_ge(mvc, g + 1)
                        nc.vector.tensor_scalar(var_c[:], mv_c[:, 1:2], XS_SCALE ** -2, EPS, ALU.mult, ALU.add).then_inc(varc_ready, 1)
                        prep_stats(n)
                        dve.wait_ge(rstdc_ready, g + 1)
                        nc.vector.tensor_scalar(ln_c[:], bank, mv_c[:, 0:1], rstd_c[:], ALU.subtract, ALU.mult).then_inc(ctx_free, 1)
                        dve.wait_ge(ctx_free, ctx_free_start + g + 1)
                        dve.wait_ge(res_in[u], 16 * (g // 2) + 16)
                        dve.wait_ge(x2_out[u], 16 * (g // 2) + 16)
                        nc.vector.tensor_tensor(x2[:, u, :], ln_c[:], x_res[:, u, :], ALU.add).then_inc(x2_ready, 1)
                        dve.wait_ge(x2_ready, g + 1)
                        nc.vector.bn_stats(st_x[:], x2[:, u, :]).then_inc(stx, 1)
                        wait_apart(dve, stx, g + 1, passed_dve)
                        nc.vector.bn_aggr(mv_x[:], st_x[:]).then_inc(mvx, 1)
                        dve.wait_ge(mvx, g + 1)
                        nc.vector.tensor_scalar(var_x[:], mv_x[:, 1:2], EPS, None, ALU.add).then_inc(varx_ready, 1)
                        prep_norm(n, u)
                        dve.wait_ge(rstdx_ready, g + 1)
                        dve.wait_ge(xo_out[u], 16 * (g // 2) + 16)
                        nc.vector.tensor_scalar(xo[:, u, :], x2[:, u, :], mv_x[:, 0:1], rstd_x[:], ALU.subtract, ALU.mult).then_inc(xo_ready, 1)

        @block.scalar
        def _(act):
            def keep_transposed(n, u):
                act.wait_ge(trans_done, n + 1)
                nc.scalar.copy(xnT[:, :, :, ds((n % WPB) * P, P)], ps_tr[u]).then_inc(xnT_ready, 1)

            with act.Fori(0, WPB // 2) as h:
                for u in range(2):
                    keep_transposed(2 * h + u, u)
            with act.Fori(0, B) as b:
                with act.Fori(0, WPB // 2) as h:
                    for u in range(2):
                        j = 2 * h + u
                        g = b * WPB + j
                        scores = ps[:, 4 * u:4 * u + chunks, :].rearrange("p c n -> p (c n)")
                        act.wait_ge(max_ready, g + 1)
                        nc.scalar.activation(E[:, 0, ds(j, 1), :], scores, ACT.Exp, bias=negmax[:, u:u + 1]).then_inc(e_hi, 1)
                        act.wait_ge(e_lo, e_lo_start + g)
                        nc.scalar.activation(e32[:], scores, ACT.Exp, bias=negmax[:, u:u + 1],
                                             accum_out=colsum[:, u:u + 1]).then_inc(e_full, 1)
                with act.Fori(0, WPB // 2) as h:
                    for u in range(2):
                        keep_transposed((b + 1) * WPB + 2 * h + u, u)

        @block.tensor
        def _(pe):
            def transposes(n, u):
                pe.wait_ge(xn_lo, n + 1)
                wait(pe, xnT_ready, n - 1)
                for part in range(2):
                    for k in range(KD):
                        last = nc.tensor.transpose(ps_tr[u][:, part, k, :], xn_hl[:, u, part, k * P:(k + 1) * P], ident[:])
                last.then_inc(trans_done, 1)

            pe.wait_ge(consts, 1)
            for n in range(2):
                transposes(n, n)
            with pe.Fori(1, WPB // 2) as h:
                for u in range(2):
                    transposes(2 * h + u, u)

            with pe.Fori(0, B) as b:
                pe.wait_ge(xnT_ready, (b + 1) * WPB)
                wait_apart(pe, ctx_free, ctx_free_start + b * WPB, passed_pe)
                with pe.Fori(0, WPB // 2) as h:
                    for u in range(2):
                        g = b * WPB + 2 * h + u
                        pe.wait_ge(e_full, g + 1)
                        rows = ds((2 * h + u) * P, P)
                        for k in range(KD):
                            for a, c in ((0, 0), (0, 1), (1, 0)):
                                for n in range(chunks):
                                    last = nc.tensor.matmul(ps[:, 4 * u + n, :], xnT[:, a, k, rows], xnT[:, c, k, n * 512:(n + 1) * 512],
                                                            start=(k == 0 and a == 0 and c == 0), stop=(k == KD - 1 and a == 1))
                        last.then_inc(scores_done, 1)
                pe.wait_ge(e_lo, e_lo_start + (b + 1) * WPB)
                pe.wait_ge(xs_lo, xs_lo_start + (b + 1) * WPB)

                def context(i, bank):
                    g = b * WPB + i
                    pe.wait_ge(ctx_free, g + 1)
                    for j in range(WPB):
                        for a, c in ((0, 0), (0, 1), (1, 0)):
                            last = nc.tensor.matmul(ps[:, bank, 0:D], E[:, a, j, ds(i * P, P)], xs[:, c, j, :],
                                                    start=(j == 0 and a == 0 and c == 0), stop=(j == WPB - 1 and a == 1))
                    last.then_inc(ctx_done, 1)

                after = (b + 1) * WPB
                context(0, 0)
                with pe.Fori(0, WPB // 4 - 1) as h:
                    for u4 in range(4):
                        context(4 * h + u4 + 1, (u4 + 1) % 4)
                        transposes(after + 4 * h + u4, u4 % 2)
                for i in range(WPB - 3, WPB):
                    context(i, i % 4)
                    transposes(after + i - 1, (i - 1) % 2)
                transposes(after + WPB - 1, (WPB - 1) % 2)


def in_range(t):
    return not isinstance(t, int) or 0 <= t < NT


def slots(eng, run):
    for s in range(FIRST_GROUP * SLOTS):
        run(s, s % SLOTS, s // 2)
    with eng.Fori(FIRST_GROUP, LAST_GROUP) as i:
        for r in range(SLOTS):
            run(SLOTS * i + r, r, SLOTS // 2 * i + r // 2)
    for s in range(LAST_GROUP * SLOTS, LAST_SLOT + 1):
        run(s, s % SLOTS, s // 2)


def phase_b(nc, w, consts, x2_dram, xs_dram, xp_dram, rot_dram, out):
    x2_v = x2_dram.rearrange("(w p) d -> p w d", p=P)
    out_v = out.rearrange("b (w p) d -> p (b w) d", p=P)
    xs_v = xs_dram.rearrange("(w p) d -> p w d", p=P)
    xp_v = xp_dram.rearrange("(w p) d -> p w d", p=P)
    rot_v = rot_dram.rearrange("(w p) n d -> p w (n d)", p=P)
    xs_prev = xs_dram[P - 1:-1, :].rearrange("(w p) d -> p w d", p=P)
    xp_prev = xp_dram[P - 1:-1, :].rearrange("(w p) d -> p w d", p=P)
    HALF = D // 2
    with ExitStack() as keep:
        def sb(name, shape, dt=F32):
            return keep.enter_context(nc.sbuf_tensor("b_" + name, shape, dt))

        wqkv = sb("wqkv", [P, LAYERS, 2, KD, 3 * INNER], F32R)
        w1 = sb("w1", [P, LAYERS, 2, KD, 2 * HPAD], F16)
        w1_unit = sb("w1_unit", [P, LAYERS])
        b1a = sb("b1a", [P, LAYERS, HC])
        b1g = sb("b1g", [P, LAYERS, HC])
        w2 = sb("w2", [P, LAYERS, HC, D])
        b2 = sb("b2", [P, LAYERS, D])
        wo = sb("wo", [P, LAYERS, HP, D])
        mask = sb("mask", [P, 5, 2 * P], BF16)
        ident_f, ident_h = sb("ident_f", [P, P]), sb("ident_h", [P, P], F16)
        mhalf = sb("mhalf", [P, 2 * HEADS])
        ps = keep.enter_context(nc.psum_tensor("b_ps", [P, 8, 512], F32))

        with ExitStack() as ctx:
            def sb(name, shape, dt=F32):
                return ctx.enter_context(nc.sbuf_tensor("p_" + name, shape, dt))

            def sem(name):
                return ctx.enter_context(nc.semaphore("p_" + name))

            wqkv_f = sb("wqkv_f", [P, LAYERS, KD, 3 * INNER])
            w1_f = sb("w1_f", [P, LAYERS, KD, 2 * HPAD])
            b1_f = sb("b1_f", [P, LAYERS, 2, HC])
            lg, lb = sb("lg", [P, LAYERS, KD]), sb("lb", [P, LAYERS, KD])
            rot_all = sb("rot_all", [P, 4, LAYERS * WPB, DH])
            mask_f = sb("mask_f", [P, 5, 2 * P])
            head_scale = sb("head_scale", [P, 2, 2, LAYERS, DH])
            top, top_all, top_min = sb("top", [P, LAYERS]), sb("top_all", [P, LAYERS]), sb("top_min", [P, LAYERS])
            pow2, pow2_inv, w1_scale = sb("pow2", [P, LAYERS]), sb("pow2_inv", [P, LAYERS]), sb("w1_scale", [P, LAYERS])
            cleared, loaded_w1, loaded_qkv, loaded_rot, loaded = (sem(n) for n in ("cleared", "loaded_w1", "loaded_qkv", "loaded_rot", "loaded"))
            loaded_wo, rot_scaled, rot_stored = sem("loaded_wo"), sem("rot_scaled"), sem("rot_stored")
            qkv_hi, bias_done, w1_gained, top_ready, top_shared = (sem(n) for n in ("qkv_hi", "bias_done", "w1_gained", "top_ready", "top_shared"))
            step, scaled, w1_hi, bias_added = sem("step"), sem("scaled"), sem("w1_hi"), sem("bias_added")
            full = HC - 1
            rest = HID - full * P
            block = ctx.enter_context(nc.Block())
            DMAS_W1, DMAS_ROT, DMAS = LAYERS * 7, 4 * LAYERS + 6, 5

            @block.sync
            def _(sp):
                sp.dma_start(wqkv_f[:].rearrange("p l k n -> p (l k) n"), w["wqkv"].rearrange("l (k p) n -> p (l k) n", p=P)).then_inc(loaded_qkv, 16)
                sp.wait_ge(cleared, 3)
                for l in range(LAYERS):
                    for half in range(2):
                        sp.dma_start(w1_f[:, l, :, half * HPAD:half * HPAD + HID],
                                     w["w1"][l, :, half * HID:(half + 1) * HID].rearrange("(k p) n -> p k n", p=P)).then_inc(loaded_w1, 16)
                        b1_half = w["b1"][l, half * HID:(half + 1) * HID]
                        sp.dma_start(b1_f[:, l, half, 0:full], b1_half[0:full * P].rearrange("(c p) -> p c", p=P), allow_slow_non_contiguous=True).then_inc(loaded_w1, 16)
                        sp.dma_start(b1_f[0:rest, l, half, full:HC], b1_half[full * P:HID].rearrange("(p c) -> p c", c=1), allow_slow_non_contiguous=True).then_inc(loaded_w1, 16)
                    sp.dma_start(w2[:, l, 0:full, :], w["w2"][l, 0:full * P, :].rearrange("(c p) d -> p c d", p=P)).then_inc(loaded_w1, 16)
                sp.dma_start(lg[:], w["ln_g"].rearrange("l (k p) -> p l k", p=P), allow_slow_non_contiguous=True).then_inc(loaded, 16)
                sp.dma_start(lb[:], w["ln_b"].rearrange("l (k p) -> p l k", p=P), allow_slow_non_contiguous=True).then_inc(loaded, 16)
                sp.dma_start(w2[0:rest, :, full, :], w["w2"][:, full * P:HID, :].rearrange("l p d -> p l d")).then_inc(loaded, 16)
                sp.dma_start(ident_f[:], consts["ident"]).then_inc(loaded, 16)
                sp.dma_start(mask_f[:], consts["mask"].rearrange("n p j -> p n j")).then_inc(loaded, 16)
                for l in range(LAYERS):
                    for n in range(4):
                        sp.dma_start(rot_all[:, n, l * WPB:(l + 1) * WPB, :], consts["rot"][n].rearrange("(w p) d -> p w d", p=P)).then_inc(loaded_rot, 16)
                for n, name in enumerate(("q_scale", "k_scale")):
                    half = DH // 2
                    sp.dma_start(head_scale[:, n, 0], w[name].partition_broadcast(P)).then_inc(loaded_rot, 16)
                    sp.dma_start(head_scale[:, n, 1, :, 0:half], w[name][:, half:DH].partition_broadcast(P)).then_inc(loaded_rot, 16)
                    sp.dma_start(head_scale[:, n, 1, :, half:DH], w[name][:, 0:half].partition_broadcast(P)).then_inc(loaded_rot, 16)
                sp.dma_start(b2[:], w["b2"].partition_broadcast(P)).then_inc(loaded_wo, 16)
                sp.dma_start(wo[:].rearrange("p l h d -> p (l h) d"), w["wo"].rearrange("l (h p) d -> p (l h) d", p=P)).then_inc(loaded_wo, 16)
                sp.wait_ge(loaded_wo, 32)
                sp.wait_ge(rot_scaled, 4 * LAYERS)
                for n in range(4):
                    sp.dma_start(rot_dram.rearrange("(w p) n d -> p n w d", p=P)[:, n], rot_all[:, n]).then_inc(rot_stored, 16)
                sp.wait_ge(rot_stored, 64)

            @block.gpsimd
            def _(pool):
                nc.gpsimd.memset(w1_f[:, :, :, HID:HPAD], 0.0).then_inc(cleared, 1)
                nc.gpsimd.memset(w1_f[:, :, :, HPAD + HID:2 * HPAD], 0.0)
                nc.gpsimd.memset(b1_f[:, :, :, full:HC], 0.0).then_inc(cleared, 1)
                nc.gpsimd.memset(w2[:, :, full, :], 0.0).then_inc(cleared, 1)
                nc.gpsimd.memset(mhalf[:], -0.5).then_inc(cleared, 1)
                pool.wait_ge(cleared, 4)
                pool.wait_ge(top_ready, LAYERS)
                nc.gpsimd.partition_all_reduce(top_all[:], top[:], P, RED_MAX).then_inc(top_shared, 1)
                pool.wait_ge(top_shared, 1)

            @block.tensor
            def _(pe):
                pe.wait_ge(loaded_w1, 16 * DMAS_W1)
                pe.wait_ge(loaded, 16 * DMAS)
                pe.wait_ge(cleared, 4)
                for l in range(LAYERS):
                    for c in range(2 * HC):
                        for k in range(KD):
                            last = nc.tensor.matmul(ps[:, l, c:c + 1], w1_f[:, l, k, c * P:(c + 1) * P], lb[:, l, k:k + 1], start=(k == 0), stop=(k == KD - 1))
                last.then_inc(bias_done, 1)

            @block.scalar
            def _(act):
                act.wait_ge(loaded_qkv, 16)
                for l in range(LAYERS):
                    nc.scalar.copy(wqkv[:, l, 0], wqkv_f[:, l]).then_inc(qkv_hi, 1)

            @block.vector
            def _(dve):
                dve.wait_ge(loaded, 16 * DMAS)
                nc.vector.tensor_copy(ident_h[:], ident_f[:])
                nc.vector.tensor_copy(mask[:], mask_f[:])
                dve.wait_ge(bias_done, 1)
                for l in range(LAYERS):
                    for k in range(KD):
                        nc.vector.tensor_scalar(w1_f[:, l, k, :], w1_f[:, l, k, :], lg[:, l, k:k + 1], None, ALU.mult).then_inc(w1_gained, 1)
                dve.wait_ge(w1_gained, LAYERS * KD)
                for l in range(LAYERS):
                    nc.vector.tensor_reduce(top[:, l:l + 1], w1_f[:, l].rearrange("p k n -> p (k n)"), AX.X, ALU.max, apply_absolute_value=True).then_inc(top_ready, 1)
                for l in range(LAYERS):
                    dve.wait_ge(qkv_hi, l + 1)
                    nc.vector.tensor_tensor(wqkv[:, l, 1], wqkv_f[:, l], wqkv[:, l, 0], ALU.subtract)
                dve.wait_ge(loaded_rot, 16 * DMAS_ROT)
                for n in range(4):
                    for l in range(LAYERS):
                        windows = rot_all[:, n, l * WPB:(l + 1) * WPB, :]
                        nc.vector.tensor_tensor(windows, windows, head_scale[:, n // 2, n % 2, l:l + 1, :].to_broadcast([P, WPB, DH]), ALU.mult).then_inc(rot_scaled, 1)
                dve.wait_ge(top_shared, 1)
                nc.vector.tensor_scalar(top_min[:], top_all[:], 1e-30, None, ALU.max).then_inc(step, 1)
                dve.wait_ge(step, 1)
                nc.vector.tensor_scalar(pow2[:].bitcast(I32), top_min[:].bitcast(I32), 0x7F800000, None, ALU.bitwise_and).then_inc(step, 1)
                dve.wait_ge(step, 2)
                nc.vector.reciprocal(pow2_inv[:], pow2[:]).then_inc(step, 1)
                nc.vector.tensor_scalar(w1_unit[:], pow2[:], 1.0 / W1_TOP, None, ALU.mult).then_inc(step, 1)
                dve.wait_ge(step, 4)
                nc.vector.tensor_scalar(w1_scale[:], pow2_inv[:], W1_TOP, None, ALU.mult).then_inc(step, 1)
                dve.wait_ge(step, 5)
                for l in range(LAYERS):
                    nc.vector.tensor_scalar(w1_f[:, l], w1_f[:, l], w1_scale[:, l:l + 1], None, ALU.mult).then_inc(scaled, 1)
                    dve.wait_ge(scaled, l + 1)
                    nc.vector.tensor_copy(w1[:, l, 0], w1_f[:, l]).then_inc(w1_hi, 1)
                    dve.wait_ge(w1_hi, l + 1)
                    nc.vector.tensor_tensor(w1[:, l, 1], w1_f[:, l], w1[:, l, 0], ALU.subtract)
                    nc.vector.tensor_scalar(w2[:, l], w2[:, l], w1_unit[:, l:l + 1], None, ALU.mult)
                    nc.vector.tensor_tensor(b1g[:, l, :], ps[:, l, HC:2 * HC], b1_f[:, l, 1, :], ALU.add)
                    nc.vector.tensor_tensor(b1_f[:, l, 0, :], ps[:, l, 0:HC], b1_f[:, l, 0, :], ALU.add).then_inc(bias_added, 1)
                    dve.wait_ge(bias_added, l + 1)
                    nc.vector.tensor_scalar(b1a[:, l, :], b1_f[:, l, 0, :], w1_scale[:, l:l + 1], None, ALU.mult)

        with ExitStack() as ctx:
            def sb(name, shape, dt=F32):
                return ctx.enter_context(nc.sbuf_tensor("b_" + name, shape, dt))

            def sem(name):
                return ctx.enter_context(nc.semaphore("b_" + name))

            rot = sb("rot", [P, 2, 4, DH])
            hx = sb("hx", [P, 2, D])
            xr = sb("xr", [P, 4, D])
            hT_hi, hT_lo = sb("hT_hi", [P, KD, P], F32R), sb("hT_lo", [P, KD, P], F32R)
            v = sb("v", [P, 4, INNER])
            kT = sb("kT", [P, HEADS, 2 * P])
            sq = sb("sq", [P, 2, INNER])
            ss, ss_min = sb("ss", [P, 2 * HEADS]), sb("ss_min", [P, 2 * HEADS])
            rn = sb("rn", [P, 2, 2 * HEADS])
            t1, t2 = sb("t1", [P, 2, INNER]), sb("t2", [P, 2, INNER])
            qr, kr, kr_raw = sb("qr", [P, INNER]), sb("kr", [P, INNER]), sb("kr_raw", [P, INNER])
            qT = sb("qT", [P, HP, P])
            negmax = sb("negmax", [P, HEADS])
            mask_now = sb("mask_now", [P, 2 * P], BF16)
            probs = sb("probs", [P, HEADS, 2 * P])
            rowsum, rinv = sb("rowsum", [P, HEADS]), sb("rinv", [P, HEADS])
            probsT = sb("probsT", [P, HP, 512])
            oT = sb("oT", [P, HP, P])
            xp = sb("xp", [P, 4, D])
            xb = sb("xb", [P, 4, D])
            h2 = sb("h2", [P, 2, D])
            st2, mv2, var2, rstd2 = sb("st2", [P, 6]), sb("mv2", [P, 2]), sb("var2", [P, 1]), sb("rstd2", [P, 1])
            xh, xh_hl = sb("xh", [P, D]), sb("xh_hl", [P, 2, D], F16)
            h2T = sb("h2T", [P, 2, KD, 2 * P], F16)
            gl = sb("gl", [P, 2, 2 * P])
            hid = sb("hid", [P, HC, 2 * P])
            xpp = sb("xpp", [P, 2, 2, D])
            stf, mvf = sb("stf", [P, 2, 6]), sb("mvf", [P, 2, 2])
            varf, rstdf = sb("varf", [P, 2]), sb("rstdf", [P, 2])
            xf = sb("xf", [P, 2, D])
            x2 = sb("x2", [P, 2, D])
            fin = sb("fin", [P, 2, 2, D])

            rot_loaded, passed_dve, passed_sp = sem("rot_loaded"), sem("passed_dve"), sem("passed_sp")
            hx_loaded, xr_loaded, h2_loaded, x2_loaded = (sem(n) for n in ("hx_loaded", "xr_loaded", "h2_loaded", "x2_loaded"))
            xp_stored, xpp_stored, fin_stored = (sem(n) for n in ("xp_stored", "xpp_stored", "fin_stored"))
            hT_done, hT_hi_kept, hT_lo_kept = (sem(n) for n in ("hT_done", "hT_hi_kept", "hT_lo_kept"))
            v_done, q_done, k_done, v_kept = (sem(n) for n in ("v_done", "q_done", "k_done", "v_kept"))
            q_sq, k_sq = sem("q_sq"), sem("k_sq")
            q_terms, k_terms = sem("q_terms"), sem("k_terms")
            ss_part, ss_ready, rn_ready = sem("ss_part"), sem("ss_ready"), sem("rn_ready")
            qr_ready, kr_sum, kr_ready = sem("qr_ready"), sem("kr_sum"), sem("kr_ready")
            kT_done, qT_done, kT_kept, qT_kept = (sem(n) for n in ("kT_done", "qT_done", "kT_kept", "qT_kept"))
            scores_done, mask_ready = sem("scores_done"), sem("mask_ready")
            scores_kept, exp_done = sem("scores_kept"), sem("exp_done")
            rinv_ready, probs_ready = sem("rinv_ready"), sem("probs_ready")
            pT_done, pT_kept_a, pT_kept_v = sem("pT_done"), sem("pT_kept_a"), sem("pT_kept_v")
            pv_done, oT_kept, wo_done, xp_ready, xb_ready = (sem(n) for n in ("pv_done", "oT_kept", "wo_done", "xp_ready", "xb_ready"))
            st2_ready, mv2_ready, var2_ready, rstd2_ready = (sem(n) for n in ("st2_ready", "mv2_ready", "var2_ready", "rstd2_ready"))
            xh_ready, xh_hi, xh_lo, h2T_done, h2T_kept = (sem(n) for n in ("xh_ready", "xh_hi", "xh_lo", "h2T_done", "h2T_kept"))
            w1_done, gelu_done, hid_ready = sem("w1_done"), sem("gelu_done"), sem("hid_ready")
            w2_done, xpp_ready = sem("w2_done"), sem("xpp_ready")
            stf_ready, mvf_ready, varf_ready = sem("stf_ready"), sem("mvf_ready"), sem("varf_ready")
            rstdf_ready, xf_ready, fin_ready = sem("rstdf_ready"), sem("xf_ready"), sem("fin_ready")
            ps_h2T = ps[:, 7, 0:D].bitcast(F16).rearrange("p (a k n) -> p a k n", a=2, k=KD)
            vk_cleared = sem("vk_cleared")
            block = ctx.enter_context(nc.Block())

            def by_head(ap):
                return ap.rearrange("p (h d) -> p h d", d=DH)

            @block.sync
            def _(sp):
                def load_hx(t, parity):
                    n = stream_block(t)
                    sp.dma_start(hx[:, parity, 0:HALF], xs_v[:, ds(n, 1), 0:HALF]).then_inc(hx_loaded, 16)
                    sp.dma_start(hx[:, parity, HALF:D], xs_prev[:, ds(n - 1, 1), HALF:D]).then_inc(hx_loaded, 16)

                def load_rot(t, parity):
                    sp.dma_start(rot[:, parity], rot_v[:, ds((t // NW) * WPB + t % WPB, 1), :]).then_inc(rot_loaded, 16)

                load_hx(0, 0)
                load_rot(0, 0)

                def run(s, r, pairs):
                    j = pairs - 3
                    c = (r // 2 - 3) % 2
                    if r % 2 == 0 and in_range(2 * j):
                        wait_apart(sp, xpp_ready, 2 * j + 2, passed_sp)
                        wait(sp, xpp_stored, 16 * j)
                        sp.dma_start(xs_v[:, ds(stream_block(2 * j + NW), 2), :], xpp[:, c]).then_inc(xpp_stored, 16)
                        wait_apart(sp, fin_ready, j + 1, passed_sp)
                        wait(sp, fin_stored, 16 * j)
                        sp.dma_start(out_v[:, ds((2 * j) % NW, 2), :], fin[:, c]).then_inc(fin_stored, 16)
                    if r % 2 == 0 and in_range(2 * j + 2):
                        wait_apart(sp, fin_ready, j + 1, passed_sp)
                        wait(sp, x2_loaded, 16 * (j + 1))
                        sp.dma_start(x2[:], x2_v[:, ds((2 * j + 2) % NW, 2), :]).then_inc(x2_loaded, 16)
                    if in_range(s + 1):
                        wait(sp, hT_done, s)
                        sp.wait_ge(hx_loaded, 32 * (s + 1))
                        load_hx(s + 1, (r + 1) % 2)
                        wait_apart(sp, k_terms, 3 * s, passed_sp)
                        sp.wait_ge(rot_loaded, 16 * (s + 1))
                        load_rot(s + 1, (r + 1) % 2)
                    if in_range(s):
                        wait_apart(sp, xp_ready, s - 3, passed_sp)
                        wait(sp, xr_loaded, 16 * s)
                        sp.dma_start(xr[:, r, :], xs_v[:, ds(stream_block(s), 1), :]).then_inc(xr_loaded, 16)
                    t = s - 2
                    if in_range(t):
                        n = stream_block(t)
                        sp.wait_ge(xp_ready, t + 1)
                        sp.dma_start(xp_v[:, ds(n, 1), :], xp[:, (r - 2) % 4, :]).then_inc(xp_stored, 16)
                        wait_apart(sp, xp_stored, 16 * (t + 1), passed_sp)
                        wait_apart(sp, xh_ready, t - 1, passed_sp)
                        wait(sp, h2_loaded, 32 * t)
                        sp.dma_start(h2[:, r % 2, 0:HALF], xp_v[:, ds(n, 1), 0:HALF]).then_inc(h2_loaded, 16)
                        sp.dma_start(h2[:, r % 2, HALF:D], xp_prev[:, ds(n - 1, 1), HALF:D]).then_inc(h2_loaded, 16)

                slots(sp, run)
                sp.wait_ge(xpp_stored, 16 * (NT // 2))
                sp.wait_ge(fin_stored, 16 * (NT // 2))

            @block.tensor
            def _(pe):
                def transpose_hx(t, r):
                    pe.wait_ge(hx_loaded, 32 * (t + 1))
                    wait(pe, h2T_kept, t - 3)
                    for k in range(KD):
                        last = nc.tensor.transpose(ps[:, 7, k * P:(k + 1) * P], hx[:, r % 2, k * P:(k + 1) * P], ident_f[:])
                    last.then_inc(hT_done, 1)

                def transpose_h2(t):
                    if in_range(t):
                        pe.wait_ge(xh_hi, t + 1)
                        pe.wait_ge(xh_lo, t + 1)
                        if in_range(t + 1):
                            pe.wait_ge(oT_kept, t + 2)
                        else:
                            pe.wait_ge(h2T_kept, t)
                        for part in range(2):
                            for k in range(KD):
                                last = nc.tensor.transpose(ps_h2T[:, part, k, :], xh_hl[:, part, k * P:(k + 1) * P], ident_h[:])
                        last.then_inc(h2T_done, 1)

                def run(s, r, pairs):
                    if in_range(s):
                        pe.wait_ge(hT_hi_kept, s + 1)
                        pe.wait_ge(hT_lo_kept, s + 1)
                        wait(pe, xp_ready, s - 2)
                        for bank, first, done in ((2, 2 * INNER, v_done), (0, 0, q_done), (1, INNER, k_done)):
                            if bank < 2:
                                wait(pe, (q_terms, k_terms)[bank], 3 * s)
                                if r % 2 == 1:
                                    wait(pe, hid_ready, HC * (pairs - 2) + bank + 1)
                            for k in range(KD):
                                for a, hT, part in ((0, hT_hi, 0), (1, hT_hi, 1), (2, hT_lo, 0)):
                                    last = nc.tensor.matmul(ps[:, bank, :], hT[:, k, :], wqkv[:, ds(s // NW, 1), part, k, first:first + INNER],
                                                            start=(k == 0 and a == 0), stop=(k == KD - 1 and a == 2))
                            last.then_inc(done, 1)
                    t = s - 1
                    if in_range(t):
                        pe.wait_ge(kr_ready, t + 1)
                        wait(pe, scores_kept, HEADS * t)
                        if r % 2 == 1:
                            wait(pe, hid_ready, HC * (pairs - 1))
                        for p in range(HP):
                            last = nc.tensor.transpose(ps[:, 6, p * P:(p + 1) * P], kr[:, p * P:(p + 1) * P], ident_f[:])
                        last.then_inc(kT_done, 1)
                        pe.wait_ge(qr_ready, t + 1)
                        if in_range(s):
                            pe.wait_ge(v_kept, s + 1)
                        else:
                            pe.wait_ge(xp_ready, s - 2)
                        for p in range(HP):
                            last = nc.tensor.transpose(ps[:, 2, p * P:(p + 1) * P], qr[:, p * P:(p + 1) * P], ident_f[:])
                        last.then_inc(qT_done, 1)
                    t = s - 2
                    if in_range(t):
                        if r % 2 == 0:
                            wait(pe, xpp_ready, s - 4)
                        elif not in_range(s - 1):
                            pe.wait_ge(hid_ready, HC * (pairs - 1))
                        for p in range(HP):
                            if p == HP - 1 and in_range(s - 1):
                                pe.wait_ge(kT_kept, 2 * s)
                            pe.wait_ge(probs_ready, HEADS * t + 2 * p + 2)
                            for n in range(4):
                                last = nc.tensor.transpose(ps[:, 3 + p, n * P:(n + 1) * P],
                                                           probs[:, 2 * p + n // 2, (n % 2) * P:(n % 2 + 1) * P], ident_f[:])
                            last.then_inc(pT_done, 1)
                        if not in_range(s):
                            pe.wait_ge(h2T_kept, s - 3)
                        for p in range(HP):
                            pe.wait_ge((pT_kept_a, pT_kept_v)[p // 2], 2 * t + p % 2 + 1)
                            for c in range(2):
                                window = (r - 2 - (r + c) % 2) % 4
                                for h in range(2):
                                    last = nc.tensor.matmul(ps[h * DH:(h + 1) * DH, 7, p * P:(p + 1) * P],
                                                            v[:, window, (2 * p + h) * DH:(2 * p + h + 1) * DH],
                                                            probsT[:, p, (2 * h + c) * P:(2 * h + c + 1) * P],
                                                            start=(c == 0), stop=(c == 1))
                        last.then_inc(pv_done, 1)
                    t = s - 1
                    if in_range(t):
                        pe.wait_ge(kT_kept, 2 * (t + 1))
                        pe.wait_ge(qT_kept, t + 1)
                        for p in range(HP):
                            if p == HP // 2:
                                transpose_h2(s - 3)
                            for h in range(2):
                                last = nc.tensor.matmul(ps[:, 3 + p, h * 2 * P:(h + 1) * 2 * P], qT[:, p, :], kT[:, 2 * p + h, :], start=True, stop=True)
                            last.then_inc(scores_done, 1)
                    else:
                        transpose_h2(s - 3)
                    t = s - 2
                    if in_range(t):
                        pe.wait_ge(oT_kept, t + 1)
                        for p in range(HP):
                            last = nc.tensor.matmul(ps[:, 2, 0:D], oT[:, p, :], wo[:, ds(t // NW, 1), p, :], start=(p == 0), stop=(p == HP - 1))
                        last.then_inc(wo_done, 1)
                    if in_range(s + 1):
                        transpose_hx(s + 1, r + 1)
                    j = pairs - 2
                    if r % 2 == 0 and in_range(2 * j):
                        pe.wait_ge(h2T_kept, 2 * j + 2)
                        if not in_range(s - 2):
                            pe.wait_ge(xpp_ready, s - 4)
                        for c, bank in enumerate(W1_BANKS):
                            if bank < 2 and in_range(s):
                                pe.wait_ge((q_terms, k_terms)[bank], 3 * (s + 1))
                            if bank > 2 and in_range(s - 1):
                                pe.wait_ge(scores_kept, HEADS * (s - 1) + 2 * (bank - 3) + 2)
                            for half in range(2):
                                for k in range(KD):
                                    for a, (wp, hp) in enumerate(((0, 0), (0, 1), (1, 0))):
                                        first = half * HPAD + c * P
                                        last = nc.tensor.matmul(ps[:, bank, half * 2 * P:(half + 1) * 2 * P],
                                                                w1[:, ds((2 * j) // NW, 1), wp, k, first:first + P], h2T[:, hp, k, :],
                                                                start=(k == 0 and a == 0), stop=(k == KD - 1 and a == 2))
                            last.then_inc(w1_done, 1)
                    if r % 2 == 1 and in_range(2 * j):
                        pe.wait_ge(hid_ready, HC * (j + 1))
                        if in_range(s - 1):
                            pe.wait_ge(scores_kept, HEADS * (s - 1) + 2)
                        for n in range(2):
                            for c in range(HC):
                                last = nc.tensor.matmul(ps[:, 3, n * D:(n + 1) * D], hid[:, c, n * P:(n + 1) * P], w2[:, ds((2 * j) // NW, 1), c, :],
                                                        start=(c == 0), stop=(c == HC - 1))
                        last.then_inc(w2_done, 1)

                transpose_hx(0, 0)
                slots(pe, run)

            @block.scalar
            def _(act):
                def keep_hT(t):
                    act.wait_ge(hT_done, t + 1)
                    wait(act, k_done, t)
                    nc.scalar.copy(hT_hi[:], ps[:, 7, 0:D].rearrange("p (k n) -> p k n", k=KD)).then_inc(hT_hi_kept, 1)

                def keep_h2T(t, r, pairs):
                    if in_range(t):
                        act.wait_ge(h2T_done, t + 1)
                        if r % 2 == 1:
                            wait(act, w1_done, HC * (pairs - 1))
                        n = (r - 3) % 2
                        nc.scalar.copy(h2T[:, :, :, n * P:(n + 1) * P], ps_h2T).then_inc(h2T_kept, 1)

                def run(s, r, pairs):
                    if in_range(s):
                        act.wait_ge(v_done, s + 1)
                        wait(act, pv_done, s - 2)
                        nc.scalar.copy(v[:, r, :], ps[:, 2, :]).then_inc(v_kept, 1)
                        wait(act, ss_part, 2 * s)
                        act.wait_ge(q_done, s + 1)
                        nc.scalar.activation(sq[:, 0, :], ps[:, 0, :], ACT.Square).then_inc(q_sq, 1)
                        act.wait_ge(k_done, s + 1)
                        nc.scalar.activation(sq[:, 1, :], ps[:, 1, :], ACT.Square).then_inc(k_sq, 1)
                    t = s - 1
                    if in_range(t):
                        act.wait_ge(kT_done, t + 1)
                        wait(act, scores_done, HP * t)
                        par = (r - 1) % 2
                        for h in range(2):
                            rows = slice(h * DH, (h + 1) * DH)
                            nc.scalar.copy(kT[rows, h::2, par * P:(par + 1) * P], ps[rows, 6, :].rearrange("p (h n) -> p h n", h=HP)).then_inc(kT_kept, 1)
                        act.wait_ge(qT_done, t + 1)
                        nc.scalar.copy(qT[:], ps[:, 2, :].rearrange("p (h n) -> p h n", h=HP)).then_inc(qT_kept, 1)
                    t = s - 2
                    if in_range(t):
                        wait(act, pv_done, t)
                        for p in range(HP // 2):
                            act.wait_ge(pT_done, HP * t + p + 1)
                            nc.scalar.copy(probsT[:, p, :], ps[:, 3 + p, :]).then_inc(pT_kept_a, 1)
                        act.wait_ge(pv_done, t + 1)
                        wait(act, wo_done, t)
                        nc.scalar.copy(oT[:], ps[:, 7, :].rearrange("p (h n) -> p h n", h=HP)).then_inc(oT_kept, 1)
                    t = s - 1
                    if in_range(t):
                        for p in range(HP):
                            if p == HP // 2:
                                keep_h2T(s - 3, r, pairs)
                            for h in range(2 * p, 2 * p + 2):
                                act.wait_ge(scores_kept, HEADS * t + h + 1)
                                nc.scalar.activation(probs[:, h, :], probs[:, h, :], ACT.Exp, bias=negmax[:, h:h + 1], scale=-1.0,
                                                     accum_out=rowsum[:, h:h + 1]).then_inc(exp_done, 1)
                    else:
                        keep_h2T(s - 3, r, pairs)
                    if in_range(s + 1):
                        keep_hT(s + 1)
                    j = pairs - 2
                    if r % 2 == 0 and in_range(2 * j):
                        for c, bank in enumerate(W1_BANKS):
                            wait(act, hid_ready, HC * j + c - 1)
                            act.wait_ge(w1_done, HC * j + c + 1)
                            nc.scalar.activation(gl[:, c % 2, :], ps[:, bank, 2 * P:4 * P], ACT.Gelu,
                                                 bias=b1g[:, ds((2 * j) // NW, 1), c], scale=w1_unit[:, ds((2 * j) // NW, 1)]).then_inc(gelu_done, 1)

                act.wait_ge(vk_cleared, 2)
                keep_hT(0)
                slots(act, run)

            @block.vector
            def _(dve):
                def keep_hT(t):
                    dve.wait_ge(hT_hi_kept, t + 1)
                    nc.vector.tensor_tensor(hT_lo[:], ps[:, 7, 0:D].rearrange("p (k n) -> p k n", k=KD), hT_hi[:], ALU.subtract).then_inc(hT_lo_kept, 1)

                def run(s, r, pairs):
                    if in_range(s):
                        dve.wait_ge(rot_loaded, 16 * (s + 1))
                        for n, squared, terms, used in ((0, q_sq, q_terms, qr_ready), (1, k_sq, k_terms, kr_sum)):
                            dve.wait_ge(squared, s + 1)
                            wait(dve, used, s)
                            x = by_head(ps[:, n, :])
                            half = DH // 2

                            def factor(which, lo, hi):
                                return rot[:, r % 2, which:which + 1, lo:hi].to_broadcast([P, HEADS, hi - lo])

                            t2_h = by_head(t2[:, n, :])
                            nc.vector.tensor_tensor(by_head(t1[:, n, :]), x, factor(2 * n, 0, DH), ALU.mult).then_inc(terms, 1)
                            nc.vector.tensor_tensor(t2_h[:, :, 0:half], x[:, :, half:DH], factor(2 * n + 1, 0, half), ALU.mult).then_inc(terms, 1)
                            nc.vector.tensor_tensor(t2_h[:, :, half:DH], x[:, :, 0:half], factor(2 * n + 1, half, DH), ALU.mult).then_inc(terms, 1)
                    t = s - 2
                    if in_range(t):
                        wait(dve, pv_done, t)
                        for p in range(HP // 2, HP):
                            dve.wait_ge(pT_done, HP * t + p + 1)
                            nc.vector.tensor_copy(probsT[:, p, :], ps[:, 3 + p, :]).then_inc(pT_kept_v, 1)
                    t = s - 3
                    if in_range(t):
                        dve.wait_ge(h2_loaded, 32 * (t + 1))
                        nc.vector.bn_stats(st2[:], h2[:, (r - 3) % 2, :]).then_inc(st2_ready, 1)
                        wait_apart(dve, st2_ready, t + 1, passed_dve)
                        nc.vector.bn_aggr(mv2[:], st2[:]).then_inc(mv2_ready, 1)
                        dve.wait_ge(mv2_ready, t + 1)
                        nc.vector.tensor_scalar(var2[:], mv2[:, 1:2], EPS, None, ALU.add).then_inc(var2_ready, 1)
                    if in_range(s):
                        for n, squared in ((0, q_sq), (1, k_sq)):
                            nc.vector.tensor_reduce(ss[:, n * HEADS:(n + 1) * HEADS], by_head(sq[:, n, :]), AX.X, ALU.add).then_inc(ss_part, 1)
                        dve.wait_ge(ss_part, 2 * (s + 1))
                        wait(dve, rn_ready, s)
                        nc.vector.tensor_scalar(ss_min[:], ss[:], 1e-24, None, ALU.max).then_inc(ss_ready, 1)
                    t = s - 3
                    if in_range(t):
                        dve.wait_ge(rstd2_ready, t + 1)
                        wait(dve, xh_lo, t)
                        nc.vector.tensor_scalar(xh[:], h2[:, (r - 3) % 2, :], mv2[:, 0:1], rstd2[:], ALU.subtract, ALU.mult).then_inc(xh_ready, 1)
                        dve.wait_ge(xh_ready, t + 1)
                        wait(dve, h2T_done, t)
                        nc.vector.tensor_copy(xh_hl[:, 0, :], xh[:]).then_inc(xh_hi, 1)
                    t = s - 1
                    if in_range(t):
                        dve.wait_ge(rn_ready, t + 1)
                        which = mask_now[:] if r == 1 else mask[:, EVEN_MASK if r == 3 else ODD_MASK, :]
                        if r == 1:
                            dve.wait_ge(mask_ready, t // SLOTS + 1)
                        wait(dve, pT_done, HP * t)
                        for p in range(HP):
                            wait_apart(dve, scores_done, HP * t + p + 1, passed_dve)
                            for h in range(2 * p, 2 * p + 2):
                                nc.vector.tensor_tensor_reduce(probs[:, h, :], ps[:, 3 + p, (h % 2) * 2 * P:(h % 2 + 1) * 2 * P], which,
                                                               rn[:, (r - 1) % 2, h:h + 1], ABOVE_ALL, ALU.add, ALU.min,
                                                               negmax[:, h:h + 1]).then_inc(scores_kept, 1)

                    def normalise(p):
                        t = s - 1
                        if in_range(t):
                            dve.wait_ge(exp_done, HEADS * t + 2 * p + 2)
                            nc.vector.reciprocal(rinv[:, 2 * p:2 * p + 2], rowsum[:, 2 * p:2 * p + 2]).then_inc(rinv_ready, 1)
                            dve.wait_ge(rinv_ready, HP * t + p + 1)
                            for h in range(2 * p, 2 * p + 2):
                                nc.vector.tensor_scalar(probs[:, h, :], probs[:, h, :], rinv[:, h:h + 1], None, ALU.mult).then_inc(probs_ready, 1)

                    normalise(0)
                    normalise(1)
                    t = s - 2
                    if in_range(t):
                        dve.wait_ge(wo_done, t + 1)
                        dve.wait_ge(xr_loaded, 16 * (t + 1))
                        wait(dve, xp_stored, 16 * (t - 3))
                        wait(dve, xb_ready, t - 3)
                        nc.vector.tensor_tensor(xp[:, (r - 2) % 4, :], ps[:, 2, 0:D], xr[:, (r - 2) % 4, :], ALU.add).then_inc(xp_ready, 1)
                    normalise(2)
                    if in_range(s + 1):
                        keep_hT(s + 1)
                    normalise(3)
                    j = pairs - 2
                    if r % 2 == 0 and in_range(2 * j):
                        wait(dve, w2_done, j)
                        for c, bank in enumerate(W1_BANKS):
                            dve.wait_ge(gelu_done, HC * j + c + 1)
                            nc.vector.scalar_tensor_tensor(hid[:, c, :], ps[:, bank, 0:2 * P], b1a[:, ds((2 * j) // NW, 1), c], gl[:, c % 2, :],
                                                           ALU.add, ALU.mult).then_inc(hid_ready, 1)
                    if r % 2 == 1 and in_range(2 * j):
                        c = (r // 2) % 2
                        dve.wait_ge(w2_done, j + 1)
                        wait(dve, xpp_stored, 16 * (j - 1))
                        for n in range(2):
                            dve.wait_ge(xb_ready, 2 * j + n + 1)
                            nc.vector.tensor_tensor(xpp[:, c, n, :], ps[:, 3, n * D:(n + 1) * D], xb[:, (r - 5 + n) % 4, :], ALU.add).then_inc(xpp_ready, 1)
                        for n in range(2):
                            dve.wait_ge(xpp_ready, 2 * j + n + 1)
                            nc.vector.bn_stats(stf[:, n, :], xpp[:, c, n, :]).then_inc(stf_ready, 1)
                        for n in range(2):
                            wait_apart(dve, stf_ready, 2 * j + n + 1, passed_dve)
                            nc.vector.bn_aggr(mvf[:, n, :], stf[:, n, :]).then_inc(mvf_ready, 1)
                        dve.wait_ge(mvf_ready, 2 * j + 2)
                        nc.vector.tensor_scalar(varf[:], mvf[:, :, 1], EPS, None, ALU.add).then_inc(varf_ready, 1)
                        dve.wait_ge(rstdf_ready, j + 1)
                        wait(dve, fin_ready, j)
                        for n in range(2):
                            nc.vector.tensor_scalar(xf[:, n, :], xpp[:, c, n, :], mvf[:, n, 0:1], rstdf[:, n:n + 1],
                                                    ALU.subtract, ALU.mult).then_inc(xf_ready, 1)

                keep_hT(0)
                slots(dve, run)

            @block.gpsimd
            def _(pool):
                def run(s, r, pairs):
                    if r == 0 and in_range(s):
                        wait(pool, scores_kept, HEADS * (s - 3))
                        nc.gpsimd.tensor_copy(mask_now[:], mask[:, ds((s // SLOTS) % (WPB // SLOTS), 1), :]).then_inc(mask_ready, 1)
                    if in_range(s):
                        pool.wait_ge(q_terms, 3 * (s + 1))
                        wait(pool, qT_done, s)
                        nc.gpsimd.tensor_tensor(qr[:], t1[:, 0, :], t2[:, 0, :], ALU.add).then_inc(qr_ready, 1)
                        pool.wait_ge(k_terms, 3 * (s + 1))
                        wait(pool, kr_ready, s)
                        nc.gpsimd.tensor_tensor(kr_raw[:], t1[:, 1, :], t2[:, 1, :], ALU.add).then_inc(kr_sum, 1)
                    t = s - 3
                    if in_range(t):
                        pool.wait_ge(var2_ready, t + 1)
                        nc.gpsimd.tensor_tensor(rstd2[:], var2[:], mhalf[:, 0:1], ALU.pow).then_inc(rstd2_ready, 1)
                        pool.wait_ge(xh_hi, t + 1)
                        nc.gpsimd.tensor_tensor(xh_hl[:, 1, :], xh[:], xh_hl[:, 0, :], ALU.subtract).then_inc(xh_lo, 1)
                    if in_range(s):
                        pool.wait_ge(ss_ready, s + 1)
                        wait(pool, scores_kept, HEADS * (s - 1))
                        nc.gpsimd.tensor_tensor(rn[:, r % 2, :], ss_min[:], mhalf[:], ALU.pow).then_inc(rn_ready, 1)
                    if in_range(s):
                        pool.wait_ge(rn_ready, s + 1)
                        pool.wait_ge(kr_sum, s + 1)
                        wait(pool, kT_done, s)
                        nc.gpsimd.tensor_tensor(by_head(kr[:]), by_head(kr_raw[:]),
                                                rn[:, r % 2, HEADS:2 * HEADS].unsqueeze(2).to_broadcast([P, HEADS, DH]), ALU.mult).then_inc(kr_ready, 1)
                    t = s - 2
                    if in_range(t):
                        pool.wait_ge(xp_ready, t + 1)
                        wait(pool, xpp_ready, t - 3)
                        nc.gpsimd.tensor_tensor(xb[:, (r - 2) % 4, :], xp[:, (r - 2) % 4, :], b2[:, ds(t // NW, 1), :], ALU.add).then_inc(xb_ready, 1)
                    j = pairs - 2
                    if r % 2 == 1 and in_range(2 * j):
                        c = (r // 2) % 2
                        pool.wait_ge(varf_ready, j + 1)
                        nc.gpsimd.tensor_tensor(rstdf[:], varf[:], mhalf[:, 0:2], ALU.pow).then_inc(rstdf_ready, 1)
                        pool.wait_ge(xf_ready, 2 * j + 2)
                        pool.wait_ge(x2_loaded, 16 * (j + 1))
                        wait(pool, fin_stored, 16 * (j - 1))
                        nc.gpsimd.tensor_tensor(fin[:, c], xf[:], x2[:], ALU.add).then_inc(fin_ready, 1)

                nc.gpsimd.memset(v[:], 0.0).then_inc(vk_cleared, 1)
                nc.gpsimd.memset(kT[:], 0.0).then_inc(vk_cleared, 1)
                slots(pool, run)


def build(nc, x, wqkv, q_scale, k_scale, wo, ln_g, ln_b, w1, b1, w2, b2, ident, rot, mask, out):
    x2_dram = nc.dram_tensor("x2_dram", [NW * P, D], F32).ap()
    xs_dram = nc.dram_tensor("xs_dram", [XS_BLOCKS * P, D], F32).ap()
    xp_dram = nc.dram_tensor("xp_dram", [XP_BLOCKS * P, D], F32).ap()
    rot_dram = nc.dram_tensor("rot_dram", [LAYERS * S, 4, DH], F32).ap()
    phase_a(nc, x, ident, x2_dram, xs_dram, xp_dram)
    weights = dict(wqkv=wqkv, q_scale=q_scale, k_scale=k_scale, wo=wo, ln_g=ln_g, ln_b=ln_b, w1=w1, b1=b1, w2=w2, b2=b2)
    phase_b(nc, weights, dict(ident=ident, rot=rot, mask=mask), x2_dram, xs_dram, xp_dram, rot_dram, out)


def rotary_tables():
    f = np.float32
    half = np.arange(0, DH, 2, dtype=f)
    inv_freq = f(1) / np.power(10000.0, (half / f(DH)).astype(np.float64)).astype(f)
    t = np.arange(S, dtype=f)
    freqs = t[:, None] * inv_freq[None, :]
    base = (half + f(0.4 * DH)) / f(1.4 * DH)
    power = (t - f(S // 2)) / f(P // 2)
    scale = np.power(base[None, :].astype(np.float64), power[:, None].astype(np.float64))
    cos, sin = np.cos(freqs.astype(np.float64)), np.sin(freqs.astype(np.float64))
    both = lambda lo, hi: np.concatenate([lo, hi], axis=1)
    tables = [both(cos, cos) * both(scale, scale) * -QK_SCALE, both(-sin, sin) * both(scale, scale) * -QK_SCALE,
              both(cos, cos) / both(scale, scale), both(-sin, sin) / both(scale, scale)]
    return np.stack(tables).astype(f)


def window_masks():
    i, j = np.arange(P)[:, None], np.arange(P)[None, :]
    own, before = np.where(j <= i, 0.0, MASKED), np.where(j >= i, 0.0, MASKED)
    none = np.full((P, P), MASKED)
    kinds = [(own, none)] + (WPB // SLOTS - 1) * [(own, before)] + [(before, own)]
    return np.stack([np.concatenate(kind, axis=1) for kind in kinds]).astype(np.float32)


_INS = ["L0_attn_x", "L0_ffn_wqkv", "L0_ffn_q_scale", "L0_ffn_k_scale", "L0_ffn_wo", "L0_ffn_ln_g", "L0_ffn_ln_b", "L0_ffn_w1", "L0_ffn_b1",
        "L0_ffn_w2", "L0_ffn_b2"]


def kernel(**inputs):
    import concourse.bacc as bacc
    from concourse.bass_utils import run_bass_kernel_spmd

    nc = bacc.Bacc("TRN2", target_bir_lowering=False, num_devices=1)
    arrays = {f"in_{name}_dram": np.ascontiguousarray(inputs[name]) for name in _INS}
    arrays["in_ident_dram"] = np.eye(P, dtype=np.float32)
    arrays["in_rot_dram"] = rotary_tables()
    arrays["in_mask_dram"] = window_masks()
    args = [nc.dram_tensor(name, a.shape, mybir.dt.from_np(a.dtype), kind="ExternalInput").ap() for name, a in arrays.items()]
    out = nc.dram_tensor("out_0_dram", (B, S, D), F32, kind="ExternalOutput").ap()
    build(nc, *args, out)
    r = run_bass_kernel_spmd(nc, [arrays], core_ids=[0])
    return r.results[0]["out_0_dram"]
```

```python
from contextlib import ExitStack

import numpy as np

import concourse.bass as bass
import concourse.mybir as mybir

F32, F32R = mybir.dt.float32, mybir.dt.float32r
F16, BF16, I32 = mybir.dt.float16, mybir.dt.bfloat16, mybir.dt.int32
ALU = mybir.AluOpType
ACT = mybir.ActivationFunctionType
AX = mybir.AxisListType
RED_MAX = bass.bass_isa.ReduceOp.max
ds = bass.ds

P = 128
B, S, D = 4, 2048, 256
KD = D // P
WPB = S // P
NW = B * WPB
LAYERS, HEADS, DH = 2, 8, 64
INNER = HEADS * DH
HP = HEADS // 2
HID = int(D * 4 * 2 / 3)
HC = -(-HID // P)
HPAD = HC * P
EPS = 1e-5
QK_SCALE = 8.0
MASKED, ABOVE_ALL = 1e30, 3e38
EVEN_MASK, ODD_MASK = 3, 4
XS_SCALE = 2.0 ** 9
W1_TOP = 2.0 ** 13
NT = LAYERS * NW
BLOCKS_PER_BATCH = WPB + 1
XS_BLOCKS = (NT + NW) + (NT + NW) // WPB
XP_BLOCKS = NT + NT // WPB
SLOTS = 4
LAST_SLOT = NT + 5
FIRST_GROUP = 2
LAST_GROUP = NT // SLOTS - 1
PARTS = ((0, 0), (0, 1), (1, 0))
HALVINGS = DH.bit_length() - 1
W1_BANKS = (0, 1, 6, 3, 4, 5)


def wait(eng, sem, count):
    if not (isinstance(count, int) and count <= 0):
        eng.wait_ge(sem, count)


def wait_apart(eng, sem, count, passed):
    if not (isinstance(count, int) and count <= 0):
        eng.wait_ge(sem, count)
        eng.sem_inc(passed, 1)


def stream_block(t):
    return t + t // WPB + 1


def phase_a(nc, x_in, ident_in, x2_dram, xs_dram, xp_dram):
    x_v = x_in.rearrange("b (w p) d -> p (b w) d", p=P)
    x2_v = x2_dram.rearrange("(w p) d -> p w d", p=P)
    xs_v = xs_dram.rearrange("(w p) d -> p w d", p=P)
    chunks = S // 512
    e_full_start = 4
    loads = 4
    x_loaded_start = 16
    ctx_free_start = 4
    e_lo_start = 1
    xs_lo_start = 1
    xs_full_start = 2
    with ExitStack() as ctx:
        def sb(name, shape, dt=F32):
            return ctx.enter_context(nc.sbuf_tensor("a_" + name, shape, dt))

        def sem(name):
            return ctx.enter_context(nc.semaphore("a_" + name))

        ident_f = sb("ident_f", [P, P])
        ident = sb("ident", [P, P], F16)
        xn = sb("xn", [P, WPB, D])
        xn_hl = sb("xn_hl", [P, 2, 2, D], F16)
        xnT = sb("xnT", [P, 2, KD, S], F16)
        E = sb("E", [P, 2, WPB, S], F16)
        e32 = sb("e32", [P, S])
        xs32 = sb("xs32", [P, D])
        xs = sb("xs", [P, 2, WPB, D], F16)
        st_first, mv_first = sb("st_first", [P, WPB, 6]), sb("mv_first", [P, WPB, 2])
        var_first, rstd_first = sb("var_first", [P, WPB]), sb("rstd_first", [P, WPB])
        negmax_part, negmax = sb("negmax_part", [P, 2, 2]), sb("negmax", [P, 2])
        colsum = sb("colsum", [P, 2, 2])
        colsum_s = sb("colsum_s", [P, 2])
        inv_sum = sb("inv_sum", [P, 2])
        st_n, mv_n, var_n, rstd_n = sb("st_n", [P, 6]), sb("mv_n", [P, 2]), sb("var_n", [P, 1]), sb("rstd_n", [P, 1])
        st_c, mv_c, var_c = sb("st_c", [P, 6]), sb("mv_c", [P, 2]), sb("var_c", [P, 1])
        pow_c, rstd_c = sb("pow_c", [P, 1]), sb("rstd_c", [P, 1])
        st_x, mv_x, var_x, rstd_x = sb("st_x", [P, 6]), sb("mv_x", [P, 2]), sb("var_x", [P, 1]), sb("rstd_x", [P, 1])
        mhalf = sb("mhalf", [P, WPB])
        unscale = sb("unscale", [P, 1])
        x_res = sb("x_res", [P, 2, D])
        ln_c = sb("ln_c", [P, D])
        x2 = sb("x2", [P, 2, D])
        xo = sb("xo", [P, 2, D])
        zeros = sb("zeros", [3 * B, D])
        ps = ctx.enter_context(nc.psum_tensor("a_ps", [P, 8, 512], F32))
        ps_tr = [ps[:, 4 + i, 0:256].bitcast(F16).rearrange("p (h k n) -> p h k n", h=2, k=KD) for i in range(2)]

        consts_in, consts, pool_consts, x_loaded = sem("consts_in"), sem("consts"), sem("pool_consts"), sem("x_loaded")
        x_first = [sem(f"x_first{q}") for q in range(loads)]
        st_first_done, mv_first_done, var_first_ready, rstd_first_ready = (sem(n) for n in (
            "st_first_done", "mv_first_done", "var_first_ready", "rstd_first_ready"))
        stn, mvn, varn_ready, rstdn_ready, xn_ready, xn_hi, xn_lo = (sem(n) for n in (
            "stn", "mvn", "varn_ready", "rstdn_ready", "xn_ready", "xn_hi", "xn_lo"))
        trans_done, xnT_ready = sem("trans_done"), sem("xnT_ready")
        scores_done, part_max, max_ready, e_hi, e_full, e_lo = (sem(n) for n in (
            "scores_done", "part_max", "max_ready", "e_hi", "e_full", "e_lo"))
        sum_scaled, inv_ready, xs_full, xs_hi, xs_lo = (sem(n) for n in (
            "sum_scaled", "inv_ready", "xs_full", "xs_hi", "xs_lo"))
        ctx_done, stc, mvc, varc_ready, powc, rstdc_ready, ctx_free = (sem(n) for n in (
            "ctx_done", "stc", "mvc", "varc_ready", "powc", "rstdc_ready", "ctx_free"))
        x2_ready, stx, mvx, varx_ready, rstdx_ready, xo_ready = (sem(n) for n in (
            "x2_ready", "stx", "mvx", "varx_ready", "rstdx_ready", "xo_ready"))
        res_in = [sem(f"res_in{i}") for i in range(2)]
        x2_out = [sem(f"x2_out{i}") for i in range(2)]
        xo_out = [sem(f"xo_out{i}") for i in range(2)]
        zero_rows = sem("zero_rows")
        passed_dve, passed_pe = sem("passed_dve"), sem("passed_pe")
        block = ctx.enter_context(nc.Block())

        @block.sync
        def _(sp):
            sp.dma_start(ident_f[:], ident_in).then_inc(consts_in, 16)
            for q in range(loads):
                part = slice(q * WPB // loads, (q + 1) * WPB // loads)
                sp.dma_start(xn[:, part, :], x_v[:, part, :]).then_inc(x_first[q], 16)
            for u in range(2):
                sp.sem_inc(x2_out[u], 16)
                sp.sem_inc(xo_out[u], 16)
            sp.sem_inc(e_full, e_full_start)
            sp.sem_inc(x_loaded, x_loaded_start)
            sp.sem_inc(ctx_free, ctx_free_start)
            sp.sem_inc(e_lo, e_lo_start)
            sp.sem_inc(xs_lo, xs_lo_start)
            sp.sem_inc(xs_full, xs_full_start)
            sp.wait_ge(pool_consts, 1)
            rows = BLOCKS_PER_BATCH * P
            sp.dma_start(xs_dram.rearrange("(q r) d -> q r d", r=rows)[:, P - 1, :], zeros[:]).then_inc(zero_rows, 16)
            sp.dma_start(xp_dram.rearrange("(q r) d -> q r d", r=rows)[:, P - 1, :], zeros[0:2 * B, :]).then_inc(zero_rows, 16)
            for u in range(2):
                sp.dma_start(x_res[:, u, :], x_v[:, u, :]).then_inc(res_in[u], 16)
            with sp.Fori(0, B) as b:
                with sp.Fori(0, loads) as q:
                    sp.wait_ge(x_loaded, x_loaded_start + 16 * (b * loads + q))
                    sp.wait_ge(xs_full, xs_full_start + b * WPB + (q + 1) * (WPB // loads))
                    sp.dma_start(xn[:, ds(q * (WPB // loads), WPB // loads), :],
                                 x_v[:, ds(((b + 1) % B) * WPB + q * (WPB // loads), WPB // loads), :]).then_inc(x_loaded, 16)
                with sp.Fori(0, WPB // 2) as h:
                    for u in range(2):
                        g = b * WPB + 2 * h + u
                        sp.wait_ge(xo_ready, g + 1)
                        sp.dma_start(x2_v[:, ds(g, 1), :], x2[:, u, :]).then_inc(x2_out[u], 16)
                        sp.dma_start(xs_v[:, ds(stream_block(g), 1), :], xo[:, u, :]).then_inc(xo_out[u], 16)
                        sp.dma_start(x_res[:, u, :], x_v[:, ds((g + 2) % NW, 1), :]).then_inc(res_in[u], 16)
            for u in range(2):
                sp.wait_ge(x2_out[u], 16 * (NW // 2 + 1))
                sp.wait_ge(xo_out[u], 16 * (NW // 2 + 1))
                sp.wait_ge(res_in[u], 16 * (NW // 2 + 1))
            sp.wait_ge(zero_rows, 32)
            sp.wait_ge(x_loaded, x_loaded_start + 16 * B * loads)

        @block.gpsimd
        def _(pool):
            nc.gpsimd.memset(mhalf[:], -0.5)
            nc.gpsimd.memset(unscale[:], 1.0 / XS_SCALE)
            nc.gpsimd.memset(zeros[:], 0.0).then_inc(pool_consts, 1)
            pool.wait_ge(pool_consts, 1)

            def norm(g):
                pool.wait_ge(varn_ready, g + 1)
                nc.gpsimd.tensor_tensor(rstd_n[:], var_n[:], mhalf[:, 0:1], ALU.pow).then_inc(rstdn_ready, 1)

            def low_part(n, u):
                pool.wait_ge(xn_hi, n + 1)
                nc.gpsimd.tensor_tensor(xn_hl[:, u, 1, :], xn[:, ds(n % WPB, 1), :], xn_hl[:, u, 0, :], ALU.subtract).then_inc(xn_lo, 1)

            pool.wait_ge(var_first_ready, 1)
            nc.gpsimd.tensor_tensor(rstd_first[:], var_first[:], mhalf[:], ALU.pow).then_inc(rstd_first_ready, 1)
            with pool.Fori(0, WPB // 2) as h:
                for u in range(2):
                    low_part(2 * h + u, u)
            with pool.Fori(0, B) as b:
                with pool.Fori(0, WPB // 2) as h:
                    for u in range(2):
                        j = 2 * h + u
                        g = b * WPB + j
                        pool.wait_ge(inv_ready, g + 1)
                        pool.wait_ge(xs_lo, xs_lo_start + g)
                        nc.gpsimd.tensor_tensor(xs32[:], xn[:, ds(j, 1), :], inv_sum[:, u:u + 1].to_broadcast([P, D]), ALU.mult).then_inc(xs_full, 1)
                        pool.wait_ge(xs_full, xs_full_start + g + 1)
                        nc.gpsimd.tensor_copy(xs[:, 0, ds(j, 1), :], xs32[:]).then_inc(xs_hi, 1)
                        pool.wait_ge(xs_hi, g + 1)
                        nc.gpsimd.tensor_tensor(xs[:, 1, ds(j, 1), :], xs32[:], xs[:, 0, ds(j, 1), :], ALU.subtract).then_inc(xs_lo, 1)

                def norms(i, u, more):
                    g = b * WPB + i
                    pool.wait_ge(varc_ready, g + 1)
                    nc.gpsimd.tensor_tensor(pow_c[:], var_c[:], mhalf[:, 0:1], ALU.pow).then_inc(powc, 1)
                    pool.wait_ge(powc, g + 1)
                    nc.gpsimd.tensor_tensor(rstd_c[:], pow_c[:], unscale[:], ALU.mult).then_inc(rstdc_ready, 1)
                    if more:
                        norm(g + 1)
                    pool.wait_ge(varx_ready, g + 1)
                    nc.gpsimd.tensor_tensor(rstd_x[:], var_x[:], mhalf[:, 0:1], ALU.pow).then_inc(rstdx_ready, 1)
                    if more:
                        low_part(g + 1 + WPB, 1 - u)

                norm(b * WPB)
                low_part((b + 1) * WPB, 0)
                with pool.Fori(0, WPB // 2 - 1) as h:
                    for u in range(2):
                        norms(2 * h + u, u, True)
                for i in range(WPB - 2, WPB):
                    norms(i, i % 2, i < WPB - 1)

        @block.vector
        def _(dve):
            dve.wait_ge(consts_in, 16)
            nc.vector.tensor_copy(ident[:], ident_f[:]).then_inc(consts, 1)

            def prep_stats(g):
                tile = xn[:, ds(g % WPB, 1), :]
                nc.vector.bn_stats(st_n[:], tile).then_inc(stn, 1)
                wait_apart(dve, stn, g + 1, passed_dve)
                nc.vector.bn_aggr(mv_n[:], st_n[:]).then_inc(mvn, 1)
                dve.wait_ge(mvn, g + 1)
                nc.vector.tensor_scalar(var_n[:], mv_n[:, 1:2], EPS, None, ALU.add).then_inc(varn_ready, 1)

            def normalise(n, u, mean, rstd):
                tile = xn[:, ds(n % WPB, 1), :]
                nc.vector.tensor_scalar(tile, tile, mean, rstd, ALU.subtract, ALU.mult).then_inc(xn_ready, 1)
                dve.wait_ge(xn_ready, n + 1)
                wait(dve, trans_done, n - 1)
                nc.vector.tensor_scalar(xn_hl[:, u, 0, :], tile, 1.0, None, ALU.mult).then_inc(xn_hi, 1)

            for n in range(WPB):
                dve.wait_ge(x_first[n * loads // WPB], 16)
                nc.vector.bn_stats(st_first[:, n, :], xn[:, n, :]).then_inc(st_first_done, 1)
            for n in range(WPB):
                dve.wait_ge(st_first_done, n + 1)
                nc.vector.bn_aggr(mv_first[:, n, :], st_first[:, n, :]).then_inc(mv_first_done, 1)
            dve.wait_ge(mv_first_done, WPB)
            nc.vector.tensor_scalar(var_first[:], mv_first[:, :, 1], EPS, None, ALU.add).then_inc(var_first_ready, 1)
            dve.wait_ge(rstd_first_ready, 1)
            for n in range(WPB):
                normalise(n, n % 2, mv_first[:, n, 0:1], rstd_first[:, n:n + 1])

            with dve.Fori(0, B) as b:
                def row_max(j):
                    g = b * WPB + j
                    u = j % 2
                    for part in range(2):
                        dve.wait_ge(scores_done, 2 * g + part + 1)
                        banks = ds(chunks * u + part * (chunks - 1), 1 if part else chunks - 1)
                        nc.vector.tensor_reduce(negmax_part[:, ds(u, 1), part], ps[:, banks, :].rearrange("p c n -> p (c n)"),
                                                AX.X, ALU.max, negate=True).then_inc(part_max, 1)
                    dve.wait_ge(part_max, 2 * g + 2)
                    nc.vector.tensor_tensor(negmax[:, ds(u, 1)], negmax_part[:, ds(u, 1), 0], negmax_part[:, ds(u, 1), 1], ALU.min).then_inc(max_ready, 1)

                def low_part(j):
                    g = b * WPB + j
                    u = j % 2
                    dve.wait_ge(e_full, e_full_start + 2 * g + 2)
                    nc.vector.tensor_scalar(colsum_s[:, ds(u, 1)], colsum[:, ds(u, 1), 0], colsum[:, ds(u, 1), 1], 1.0 / XS_SCALE,
                                            ALU.add, ALU.mult).then_inc(sum_scaled, 1)
                    nc.vector.tensor_tensor(E[:, 1, ds(j, 1), :], e32[:], E[:, 0, ds(j, 1), :], ALU.subtract).then_inc(e_lo, 1)
                    dve.wait_ge(sum_scaled, g + 1)
                    dve.wait_ge(xs_full, xs_full_start + g - 1)
                    nc.vector.reciprocal(inv_sum[:, ds(u, 1)], colsum_s[:, ds(u, 1)]).then_inc(inv_ready, 1)

                row_max(0)
                with dve.Fori(1, WPB) as j:
                    row_max(j)
                    low_part(j - 1)
                low_part(WPB - 1)
                def next_stats(i):
                    g = b * WPB + i
                    if isinstance(i, int) and i % (WPB // loads) == 0:
                        wait_apart(dve, x_loaded, x_loaded_start + 16 * (b * loads + i // (WPB // loads) + 1), passed_dve)
                    prep_stats(g)

                def next_norm(i, u):
                    g = b * WPB + i
                    dve.wait_ge(rstdn_ready, g + 1)
                    normalise(g + WPB, u, mv_n[:, 0:1], rstd_n[:])

                def finish(i, bank, more):
                    g = b * WPB + i
                    u = bank % 2
                    context = ps[:, bank, 0:D]
                    dve.wait_ge(ctx_done, g + 1)
                    nc.vector.bn_stats(st_c[:], context).then_inc(stc, 1)
                    wait_apart(dve, stc, g + 1, passed_dve)
                    nc.vector.bn_aggr(mv_c[:], st_c[:]).then_inc(mvc, 1)
                    dve.wait_ge(mvc, g + 1)
                    nc.vector.tensor_scalar(var_c[:], mv_c[:, 1:2], XS_SCALE ** -2, EPS, ALU.mult, ALU.add).then_inc(varc_ready, 1)
                    if more:
                        next_stats(i + 1)
                    dve.wait_ge(rstdc_ready, g + 1)
                    nc.vector.tensor_scalar(ln_c[:], context, mv_c[:, 0:1], rstd_c[:], ALU.subtract, ALU.mult).then_inc(ctx_free, 1)
                    dve.wait_ge(ctx_free, ctx_free_start + g + 1)
                    dve.wait_ge(res_in[u], 16 * (g // 2) + 16)
                    dve.wait_ge(x2_out[u], 16 * (g // 2) + 16)
                    nc.vector.tensor_tensor(x2[:, u, :], ln_c[:], x_res[:, u, :], ALU.add).then_inc(x2_ready, 1)
                    dve.wait_ge(x2_ready, g + 1)
                    nc.vector.bn_stats(st_x[:], x2[:, u, :]).then_inc(stx, 1)
                    wait_apart(dve, stx, g + 1, passed_dve)
                    nc.vector.bn_aggr(mv_x[:], st_x[:]).then_inc(mvx, 1)
                    dve.wait_ge(mvx, g + 1)
                    nc.vector.tensor_scalar(var_x[:], mv_x[:, 1:2], EPS, None, ALU.add).then_inc(varx_ready, 1)
                    if more:
                        next_norm(i + 1, 1 - u)
                    dve.wait_ge(rstdx_ready, g + 1)
                    dve.wait_ge(xo_out[u], 16 * (g // 2) + 16)
                    nc.vector.tensor_scalar(xo[:, u, :], x2[:, u, :], mv_x[:, 0:1], rstd_x[:], ALU.subtract, ALU.mult).then_inc(xo_ready, 1)

                next_stats(0)
                next_norm(0, 0)
                with dve.Fori(0, WPB // 4 - 1) as h:
                    for u4 in range(4):
                        if u4 == 3:
                            wait_apart(dve, x_loaded, x_loaded_start + 16 * (b * loads + h + 2), passed_dve)
                        finish(4 * h + u4, u4, True)
                for i in range(WPB - 4, WPB):
                    finish(i, i % 4, i < WPB - 1)

        @block.scalar
        def _(act):
            def keep_transposed(n, u):
                act.wait_ge(trans_done, n + 1)
                nc.scalar.copy(xnT[:, :, :, ds((n % WPB) * P, P)], ps_tr[u]).then_inc(xnT_ready, 1)

            with act.Fori(0, WPB // 2) as h:
                for u in range(2):
                    keep_transposed(2 * h + u, u)
            with act.Fori(0, B) as b:
                with act.Fori(0, WPB // 2) as h:
                    for u in range(2):
                        j = 2 * h + u
                        g = b * WPB + j
                        scores = ps[:, 4 * u:4 * u + chunks, :].rearrange("p c n -> p (c n)")
                        act.wait_ge(max_ready, g + 1)
                        nc.scalar.activation(E[:, 0, ds(j, 1), :], scores, ACT.Exp, bias=negmax[:, u:u + 1]).then_inc(e_hi, 1)
                        act.wait_ge(e_lo, e_lo_start + g)
                        for half in range(2):
                            columns = slice(half * S // 2, (half + 1) * S // 2)
                            nc.scalar.activation(e32[:, columns], scores[:, columns], ACT.Exp, bias=negmax[:, u:u + 1],
                                                 accum_out=colsum[:, u, half:half + 1]).then_inc(e_full, 1)
                with act.Fori(0, WPB // 2) as h:
                    for u in range(2):
                        keep_transposed((b + 1) * WPB + 2 * h + u, u)

        @block.tensor
        def _(pe):
            def transposes(n, u):
                pe.wait_ge(xn_lo, n + 1)
                wait(pe, xnT_ready, n - 1)
                for part in range(2):
                    for k in range(KD):
                        last = nc.tensor.transpose(ps_tr[u][:, part, k, :], xn_hl[:, u, part, k * P:(k + 1) * P], ident[:])
                last.then_inc(trans_done, 1)

            pe.wait_ge(consts, 1)
            for n in range(2):
                transposes(n, n)
            with pe.Fori(1, WPB // 2) as h:
                for u in range(2):
                    transposes(2 * h + u, u)

            with pe.Fori(0, B) as b:
                with pe.Fori(0, WPB // 2) as h:
                    for u in range(2):
                        g = b * WPB + 2 * h + u
                        rows = ds((2 * h + u) * P, P)
                        for n in range(chunks):
                            pe.wait_ge(xnT_ready, b * WPB + (n + 1) * WPB // chunks)
                            wait_apart(pe, ctx_free, b * WPB + n + 1, passed_pe)
                            pe.wait_ge(e_full, 2 * g + n // 2 + 1)
                            for k in range(KD):
                                for a, c in ((0, 0), (0, 1), (1, 0)):
                                    last = nc.tensor.matmul(ps[:, 4 * u + n, :], xnT[:, a, k, rows], xnT[:, c, k, n * 512:(n + 1) * 512],
                                                            start=(k == 0 and a == 0 and c == 0), stop=(k == KD - 1 and a == 1))
                            if n >= chunks - 2:
                                last.then_inc(scores_done, 1)

                def products(i, bank, j):
                    for a, c in ((0, 0), (0, 1), (1, 0)):
                        last = nc.tensor.matmul(ps[:, bank, 0:D], E[:, a, j, ds(i * P, P)], xs[:, c, j, :],
                                                start=(j == 0 and a == 0 and c == 0), stop=(j == WPB - 1 and a == 1))
                    if j == WPB - 1:
                        last.then_inc(ctx_done, 1)

                def context(i, bank):
                    pe.wait_ge(ctx_free, b * WPB + i + 1)
                    for j in range(WPB):
                        products(i, bank, j)

                after = (b + 1) * WPB
                wait_apart(pe, ctx_free, ctx_free_start + b * WPB, passed_pe)
                pe.wait_ge(e_full, e_full_start + 2 * (b * WPB + WPB - 1))
                for last_rows in (False, True):
                    for j in (range(WPB - 2, WPB) if last_rows else range(WPB - 2)):
                        rows_made = WPB - 2 if j == 0 else j + 1
                        if rows_made > j + 1 or last_rows:
                            wait_apart(pe, e_lo, e_lo_start + b * WPB + rows_made, passed_pe)
                            wait_apart(pe, xs_lo, xs_lo_start + b * WPB + rows_made, passed_pe)
                        for i in range(2):
                            products(i, i, j)
                transposes(after, 0)
                with pe.Fori(0, WPB // 4 - 1) as h:
                    for u4 in range(4):
                        context(4 * h + u4 + 2, (u4 + 2) % 4)
                        transposes(after + 4 * h + u4 + 1, (u4 + 1) % 2)
                for i in range(WPB - 2, WPB):
                    context(i, i % 4)
                    transposes(after + i - 1, (i - 1) % 2)
                transposes(after + WPB - 1, (WPB - 1) % 2)


def in_range(t):
    return not isinstance(t, int) or 0 <= t < NT


def slots(eng, run):
    for s in range(FIRST_GROUP * SLOTS):
        run(s, s % SLOTS, s // 2)
    with eng.Fori(FIRST_GROUP, LAST_GROUP) as i:
        for r in range(SLOTS):
            run(SLOTS * i + r, r, SLOTS // 2 * i + r // 2)
    for s in range(LAST_GROUP * SLOTS, LAST_SLOT + 1):
        run(s, s % SLOTS, s // 2)


def phase_b(nc, w, consts, x2_dram, xs_dram, xp_dram, rot_dram, out):
    x2_v = x2_dram.rearrange("(w p) d -> p w d", p=P)
    out_v = out.rearrange("b (w p) d -> p (b w) d", p=P)
    xs_v = xs_dram.rearrange("(w p) d -> p w d", p=P)
    xp_v = xp_dram.rearrange("(w p) d -> p w d", p=P)
    rot_v = rot_dram.rearrange("(w p) n d -> p w (n d)", p=P)
    xs_prev = xs_dram[P - 1:-1, :].rearrange("(w p) d -> p w d", p=P)
    xp_prev = xp_dram[P - 1:-1, :].rearrange("(w p) d -> p w d", p=P)
    HALF = D // 2
    with ExitStack() as keep:
        def sb(name, shape, dt=F32):
            return keep.enter_context(nc.sbuf_tensor("b_" + name, shape, dt))

        wqkv = sb("wqkv", [P, LAYERS, 2, KD, 3 * INNER], F32R)
        w1 = sb("w1", [P, LAYERS, 2, KD, 2 * HPAD], F16)
        w1_unit = sb("w1_unit", [P, LAYERS])
        b1a = sb("b1a", [P, LAYERS, HC])
        b1g = sb("b1g", [P, LAYERS, HC])
        w2 = sb("w2", [P, LAYERS, HC, D])
        b2 = sb("b2", [P, LAYERS, D])
        wo = sb("wo", [P, LAYERS, 2, HP, D], F32R)
        mask = sb("mask", [P, 5, 2 * P], BF16)
        ident_f, ident_h = sb("ident_f", [P, P]), sb("ident_h", [P, P], F16)
        mhalf = sb("mhalf", [P, 2 * HEADS])
        ps = keep.enter_context(nc.psum_tensor("b_ps", [P, 8, 512], F32))

        with ExitStack() as ctx:
            def sb(name, shape, dt=F32):
                return ctx.enter_context(nc.sbuf_tensor("p_" + name, shape, dt))

            def sem(name):
                return ctx.enter_context(nc.semaphore("p_" + name))

            wqkv_f = sb("wqkv_f", [P, LAYERS, KD, 3 * INNER])
            w1_f = sb("w1_f", [P, LAYERS, KD, 2 * HPAD])
            b1_f = sb("b1_f", [P, LAYERS, 2, HC])
            lg, lb = sb("lg", [P, LAYERS, KD]), sb("lb", [P, LAYERS, KD])
            rot_all = sb("rot_all", [P, 4, LAYERS * WPB, DH])
            mask_f = sb("mask_f", [P, 5, 2 * P])
            wo_f = sb("wo_f", [P, LAYERS, HP, D])
            head_scale = sb("head_scale", [P, 2, 2, LAYERS, DH])
            top, top_all, top_min = sb("top", [P, LAYERS]), sb("top_all", [P, LAYERS]), sb("top_min", [P, LAYERS])
            pow2, pow2_inv, w1_scale = sb("pow2", [P, LAYERS]), sb("pow2_inv", [P, LAYERS]), sb("w1_scale", [P, LAYERS])
            cleared, loaded_w1, loaded_qkv, loaded_rot, loaded = (sem(n) for n in ("cleared", "loaded_w1", "loaded_qkv", "loaded_rot", "loaded"))
            loaded_wo, wo_hi, rot_scaled, rot_stored = sem("loaded_wo"), sem("wo_hi"), sem("rot_scaled"), sem("rot_stored")
            qkv_hi, bias_done, w1_gained, top_ready, top_shared = (sem(n) for n in ("qkv_hi", "bias_done", "w1_gained", "top_ready", "top_shared"))
            step, scaled, w1_hi, bias_added = sem("step"), sem("scaled"), sem("w1_hi"), sem("bias_added")
            full = HC - 1
            rest = HID - full * P
            block = ctx.enter_context(nc.Block())
            DMAS_W1, DMAS_ROT, DMAS = LAYERS * 7, 4 * LAYERS + 6, 5

            @block.sync
            def _(sp):
                sp.dma_start(wqkv_f[:].rearrange("p l k n -> p (l k) n"), w["wqkv"].rearrange("l (k p) n -> p (l k) n", p=P)).then_inc(loaded_qkv, 16)
                sp.wait_ge(cleared, 3)
                for l in range(LAYERS):
                    for half in range(2):
                        sp.dma_start(w1_f[:, l, :, half * HPAD:half * HPAD + HID],
                                     w["w1"][l, :, half * HID:(half + 1) * HID].rearrange("(k p) n -> p k n", p=P)).then_inc(loaded_w1, 16)
                        b1_half = w["b1"][l, half * HID:(half + 1) * HID]
                        sp.dma_start(b1_f[:, l, half, 0:full], b1_half[0:full * P].rearrange("(c p) -> p c", p=P), allow_slow_non_contiguous=True).then_inc(loaded_w1, 16)
                        sp.dma_start(b1_f[0:rest, l, half, full:HC], b1_half[full * P:HID].rearrange("(p c) -> p c", c=1), allow_slow_non_contiguous=True).then_inc(loaded_w1, 16)
                    sp.dma_start(w2[:, l, 0:full, :], w["w2"][l, 0:full * P, :].rearrange("(c p) d -> p c d", p=P)).then_inc(loaded_w1, 16)
                sp.dma_start(b2[:], w["b2"].partition_broadcast(P)).then_inc(loaded_wo, 16)
                sp.dma_start(lg[:], w["ln_g"].rearrange("l (k p) -> p l k", p=P), allow_slow_non_contiguous=True).then_inc(loaded, 16)
                sp.dma_start(lb[:], w["ln_b"].rearrange("l (k p) -> p l k", p=P), allow_slow_non_contiguous=True).then_inc(loaded, 16)
                sp.dma_start(w2[0:rest, :, full, :], w["w2"][:, full * P:HID, :].rearrange("l p d -> p l d")).then_inc(loaded, 16)
                sp.dma_start(ident_f[:], consts["ident"]).then_inc(loaded, 16)
                sp.dma_start(mask_f[:], consts["mask"].rearrange("n p j -> p n j")).then_inc(loaded, 16)
                for l in range(LAYERS):
                    for n in range(4):
                        sp.dma_start(rot_all[:, n, l * WPB:(l + 1) * WPB, :], consts["rot"][n].rearrange("(w p) d -> p w d", p=P)).then_inc(loaded_rot, 16)
                for n, name in enumerate(("q_scale", "k_scale")):
                    half = DH // 2
                    sp.dma_start(head_scale[:, n, 0], w[name].partition_broadcast(P)).then_inc(loaded_rot, 16)
                    sp.dma_start(head_scale[:, n, 1, :, 0:half], w[name][:, half:DH].partition_broadcast(P)).then_inc(loaded_rot, 16)
                    sp.dma_start(head_scale[:, n, 1, :, half:DH], w[name][:, 0:half].partition_broadcast(P)).then_inc(loaded_rot, 16)
                sp.dma_start(wo_f[:].rearrange("p l h d -> p (l h) d"), w["wo"].rearrange("l (h p) d -> p (l h) d", p=P)).then_inc(loaded_wo, 16)
                sp.wait_ge(loaded_wo, 32)
                sp.wait_ge(rot_scaled, 4 * LAYERS)
                for n in range(4):
                    sp.dma_start(rot_dram.rearrange("(w p) n d -> p n w d", p=P)[:, n], rot_all[:, n]).then_inc(rot_stored, 16)
                sp.wait_ge(rot_stored, 64)

            @block.gpsimd
            def _(pool):
                nc.gpsimd.memset(w1_f[:, :, :, HID:HPAD], 0.0).then_inc(cleared, 1)
                nc.gpsimd.memset(w1_f[:, :, :, HPAD + HID:2 * HPAD], 0.0)
                nc.gpsimd.memset(b1_f[:, :, :, full:HC], 0.0).then_inc(cleared, 1)
                nc.gpsimd.memset(w2[:, :, full, :], 0.0).then_inc(cleared, 1)
                nc.gpsimd.memset(mhalf[:], -0.5).then_inc(cleared, 1)
                pool.wait_ge(cleared, 4)
                pool.wait_ge(top_ready, LAYERS)
                nc.gpsimd.partition_all_reduce(top_all[:], top[:], P, RED_MAX).then_inc(top_shared, 1)
                pool.wait_ge(top_shared, 1)

            @block.tensor
            def _(pe):
                pe.wait_ge(loaded_w1, 16 * DMAS_W1)
                pe.wait_ge(loaded, 16 * DMAS)
                pe.wait_ge(cleared, 4)
                for l in range(LAYERS):
                    for c in range(2 * HC):
                        for k in range(KD):
                            last = nc.tensor.matmul(ps[:, l, c:c + 1], w1_f[:, l, k, c * P:(c + 1) * P], lb[:, l, k:k + 1], start=(k == 0), stop=(k == KD - 1))
                last.then_inc(bias_done, 1)

            @block.scalar
            def _(act):
                act.wait_ge(loaded_qkv, 16)
                for l in range(LAYERS):
                    nc.scalar.copy(wqkv[:, l, 0], wqkv_f[:, l]).then_inc(qkv_hi, 1)
                act.wait_ge(loaded_wo, 32)
                for l in range(LAYERS):
                    nc.scalar.copy(wo[:, l, 0], wo_f[:, l]).then_inc(wo_hi, 1)

            @block.vector
            def _(dve):
                dve.wait_ge(loaded, 16 * DMAS)
                nc.vector.tensor_copy(ident_h[:], ident_f[:])
                nc.vector.tensor_copy(mask[:], mask_f[:])
                dve.wait_ge(bias_done, 1)
                for l in range(LAYERS):
                    for k in range(KD):
                        nc.vector.tensor_scalar(w1_f[:, l, k, :], w1_f[:, l, k, :], lg[:, l, k:k + 1], None, ALU.mult).then_inc(w1_gained, 1)
                dve.wait_ge(w1_gained, LAYERS * KD)
                for l in range(LAYERS):
                    nc.vector.tensor_reduce(top[:, l:l + 1], w1_f[:, l].rearrange("p k n -> p (k n)"), AX.X, ALU.max, apply_absolute_value=True).then_inc(top_ready, 1)
                for l in range(LAYERS):
                    dve.wait_ge(qkv_hi, l + 1)
                    nc.vector.tensor_tensor(wqkv[:, l, 1], wqkv_f[:, l], wqkv[:, l, 0], ALU.subtract)
                    dve.wait_ge(wo_hi, l + 1)
                    nc.vector.tensor_tensor(wo[:, l, 1], wo_f[:, l], wo[:, l, 0], ALU.subtract)
                dve.wait_ge(loaded_rot, 16 * DMAS_ROT)
                for n in range(4):
                    for l in range(LAYERS):
                        windows = rot_all[:, n, l * WPB:(l + 1) * WPB, :]
                        nc.vector.tensor_tensor(windows, windows, head_scale[:, n // 2, n % 2, l:l + 1, :].to_broadcast([P, WPB, DH]), ALU.mult).then_inc(rot_scaled, 1)
                dve.wait_ge(top_shared, 1)
                nc.vector.tensor_scalar(top_min[:], top_all[:], 1e-30, None, ALU.max).then_inc(step, 1)
                dve.wait_ge(step, 1)
                nc.vector.tensor_scalar(pow2[:].bitcast(I32), top_min[:].bitcast(I32), 0x7F800000, None, ALU.bitwise_and).then_inc(step, 1)
                dve.wait_ge(step, 2)
                nc.vector.reciprocal(pow2_inv[:], pow2[:]).then_inc(step, 1)
                nc.vector.tensor_scalar(w1_unit[:], pow2[:], 1.0 / W1_TOP, None, ALU.mult).then_inc(step, 1)
                dve.wait_ge(step, 4)
                nc.vector.tensor_scalar(w1_scale[:], pow2_inv[:], W1_TOP, None, ALU.mult).then_inc(step, 1)
                dve.wait_ge(step, 5)
                for l in range(LAYERS):
                    nc.vector.tensor_scalar(w1_f[:, l], w1_f[:, l], w1_scale[:, l:l + 1], None, ALU.mult).then_inc(scaled, 1)
                    dve.wait_ge(scaled, l + 1)
                    nc.vector.tensor_copy(w1[:, l, 0], w1_f[:, l]).then_inc(w1_hi, 1)
                    dve.wait_ge(w1_hi, l + 1)
                    nc.vector.tensor_tensor(w1[:, l, 1], w1_f[:, l], w1[:, l, 0], ALU.subtract)
                    nc.vector.tensor_scalar(w2[:, l], w2[:, l], w1_unit[:, l:l + 1], None, ALU.mult)
                    nc.vector.tensor_tensor(b1g[:, l, :], ps[:, l, HC:2 * HC], b1_f[:, l, 1, :], ALU.add)
                    nc.vector.tensor_tensor(b1_f[:, l, 0, :], ps[:, l, 0:HC], b1_f[:, l, 0, :], ALU.add).then_inc(bias_added, 1)
                    dve.wait_ge(bias_added, l + 1)
                    nc.vector.tensor_scalar(b1a[:, l, :], b1_f[:, l, 0, :], w1_scale[:, l:l + 1], None, ALU.mult)

        with ExitStack() as ctx:
            def sb(name, shape, dt=F32):
                return ctx.enter_context(nc.sbuf_tensor("b_" + name, shape, dt))

            def sem(name):
                return ctx.enter_context(nc.semaphore("b_" + name))

            rot = sb("rot", [P, 2, 4, DH])
            hx = sb("hx", [P, 2, D])
            xr = sb("xr", [P, 2, D])
            hT_hi, hT_lo = sb("hT_hi", [P, KD, P], F32R), sb("hT_lo", [P, KD, P], F32R)
            v = sb("v", [P, 4, INNER])
            kT = sb("kT", [P, 2, HEADS, 2 * P], F32R)
            sq = sb("sq", [P, 2 * HEADS, DH])
            ss_min = sb("ss_min", [P, 2 * HEADS])
            rn = sb("rn", [P, 2, 2 * HEADS])
            t1, t2 = sb("t1", [P, 2, INNER]), sb("t2", [P, 2, INNER])
            qr, kr = sb("qr", [P, INNER]), sb("kr", [P, INNER])
            qT = sb("qT", [P, 2, HP, P], F32R)
            negmax = sb("negmax", [P, HEADS])
            mask_now = sb("mask_now", [P, 2 * P], BF16)
            probs = sb("probs", [P, HEADS, 2 * P])
            rowsum, rinv = sb("rowsum", [P, HEADS]), sb("rinv", [P, HEADS])
            probsT = sb("probsT", [P, HP, 512])
            oT = sb("oT", [P, 2, HP, P], F32R)
            xp = sb("xp", [P, 2, D])
            xb = sb("xb", [P, 4, D])
            h2 = sb("h2", [P, 2, D])
            st2, mv2, var2, rstd2 = sb("st2", [P, 6]), sb("mv2", [P, 2]), sb("var2", [P, 1]), sb("rstd2", [P, 1])
            xh, xh_hl = sb("xh", [P, D]), sb("xh_hl", [P, 2, D], F16)
            h2T = sb("h2T", [P, 2, KD, 2 * P], F16)
            gl = sb("gl", [P, 2, 2 * P])
            hid = sb("hid", [P, HC, 2 * P])
            xpp = sb("xpp", [P, 2, D])
            stf, mvf = sb("stf", [P, 2, 6]), sb("mvf", [P, 2, 2])
            varf, rstdf = sb("varf", [P, 2]), sb("rstdf", [P, 2])
            x2 = sb("x2", [P, 2, D])
            fin = sb("fin", [P, 2, D])

            rot_loaded, passed_dve, passed_sp = sem("rot_loaded"), sem("passed_dve"), sem("passed_sp")
            hx_loaded, xr_loaded, h2_loaded, x2_loaded = (sem(n) for n in ("hx_loaded", "xr_loaded", "h2_loaded", "x2_loaded"))
            xp_stored, xpp_stored, fin_stored = (sem(n) for n in ("xp_stored", "xpp_stored", "fin_stored"))
            hT_done, hT_hi_kept, hT_lo_kept = (sem(n) for n in ("hT_done", "hT_hi_kept", "hT_lo_kept"))
            v_done, q_done, k_done, v_kept = (sem(n) for n in ("v_done", "q_done", "k_done", "v_kept"))
            q_sq, k_sq = sem("q_sq"), sem("k_sq")
            q_terms, k_terms = sem("q_terms"), sem("k_terms")
            ss_halved, ss_ready, rn_ready = sem("ss_halved"), sem("ss_ready"), sem("rn_ready")
            qr_ready, kr_sum, kr_ready = sem("qr_ready"), sem("kr_sum"), sem("kr_ready")
            kT_done, qT_done, kT_hi, kT_lo, qT_hi, qT_lo = (sem(n) for n in (
                "kT_done", "qT_done", "kT_hi", "kT_lo", "qT_hi", "qT_lo"))
            scores_done, mask_ready = sem("scores_done"), sem("mask_ready")
            scores_kept, exp_done = sem("scores_kept"), sem("exp_done")
            rinv_ready, probs_ready = sem("rinv_ready"), sem("probs_ready")
            pT_done, pT_kept = sem("pT_done"), sem("pT_kept")
            pv_done, oT_hi, oT_lo, wo_done, xp_ready, xb_ready = (sem(n) for n in ("pv_done", "oT_hi", "oT_lo", "wo_done", "xp_ready", "xb_ready"))
            st2_ready, mv2_ready, var2_ready, rstd2_ready = (sem(n) for n in ("st2_ready", "mv2_ready", "var2_ready", "rstd2_ready"))
            xh_ready, xh_hi, xh_lo, h2T_done, h2T_kept = (sem(n) for n in ("xh_ready", "xh_hi", "xh_lo", "h2T_done", "h2T_kept"))
            w1_done, gelu_done, hid_ready = sem("w1_done"), sem("gelu_done"), sem("hid_ready")
            w2_done, xpp_ready = sem("w2_done"), sem("xpp_ready")
            stf_ready, mvf_ready, varf_ready = sem("stf_ready"), sem("mvf_ready"), sem("varf_ready")
            rstdf_ready, xf_ready, fin_ready = sem("rstdf_ready"), sem("xf_ready"), sem("fin_ready")
            ps_h2T = ps[:, 7, 0:D].bitcast(F16).rearrange("p (a k n) -> p a k n", a=2, k=KD)
            vk_cleared = sem("vk_cleared")
            block = ctx.enter_context(nc.Block())

            def by_head(ap):
                return ap.rearrange("p (h d) -> p h d", d=DH)

            def by_pair(ap):
                return ap.rearrange("p (h n) -> p h n", h=HP)

            @block.sync
            def _(sp):
                def load_hx(t, parity):
                    n = stream_block(t)
                    sp.dma_start(hx[:, parity, 0:HALF], xs_v[:, ds(n, 1), 0:HALF]).then_inc(hx_loaded, 16)
                    sp.dma_start(hx[:, parity, HALF:D], xs_prev[:, ds(n - 1, 1), HALF:D]).then_inc(hx_loaded, 16)

                def load_rot(t, parity):
                    sp.dma_start(rot[:, parity], rot_v[:, ds((t // NW) * WPB + t % WPB, 1), :]).then_inc(rot_loaded, 16)

                load_hx(0, 0)
                load_rot(0, 0)

                def run(s, r, pairs):
                    j = pairs - 3
                    if r % 2 == 0 and in_range(2 * j):
                        wait_apart(sp, xpp_ready, 2 * j + 2, passed_sp)
                        wait(sp, xpp_stored, 16 * j)
                        sp.dma_start(xs_v[:, ds(stream_block(2 * j + NW), 2), :], xpp[:]).then_inc(xpp_stored, 16)
                    if r % 2 == 1 and in_range(2 * j):
                        wait_apart(sp, fin_ready, j + 1, passed_sp)
                        wait(sp, fin_stored, 16 * j)
                        sp.dma_start(out_v[:, ds((2 * j) % NW, 2), :], fin[:]).then_inc(fin_stored, 16)
                    if r % 2 == 1 and in_range(2 * j + 2):
                        wait(sp, x2_loaded, 16 * (j + 1))
                        sp.dma_start(x2[:], x2_v[:, ds((2 * j + 2) % NW, 2), :]).then_inc(x2_loaded, 16)
                    if in_range(s + 1):
                        wait(sp, hT_done, s)
                        sp.wait_ge(hx_loaded, 32 * (s + 1))
                        load_hx(s + 1, (r + 1) % 2)
                        wait_apart(sp, k_terms, 3 * s, passed_sp)
                        sp.wait_ge(rot_loaded, 16 * (s + 1))
                        load_rot(s + 1, (r + 1) % 2)
                    t = s - 1
                    if in_range(t):
                        wait_apart(sp, xp_ready, t - 1, passed_sp)
                        wait(sp, xr_loaded, 16 * t)
                        sp.dma_start(xr[:, (r - 1) % 2, :], xs_v[:, ds(stream_block(t), 1), :]).then_inc(xr_loaded, 16)
                    t = s - 2
                    if in_range(t):
                        n = stream_block(t)
                        sp.wait_ge(xp_ready, t + 1)
                        sp.dma_start(xp_v[:, ds(n, 1), :], xp[:, r % 2, :]).then_inc(xp_stored, 16)
                        wait_apart(sp, xp_stored, 16 * (t + 1), passed_sp)
                        wait_apart(sp, xh_ready, t - 1, passed_sp)
                        wait(sp, h2_loaded, 32 * t)
                        sp.dma_start(h2[:, r % 2, 0:HALF], xp_v[:, ds(n, 1), 0:HALF]).then_inc(h2_loaded, 16)
                        sp.dma_start(h2[:, r % 2, HALF:D], xp_prev[:, ds(n - 1, 1), HALF:D]).then_inc(h2_loaded, 16)

                slots(sp, run)
                sp.wait_ge(xpp_stored, 16 * (NT // 2))
                sp.wait_ge(fin_stored, 16 * (NT // 2))

            @block.tensor
            def _(pe):
                def transpose_hx(t, r):
                    pe.wait_ge(hx_loaded, 32 * (t + 1))
                    wait(pe, h2T_kept, t - 3)
                    for k in range(KD):
                        last = nc.tensor.transpose(ps[:, 7, k * P:(k + 1) * P], hx[:, r % 2, k * P:(k + 1) * P], ident_f[:])
                    last.then_inc(hT_done, 1)

                def transpose_h2(t):
                    if in_range(t):
                        pe.wait_ge(xh_hi, t + 1)
                        pe.wait_ge(xh_lo, t + 1)
                        if in_range(t + 1):
                            pe.wait_ge(oT_lo, t + 2)
                        else:
                            pe.wait_ge(h2T_kept, t)
                        for part in range(2):
                            for k in range(KD):
                                last = nc.tensor.transpose(ps_h2T[:, part, k, :], xh_hl[:, part, k * P:(k + 1) * P], ident_h[:])
                        last.then_inc(h2T_done, 1)

                def run(s, r, pairs):
                    t = s - 1
                    if in_range(t):
                        pe.wait_ge(kr_ready, t + 1)
                        wait(pe, scores_kept, HEADS * t)
                        if r % 2 == 1:
                            wait(pe, hid_ready, HC * (pairs - 2) + W1_BANKS.index(6) + 1)
                        for p in range(HP):
                            last = nc.tensor.transpose(ps[:, 6, p * P:(p + 1) * P], kr[:, p * P:(p + 1) * P], ident_f[:])
                        last.then_inc(kT_done, 1)
                        pe.wait_ge(qr_ready, t + 1)
                        pe.wait_ge(v_kept, t + 1)
                        wait(pe, xp_ready, s - 2)
                        for p in range(HP):
                            last = nc.tensor.transpose(ps[:, 2, p * P:(p + 1) * P], qr[:, p * P:(p + 1) * P], ident_f[:])
                        last.then_inc(qT_done, 1)
                    if in_range(s):
                        pe.wait_ge(hT_hi_kept, s + 1)
                        pe.wait_ge(hT_lo_kept, s + 1)
                        for bank, done in ((0, q_done), (1, k_done), (2, v_done)):
                            if bank == 2:
                                wait(pe, qT_lo, s)
                            else:
                                wait(pe, (q_terms, k_terms)[bank], 3 * s)
                                if r % 2 == 1:
                                    wait(pe, hid_ready, HC * (pairs - 2) + bank + 1)
                            for k in range(KD):
                                for a, hT, part in ((0, hT_hi, 0), (1, hT_hi, 1), (2, hT_lo, 0)):
                                    last = nc.tensor.matmul(ps[:, bank, :], hT[:, k, :],
                                                            wqkv[:, ds(s // NW, 1), part, k, bank * INNER:(bank + 1) * INNER],
                                                            start=(k == 0 and a == 0), stop=(k == KD - 1 and a == 2))
                            last.then_inc(done, 1)
                    t = s - 2
                    if in_range(t):
                        if r % 2 == 0:
                            wait(pe, xpp_ready, s - 4)
                        else:
                            wait(pe, hid_ready, HC * (pairs - 1))
                        for p in range(HP):
                            if p == HP - 1 and in_range(s - 1):
                                pe.wait_ge(kT_lo, 2 * s)
                            pe.wait_ge(probs_ready, HEADS * t + 2 * p + 2)
                            for n in range(4):
                                last = nc.tensor.transpose(ps[:, 3 + p, n * P:(n + 1) * P],
                                                           probs[:, 2 * p + n // 2, (n % 2) * P:(n % 2 + 1) * P], ident_f[:])
                            last.then_inc(pT_done, 1)
                        pe.wait_ge(v_kept, t + 1)
                        if not in_range(s):
                            pe.wait_ge(h2T_kept, s - 3)
                        for p in range(HP):
                            pe.wait_ge(pT_kept, HP * t + p + 1)
                            for c in range(2):
                                window = (r - 2 - (r + c) % 2) % 4
                                for h in range(2):
                                    last = nc.tensor.matmul(ps[h * DH:(h + 1) * DH, 7, p * P:(p + 1) * P],
                                                            v[:, window, (2 * p + h) * DH:(2 * p + h + 1) * DH],
                                                            probsT[:, p, (2 * h + c) * P:(2 * h + c + 1) * P],
                                                            start=(c == 0), stop=(c == 1))
                        last.then_inc(pv_done, 1)
                    t = s - 1
                    if in_range(t):
                        pe.wait_ge(kT_lo, 2 * (t + 1))
                        pe.wait_ge(qT_lo, t + 1)
                        for p in range(HP):
                            if p == HP // 2:
                                transpose_h2(s - 3)
                            for h in range(2):
                                for a, (qp, kp) in enumerate(PARTS):
                                    last = nc.tensor.matmul(ps[:, 3 + p, h * 2 * P:(h + 1) * 2 * P], qT[:, qp, p, :], kT[:, kp, 2 * p + h, :],
                                                            start=(a == 0), stop=(a == 2))
                            last.then_inc(scores_done, 1)
                    else:
                        transpose_h2(s - 3)
                    t = s - 2
                    if in_range(t):
                        pe.wait_ge(oT_lo, t + 1)
                        if in_range(s):
                            pe.wait_ge(v_kept, s + 1)
                        else:
                            pe.wait_ge(xp_ready, s - 2)
                        for p in range(HP):
                            for a, (op, wp) in enumerate(PARTS):
                                last = nc.tensor.matmul(ps[:, 2, 0:D], oT[:, op, p, :], wo[:, ds(t // NW, 1), wp, p, :],
                                                        start=(p == 0 and a == 0), stop=(p == HP - 1 and a == 2))
                        last.then_inc(wo_done, 1)
                    if in_range(s + 1):
                        transpose_hx(s + 1, r + 1)
                    j = pairs - 2
                    if r % 2 == 0 and in_range(2 * j):
                        pe.wait_ge(h2T_kept, 2 * j + 2)
                        if not in_range(s - 2):
                            pe.wait_ge(xpp_ready, s - 4)
                        for c, bank in enumerate(W1_BANKS):
                            if bank < 2 and in_range(s):
                                pe.wait_ge((q_terms, k_terms)[bank], 3 * (s + 1))
                            if bank > 2 and in_range(s - 1):
                                pe.wait_ge(scores_kept, HEADS * (s - 1) + 2 * (bank - 3) + 2)
                            for half in range(2):
                                for k in range(KD):
                                    for a, (wp, hp) in enumerate(PARTS):
                                        first = half * HPAD + c * P
                                        last = nc.tensor.matmul(ps[:, bank, half * 2 * P:(half + 1) * 2 * P],
                                                                w1[:, ds((2 * j) // NW, 1), wp, k, first:first + P], h2T[:, hp, k, :],
                                                                start=(k == 0 and a == 0), stop=(k == KD - 1 and a == 2))
                            last.then_inc(w1_done, 1)
                    if r % 2 == 1 and in_range(2 * j):
                        pe.wait_ge(hid_ready, HC * (j + 1))
                        if in_range(s - 1):
                            pe.wait_ge(scores_kept, HEADS * (s - 1) + 2)
                        for n in range(2):
                            for c in range(HC):
                                last = nc.tensor.matmul(ps[:, 3, n * D:(n + 1) * D], hid[:, c, n * P:(n + 1) * P], w2[:, ds((2 * j) // NW, 1), c, :],
                                                        start=(c == 0), stop=(c == HC - 1))
                        last.then_inc(w2_done, 1)

                transpose_hx(0, 0)
                slots(pe, run)

            @block.scalar
            def _(act):
                def keep_hT(t):
                    act.wait_ge(hT_done, t + 1)
                    wait(act, k_done, t)
                    nc.scalar.copy(hT_hi[:], ps[:, 7, 0:D].rearrange("p (k n) -> p k n", k=KD)).then_inc(hT_hi_kept, 1)

                def keep_h2T(t, r, pairs):
                    if in_range(t):
                        act.wait_ge(h2T_done, t + 1)
                        if r % 2 == 1:
                            wait(act, w1_done, HC * (pairs - 1))
                        n = (r - 3) % 2
                        nc.scalar.copy(h2T[:, :, :, n * P:(n + 1) * P], ps_h2T).then_inc(h2T_kept, 1)

                def run(s, r, pairs):
                    t = s - 1
                    if in_range(t):
                        act.wait_ge(kT_done, t + 1)
                        wait(act, scores_done, HP * t)
                        par = (r - 1) % 2
                        for h in range(2):
                            rows = slice(h * DH, (h + 1) * DH)
                            nc.scalar.copy(kT[rows, 0, h::2, par * P:(par + 1) * P], by_pair(ps[rows, 6, :])).then_inc(kT_hi, 1)
                        act.wait_ge(qT_done, t + 1)
                        nc.scalar.copy(qT[:, 0], by_pair(ps[:, 2, :])).then_inc(qT_hi, 1)
                    if in_range(s):
                        wait(act, ss_ready, s)
                        act.wait_ge(q_done, s + 1)
                        nc.scalar.activation(sq[:, 0:HEADS, :], by_head(ps[:, 0, :]), ACT.Square).then_inc(q_sq, 1)
                        act.wait_ge(k_done, s + 1)
                        nc.scalar.activation(sq[:, HEADS:2 * HEADS, :], by_head(ps[:, 1, :]), ACT.Square).then_inc(k_sq, 1)
                        act.wait_ge(v_done, s + 1)
                        wait(act, pv_done, s - 2)
                        nc.scalar.copy(v[:, r, :], ps[:, 2, :]).then_inc(v_kept, 1)
                    t = s - 2
                    if in_range(t):
                        wait(act, pv_done, t)
                        for p in range(HP):
                            act.wait_ge(pT_done, HP * t + p + 1)
                            nc.scalar.copy(probsT[:, p, :], ps[:, 3 + p, :]).then_inc(pT_kept, 1)
                        act.wait_ge(pv_done, t + 1)
                        wait(act, wo_done, t)
                        nc.scalar.copy(oT[:, 0], by_pair(ps[:, 7, :])).then_inc(oT_hi, 1)
                    t = s - 1
                    if in_range(t):
                        for p in range(HP):
                            if p == HP // 2:
                                keep_h2T(s - 3, r, pairs)
                            for h in range(2 * p, 2 * p + 2):
                                act.wait_ge(scores_kept, HEADS * t + h + 1)
                                nc.scalar.activation(probs[:, h, :], probs[:, h, :], ACT.Exp, bias=negmax[:, h:h + 1], scale=-1.0,
                                                     accum_out=rowsum[:, h:h + 1]).then_inc(exp_done, 1)
                    else:
                        keep_h2T(s - 3, r, pairs)
                    if in_range(s + 1):
                        keep_hT(s + 1)
                    j = pairs - 2
                    if r % 2 == 0 and in_range(2 * j):
                        for c, bank in enumerate(W1_BANKS):
                            wait(act, hid_ready, HC * j + c - 1)
                            act.wait_ge(w1_done, HC * j + c + 1)
                            nc.scalar.activation(gl[:, c % 2, :], ps[:, bank, 2 * P:4 * P], ACT.Gelu,
                                                 bias=b1g[:, ds((2 * j) // NW, 1), c], scale=w1_unit[:, ds((2 * j) // NW, 1)]).then_inc(gelu_done, 1)

                act.wait_ge(vk_cleared, 2)
                keep_hT(0)
                slots(act, run)

            @block.vector
            def _(dve):
                def keep_hT(t):
                    dve.wait_ge(hT_hi_kept, t + 1)
                    nc.vector.tensor_tensor(hT_lo[:], ps[:, 7, 0:D].rearrange("p (k n) -> p k n", k=KD), hT_hi[:], ALU.subtract).then_inc(hT_lo_kept, 1)

                def rotate(s, r, n, squared, terms, used):
                    if in_range(s):
                        dve.wait_ge(rot_loaded, 16 * (s + 1))
                        dve.wait_ge(squared, s + 1)
                        wait(dve, used, s)
                        x = by_head(ps[:, n, :])
                        half = DH // 2

                        def factor(which, lo, hi):
                            return rot[:, r % 2, which:which + 1, lo:hi].to_broadcast([P, HEADS, hi - lo])

                        t2_h = by_head(t2[:, n, :])
                        nc.vector.tensor_tensor(by_head(t1[:, n, :]), x, factor(2 * n, 0, DH), ALU.mult).then_inc(terms, 1)
                        nc.vector.tensor_tensor(t2_h[:, :, 0:half], x[:, :, half:DH], factor(2 * n + 1, 0, half), ALU.mult).then_inc(terms, 1)
                        nc.vector.tensor_tensor(t2_h[:, :, half:DH], x[:, :, 0:half], factor(2 * n + 1, half, DH), ALU.mult).then_inc(terms, 1)

                def floor_norms(s):
                    if in_range(s):
                        dve.wait_ge(ss_halved, HALVINGS * (s + 1))
                        wait(dve, rn_ready, s)
                        nc.vector.tensor_scalar(ss_min[:], sq[:, :, 0], 1e-24, None, ALU.max).then_inc(ss_ready, 1)

                def layer_output(j, r):
                    if r % 2 == 0 and in_range(2 * j):
                        dve.wait_ge(w2_done, j + 1)
                        wait(dve, xpp_stored, 16 * j)
                        for n in range(2):
                            dve.wait_ge(xb_ready, 2 * j + n + 1)
                            nc.vector.tensor_tensor(xpp[:, n, :], ps[:, 3, n * D:(n + 1) * D], xb[:, (r - 6 + n) % 4, :], ALU.add).then_inc(xpp_ready, 1)

                def output_stats(j, r):
                    if r % 2 == 0 and in_range(2 * j):
                        for n in range(2):
                            dve.wait_ge(xpp_ready, 2 * j + n + 1)
                            nc.vector.bn_stats(stf[:, n, :], xpp[:, n, :]).then_inc(stf_ready, 1)
                        for n in range(2):
                            wait_apart(dve, stf_ready, 2 * j + n + 1, passed_dve)
                            nc.vector.bn_aggr(mvf[:, n, :], stf[:, n, :]).then_inc(mvf_ready, 1)
                        dve.wait_ge(mvf_ready, 2 * j + 2)
                        nc.vector.tensor_scalar(varf[:], mvf[:, :, 1], EPS, None, ALU.add).then_inc(varf_ready, 1)

                def output_norm(j, r):
                    if r % 2 == 0 and in_range(2 * j):
                        dve.wait_ge(rstdf_ready, j + 1)
                        wait(dve, fin_stored, 16 * j)
                        for n in range(2):
                            nc.vector.tensor_scalar(fin[:, n, :], xpp[:, n, :], mvf[:, n, 0:1], rstdf[:, n:n + 1],
                                                    ALU.subtract, ALU.mult).then_inc(xf_ready, 1)

                def oT_low(t):
                    if in_range(t):
                        dve.wait_ge(oT_hi, t + 1)
                        nc.vector.tensor_tensor(oT[:, 1], by_pair(ps[:, 7, :]), oT[:, 0], ALU.subtract).then_inc(oT_lo, 1)

                def run(s, r, pairs):
                    t = s - 1
                    if in_range(t):
                        par = (r - 1) % 2
                        for h in range(2):
                            rows = slice(h * DH, (h + 1) * DH)
                            at = (rows, slice(h, HEADS, 2), slice(par * P, (par + 1) * P))
                            dve.wait_ge(kT_hi, 2 * t + h + 1)
                            nc.vector.tensor_tensor(kT[at[0], 1, at[1], at[2]], by_pair(ps[rows, 6, :]), kT[at[0], 0, at[1], at[2]],
                                                    ALU.subtract).then_inc(kT_lo, 1)
                        dve.wait_ge(qT_hi, t + 1)
                        nc.vector.tensor_tensor(qT[:, 1], by_pair(ps[:, 2, :]), qT[:, 0], ALU.subtract).then_inc(qT_lo, 1)
                    layer_output(pairs - 3, r)
                    t = s - 3
                    if in_range(t):
                        dve.wait_ge(h2_loaded, 32 * (t + 1))
                        nc.vector.bn_stats(st2[:], h2[:, (r - 3) % 2, :]).then_inc(st2_ready, 1)
                        wait_apart(dve, st2_ready, t + 1, passed_dve)
                        nc.vector.bn_aggr(mv2[:], st2[:]).then_inc(mv2_ready, 1)
                        dve.wait_ge(mv2_ready, t + 1)
                        nc.vector.tensor_scalar(var2[:], mv2[:, 1:2], EPS, None, ALU.add).then_inc(var2_ready, 1)
                    rotate(s, r, 0, q_sq, q_terms, qr_ready)
                    t = s - 3
                    if in_range(t):
                        dve.wait_ge(rstd2_ready, t + 1)
                        wait(dve, xh_lo, t)
                        nc.vector.tensor_scalar(xh[:], h2[:, (r - 3) % 2, :], mv2[:, 0:1], rstd2[:], ALU.subtract, ALU.mult).then_inc(xh_ready, 1)
                        dve.wait_ge(xh_ready, t + 1)
                        wait(dve, h2T_done, t)
                        nc.vector.tensor_copy(xh_hl[:, 0, :], xh[:]).then_inc(xh_hi, 1)
                    rotate(s, r, 1, k_sq, k_terms, kr_ready)
                    oT_low(s - 2)
                    t = s - 1
                    if in_range(t):
                        dve.wait_ge(rn_ready, t + 1)
                        which = mask_now[:] if r == 1 else mask[:, EVEN_MASK if r == 3 else ODD_MASK, :]
                        if r == 1:
                            dve.wait_ge(mask_ready, t // SLOTS + 1)
                        wait(dve, pT_done, HP * t)
                        for p in range(HP):
                            if p == HP - 1:
                                floor_norms(s)
                            wait_apart(dve, scores_done, HP * t + p + 1, passed_dve)
                            for h in range(2 * p, 2 * p + 2):
                                nc.vector.tensor_tensor_reduce(probs[:, h, :], ps[:, 3 + p, (h % 2) * 2 * P:(h % 2 + 1) * 2 * P], which,
                                                               rn[:, (r - 1) % 2, h:h + 1], ABOVE_ALL, ALU.add, ALU.min,
                                                               negmax[:, h:h + 1]).then_inc(scores_kept, 1)
                    else:
                        floor_norms(s)

                    def normalise(p):
                        t = s - 1
                        if in_range(t):
                            dve.wait_ge(exp_done, HEADS * t + 2 * p + 2)
                            nc.vector.reciprocal(rinv[:, 2 * p:2 * p + 2], rowsum[:, 2 * p:2 * p + 2]).then_inc(rinv_ready, 1)
                            dve.wait_ge(rinv_ready, HP * t + p + 1)
                            for h in range(2 * p, 2 * p + 2):
                                nc.vector.tensor_scalar(probs[:, h, :], probs[:, h, :], rinv[:, h:h + 1], None, ALU.mult).then_inc(probs_ready, 1)

                    output_stats(pairs - 3, r)
                    normalise(0)
                    normalise(1)
                    t = s - 2
                    if in_range(t):
                        dve.wait_ge(wo_done, t + 1)
                        dve.wait_ge(xr_loaded, 16 * (t + 1))
                        wait(dve, xp_stored, 16 * (t - 1))
                        wait(dve, xb_ready, t - 1)
                        nc.vector.tensor_tensor(xp[:, r % 2, :], ps[:, 2, 0:D], xr[:, r % 2, :], ALU.add).then_inc(xp_ready, 1)
                    normalise(2)
                    if in_range(s + 1):
                        keep_hT(s + 1)
                    output_norm(pairs - 3, r)
                    normalise(3)
                    j = pairs - 2
                    if r % 2 == 0 and in_range(2 * j):
                        wait(dve, w2_done, j)
                        for c, bank in enumerate(W1_BANKS):
                            dve.wait_ge(gelu_done, HC * j + c + 1)
                            nc.vector.scalar_tensor_tensor(hid[:, c, :], ps[:, bank, 0:2 * P], b1a[:, ds((2 * j) // NW, 1), c], gl[:, c % 2, :],
                                                           ALU.add, ALU.mult).then_inc(hid_ready, 1)

                keep_hT(0)
                slots(dve, run)

            @block.gpsimd
            def _(pool):
                def run(s, r, pairs):
                    if r == 0 and in_range(s):
                        wait(pool, scores_kept, HEADS * (s - 3))
                        nc.gpsimd.tensor_copy(mask_now[:], mask[:, ds((s // SLOTS) % (WPB // SLOTS), 1), :]).then_inc(mask_ready, 1)
                    t = s - 3
                    if in_range(t):
                        pool.wait_ge(var2_ready, t + 1)
                        nc.gpsimd.tensor_tensor(rstd2[:], var2[:], mhalf[:, 0:1], ALU.pow).then_inc(rstd2_ready, 1)
                        pool.wait_ge(xh_hi, t + 1)
                        nc.gpsimd.tensor_tensor(xh_hl[:, 1, :], xh[:], xh_hl[:, 0, :], ALU.subtract).then_inc(xh_lo, 1)
                    if in_range(s):
                        pool.wait_ge(q_terms, 3 * (s + 1))
                        wait(pool, qT_done, s)
                        nc.gpsimd.tensor_tensor(qr[:], t1[:, 0, :], t2[:, 0, :], ALU.add).then_inc(qr_ready, 1)
                        pool.wait_ge(k_sq, s + 1)
                        for n in range(HALVINGS):
                            width = DH >> (n + 1)
                            target = sq[:, :, 0:width]
                            wait(pool, ss_halved, HALVINGS * s + n)
                            nc.gpsimd.tensor_tensor(target, target, sq[:, :, width:2 * width], ALU.add).then_inc(ss_halved, 1)
                        pool.wait_ge(k_terms, 3 * (s + 1))
                        nc.gpsimd.tensor_tensor(t1[:, 1, :], t1[:, 1, :], t2[:, 1, :], ALU.add).then_inc(kr_sum, 1)
                        pool.wait_ge(ss_ready, s + 1)
                        wait(pool, scores_kept, HEADS * (s - 1))
                        nc.gpsimd.tensor_tensor(rn[:, r % 2, :], ss_min[:], mhalf[:], ALU.pow).then_inc(rn_ready, 1)
                    j = pairs - 3
                    if r % 2 == 0 and in_range(2 * j):
                        pool.wait_ge(varf_ready, j + 1)
                        nc.gpsimd.tensor_tensor(rstdf[:], varf[:], mhalf[:, 0:2], ALU.pow).then_inc(rstdf_ready, 1)
                    if in_range(s):
                        pool.wait_ge(rn_ready, s + 1)
                        pool.wait_ge(kr_sum, s + 1)
                        wait(pool, kT_done, s)
                        nc.gpsimd.tensor_tensor(by_head(kr[:]), by_head(t1[:, 1, :]),
                                                rn[:, r % 2, HEADS:2 * HEADS].unsqueeze(2).to_broadcast([P, HEADS, DH]), ALU.mult).then_inc(kr_ready, 1)
                    t = s - 2
                    if in_range(t):
                        pool.wait_ge(xp_ready, t + 1)
                        wait(pool, xpp_ready, t - 3)
                        nc.gpsimd.tensor_tensor(xb[:, (r - 2) % 4, :], xp[:, r % 2, :], b2[:, ds(t // NW, 1), :], ALU.add).then_inc(xb_ready, 1)
                    j = pairs - 3
                    if r % 2 == 0 and in_range(2 * j):
                        pool.wait_ge(xf_ready, 2 * j + 2)
                        pool.wait_ge(x2_loaded, 16 * (j + 1))
                        nc.gpsimd.tensor_tensor(fin[:], fin[:], x2[:], ALU.add).then_inc(fin_ready, 1)

                nc.gpsimd.memset(v[:], 0.0).then_inc(vk_cleared, 1)
                nc.gpsimd.memset(kT[:].bitcast(F32), 0.0).then_inc(vk_cleared, 1)
                slots(pool, run)


def build(nc, x, wqkv, q_scale, k_scale, wo, ln_g, ln_b, w1, b1, w2, b2, ident, rot, mask, out):
    x2_dram = nc.dram_tensor("x2_dram", [NW * P, D], F32).ap()
    xs_dram = nc.dram_tensor("xs_dram", [XS_BLOCKS * P, D], F32).ap()
    xp_dram = nc.dram_tensor("xp_dram", [XP_BLOCKS * P, D], F32).ap()
    rot_dram = nc.dram_tensor("rot_dram", [LAYERS * S, 4, DH], F32).ap()
    phase_a(nc, x, ident, x2_dram, xs_dram, xp_dram)
    weights = dict(wqkv=wqkv, q_scale=q_scale, k_scale=k_scale, wo=wo, ln_g=ln_g, ln_b=ln_b, w1=w1, b1=b1, w2=w2, b2=b2)
    phase_b(nc, weights, dict(ident=ident, rot=rot, mask=mask), x2_dram, xs_dram, xp_dram, rot_dram, out)


def rotary_tables():
    f = np.float32
    half = np.arange(0, DH, 2, dtype=f)
    inv_freq = f(1) / np.power(10000.0, (half / f(DH)).astype(np.float64)).astype(f)
    t = np.arange(S, dtype=f)
    freqs = t[:, None] * inv_freq[None, :]
    base = (half + f(0.4 * DH)) / f(1.4 * DH)
    power = (t - f(S // 2)) / f(P // 2)
    scale = np.power(base[None, :].astype(np.float64), power[:, None].astype(np.float64))
    cos, sin = np.cos(freqs.astype(np.float64)), np.sin(freqs.astype(np.float64))
    both = lambda lo, hi: np.concatenate([lo, hi], axis=1)
    tables = [both(cos, cos) * both(scale, scale) * -QK_SCALE, both(-sin, sin) * both(scale, scale) * -QK_SCALE,
              both(cos, cos) / both(scale, scale), both(-sin, sin) / both(scale, scale)]
    return np.stack(tables).astype(f)


def window_masks():
    i, j = np.arange(P)[:, None], np.arange(P)[None, :]
    own, before = np.where(j <= i, 0.0, MASKED), np.where(j >= i, 0.0, MASKED)
    none = np.full((P, P), MASKED)
    kinds = [(own, none)] + (WPB // SLOTS - 1) * [(own, before)] + [(before, own)]
    return np.stack([np.concatenate(kind, axis=1) for kind in kinds]).astype(np.float32)


_INS = ["L0_attn_x", "L0_ffn_wqkv", "L0_ffn_q_scale", "L0_ffn_k_scale", "L0_ffn_wo", "L0_ffn_ln_g", "L0_ffn_ln_b", "L0_ffn_w1", "L0_ffn_b1",
        "L0_ffn_w2", "L0_ffn_b2"]


def kernel(**inputs):
    import concourse.bacc as bacc
    from concourse.bass_utils import run_bass_kernel_spmd

    nc = bacc.Bacc("TRN2", target_bir_lowering=False, num_devices=1)
    arrays = {f"in_{name}_dram": np.ascontiguousarray(inputs[name]) for name in _INS}
    arrays["in_ident_dram"] = np.eye(P, dtype=np.float32)
    arrays["in_rot_dram"] = rotary_tables()
    arrays["in_mask_dram"] = window_masks()
    args = [nc.dram_tensor(name, a.shape, mybir.dt.from_np(a.dtype), kind="ExternalInput").ap() for name, a in arrays.items()]
    out = nc.dram_tensor("out_0_dram", (B, S, D), F32, kind="ExternalOutput").ap()
    build(nc, *args, out)
    r = run_bass_kernel_spmd(nc, [arrays], core_ids=[0])
    return r.results[0]["out_0_dram"]
```

```python
from contextlib import ExitStack

import numpy as np

import concourse.bass as bass
import concourse.mybir as mybir

F32, F32R = mybir.dt.float32, mybir.dt.float32r
F16, BF16, I32 = mybir.dt.float16, mybir.dt.bfloat16, mybir.dt.int32
ALU = mybir.AluOpType
ACT = mybir.ActivationFunctionType
AX = mybir.AxisListType
RED_MAX = bass.bass_isa.ReduceOp.max
ds = bass.ds

P = 128
B, S, D = 4, 2048, 256
KD = D // P
WPB = S // P
NW = B * WPB
LAYERS, HEADS, DH = 2, 8, 64
INNER = HEADS * DH
HP = HEADS // 2
HID = int(D * 4 * 2 / 3)
FULL = HID // P
REST = HID - FULL * P
HC = FULL + 1
W1_BLOCKS = 2 * FULL + 1
SECOND_REST = P // 2
assert 0 < REST <= P // 2
EPS = 1e-5
QK_SCALE = 8.0
MASKED, ABOVE_ALL = 1e30, 3e38
EVEN_MASK, ODD_MASK = 3, 4
H2T_AT = 1
XS_SCALE = 2.0 ** 9
W1_TOP = 2.0 ** 13
NT = LAYERS * NW
BLOCKS_PER_BATCH = WPB + 1
STREAM_BLOCKS = NT + NT // WPB
SLOTS = 4
LAST_SLOT = NT + 6
FILL_GROUPS = 2
PARTS = ((0, 0), (0, 1), (1, 0))
HALVINGS = DH.bit_length() - 1
W1_BANKS = (0, 1, 6, 3, 4, 5)


def wait(eng, sem, count):
    if not (isinstance(count, int) and count <= 0):
        eng.wait_ge(sem, count)


def wait_apart(eng, sem, count, passed):
    if not (isinstance(count, int) and count <= 0):
        eng.wait_ge(sem, count)
        eng.sem_inc(passed, 1)


def stream_block(t):
    return t + t // WPB + 1


def phase_a(nc, x_in, ident_in, x2_dram, xs_dram, xp_dram):
    x_v = x_in.rearrange("b (w p) d -> p (b w) d", p=P)
    x2_v = x2_dram.rearrange("(w p) d -> p w d", p=P)
    xs_v = xs_dram.rearrange("(w p) d -> p w d", p=P)
    chunks = S // 512
    e_full_start = 4
    loads = 4
    x_loaded_start = 16
    ctx_free_start = 4
    e_lo_start = 1
    xs_lo_start = 1
    xs_full_start = 2
    with ExitStack() as ctx:
        def sb(name, shape, dt=F32):
            return ctx.enter_context(nc.sbuf_tensor("a_" + name, shape, dt))

        def sem(name):
            return ctx.enter_context(nc.semaphore("a_" + name))

        ident_f = sb("ident_f", [P, P])
        ident = sb("ident", [P, P], F16)
        xn = sb("xn", [P, WPB, D])
        xn_hl = sb("xn_hl", [P, 2, 2, D], F16)
        xnT = sb("xnT", [P, 2, KD, S], F16)
        E = sb("E", [P, 2, WPB, S], F16)
        e32 = sb("e32", [P, S])
        xs32 = sb("xs32", [P, D])
        xs = sb("xs", [P, 2, WPB, D], F16)
        st_first, mv_first = sb("st_first", [P, WPB, 6]), sb("mv_first", [P, WPB, 2])
        var_first, rstd_first = sb("var_first", [P, WPB]), sb("rstd_first", [P, WPB])
        negmax_part, negmax = sb("negmax_part", [P, 2, 2]), sb("negmax", [P, 2])
        colsum = sb("colsum", [P, 2, 2])
        colsum_s = sb("colsum_s", [P, 2])
        inv_sum = sb("inv_sum", [P, 2])
        st_n, mv_n, var_n, rstd_n = sb("st_n", [P, 6]), sb("mv_n", [P, 2]), sb("var_n", [P, 1]), sb("rstd_n", [P, 1])
        st_c, mv_c, var_c = sb("st_c", [P, 6]), sb("mv_c", [P, 2]), sb("var_c", [P, 1])
        pow_c, rstd_c = sb("pow_c", [P, 1]), sb("rstd_c", [P, 1])
        st_x, mv_x, var_x, rstd_x = sb("st_x", [P, 6]), sb("mv_x", [P, 2]), sb("var_x", [P, 1]), sb("rstd_x", [P, 1])
        mhalf = sb("mhalf", [P, WPB])
        unscale = sb("unscale", [P, 1])
        x_res = sb("x_res", [P, 2, D])
        ln_c = sb("ln_c", [P, D])
        x2 = sb("x2", [P, 2, D])
        xo = sb("xo", [P, 2, D])
        zeros = sb("zeros", [LAYERS * B, D])
        ps = ctx.enter_context(nc.psum_tensor("a_ps", [P, 8, 512], F32))
        ps_tr = [ps[:, 4 + i, 0:256].bitcast(F16).rearrange("p (h k n) -> p h k n", h=2, k=KD) for i in range(2)]

        consts_in, consts, pool_consts, x_loaded = sem("consts_in"), sem("consts"), sem("pool_consts"), sem("x_loaded")
        x_first = [sem(f"x_first{q}") for q in range(loads)]
        st_first_done, mv_first_done, var_first_ready, rstd_first_ready = (sem(n) for n in (
            "st_first_done", "mv_first_done", "var_first_ready", "rstd_first_ready"))
        stn, mvn, varn_ready, rstdn_ready, xn_ready, xn_hi, xn_lo = (sem(n) for n in (
            "stn", "mvn", "varn_ready", "rstdn_ready", "xn_ready", "xn_hi", "xn_lo"))
        trans_done, xnT_ready = sem("trans_done"), sem("xnT_ready")
        scores_done, part_max, max_ready, e_hi, e_full, e_lo = (sem(n) for n in (
            "scores_done", "part_max", "max_ready", "e_hi", "e_full", "e_lo"))
        sum_scaled, inv_ready, xs_full, xs_hi, xs_lo = (sem(n) for n in (
            "sum_scaled", "inv_ready", "xs_full", "xs_hi", "xs_lo"))
        ctx_done, stc, mvc, varc_ready, powc, rstdc_ready, ctx_free = (sem(n) for n in (
            "ctx_done", "stc", "mvc", "varc_ready", "powc", "rstdc_ready", "ctx_free"))
        x2_ready, stx, mvx, varx_ready, rstdx_ready, xo_ready = (sem(n) for n in (
            "x2_ready", "stx", "mvx", "varx_ready", "rstdx_ready", "xo_ready"))
        res_in = [sem(f"res_in{i}") for i in range(2)]
        x2_out = [sem(f"x2_out{i}") for i in range(2)]
        xo_out = [sem(f"xo_out{i}") for i in range(2)]
        zero_rows = sem("zero_rows")
        passed_dve, passed_pe = sem("passed_dve"), sem("passed_pe")
        block = ctx.enter_context(nc.Block())

        @block.sync
        def _(sp):
            sp.dma_start(ident_f[:], ident_in).then_inc(consts_in, 16)
            for q in range(loads):
                part = slice(q * WPB // loads, (q + 1) * WPB // loads)
                sp.dma_start(xn[:, part, :], x_v[:, part, :]).then_inc(x_first[q], 16)
            for u in range(2):
                sp.sem_inc(x2_out[u], 16)
                sp.sem_inc(xo_out[u], 16)
            sp.sem_inc(e_full, e_full_start)
            sp.sem_inc(x_loaded, x_loaded_start)
            sp.sem_inc(ctx_free, ctx_free_start)
            sp.sem_inc(e_lo, e_lo_start)
            sp.sem_inc(xs_lo, xs_lo_start)
            sp.sem_inc(xs_full, xs_full_start)
            sp.wait_ge(pool_consts, 1)
            rows = BLOCKS_PER_BATCH * P
            sp.dma_start(xs_dram.rearrange("(q r) d -> q r d", r=rows)[:, P - 1, :], zeros[:]).then_inc(zero_rows, 16)
            sp.dma_start(xp_dram.rearrange("(q r) d -> q r d", r=rows)[:, P - 1, :], zeros[:]).then_inc(zero_rows, 16)
            for u in range(2):
                sp.dma_start(x_res[:, u, :], x_v[:, u, :]).then_inc(res_in[u], 16)
            with sp.Fori(0, B) as b:
                with sp.Fori(0, loads) as q:
                    sp.wait_ge(x_loaded, x_loaded_start + 16 * (b * loads + q))
                    sp.wait_ge(xs_full, xs_full_start + b * WPB + (q + 1) * (WPB // loads))
                    sp.dma_start(xn[:, ds(q * (WPB // loads), WPB // loads), :],
                                 x_v[:, ds(((b + 1) % B) * WPB + q * (WPB // loads), WPB // loads), :]).then_inc(x_loaded, 16)
                with sp.Fori(0, WPB // 2) as h:
                    for u in range(2):
                        g = b * WPB + 2 * h + u
                        sp.wait_ge(xo_ready, g + 1)
                        sp.dma_start(x2_v[:, ds(g, 1), :], x2[:, u, :]).then_inc(x2_out[u], 16)
                        sp.dma_start(xs_v[:, ds(stream_block(g), 1), :], xo[:, u, :]).then_inc(xo_out[u], 16)
                        sp.dma_start(x_res[:, u, :], x_v[:, ds((g + 2) % NW, 1), :]).then_inc(res_in[u], 16)
            for u in range(2):
                sp.wait_ge(x2_out[u], 16 * (NW // 2 + 1))
                sp.wait_ge(xo_out[u], 16 * (NW // 2 + 1))
                sp.wait_ge(res_in[u], 16 * (NW // 2 + 1))
            sp.wait_ge(zero_rows, 32)
            sp.wait_ge(x_loaded, x_loaded_start + 16 * B * loads)

        @block.gpsimd
        def _(pool):
            nc.gpsimd.memset(mhalf[:], -0.5)
            nc.gpsimd.memset(unscale[:], 1.0 / XS_SCALE)
            nc.gpsimd.memset(zeros[:], 0.0).then_inc(pool_consts, 1)
            pool.wait_ge(pool_consts, 1)

            def norm(g):
                pool.wait_ge(varn_ready, g + 1)
                nc.gpsimd.tensor_tensor(rstd_n[:], var_n[:], mhalf[:, 0:1], ALU.pow).then_inc(rstdn_ready, 1)

            def low_part(n, u):
                pool.wait_ge(xn_hi, n + 1)
                nc.gpsimd.tensor_tensor(xn_hl[:, u, 1, :], xn[:, ds(n % WPB, 1), :], xn_hl[:, u, 0, :], ALU.subtract).then_inc(xn_lo, 1)

            pool.wait_ge(var_first_ready, 1)
            nc.gpsimd.tensor_tensor(rstd_first[:], var_first[:], mhalf[:], ALU.pow).then_inc(rstd_first_ready, 1)
            with pool.Fori(0, WPB // 2) as h:
                for u in range(2):
                    low_part(2 * h + u, u)
            with pool.Fori(0, B) as b:
                with pool.Fori(0, WPB // 2) as h:
                    for u in range(2):
                        j = 2 * h + u
                        g = b * WPB + j
                        pool.wait_ge(inv_ready, g + 1)
                        pool.wait_ge(xs_lo, xs_lo_start + g)
                        nc.gpsimd.tensor_tensor(xs32[:], xn[:, ds(j, 1), :], inv_sum[:, u:u + 1].to_broadcast([P, D]), ALU.mult).then_inc(xs_full, 1)
                        pool.wait_ge(xs_full, xs_full_start + g + 1)
                        nc.gpsimd.tensor_copy(xs[:, 0, ds(j, 1), :], xs32[:]).then_inc(xs_hi, 1)
                        pool.wait_ge(xs_hi, g + 1)
                        nc.gpsimd.tensor_tensor(xs[:, 1, ds(j, 1), :], xs32[:], xs[:, 0, ds(j, 1), :], ALU.subtract).then_inc(xs_lo, 1)

                def norms(i, u, more):
                    g = b * WPB + i
                    pool.wait_ge(varc_ready, g + 1)
                    nc.gpsimd.tensor_tensor(pow_c[:], var_c[:], mhalf[:, 0:1], ALU.pow).then_inc(powc, 1)
                    pool.wait_ge(powc, g + 1)
                    nc.gpsimd.tensor_tensor(rstd_c[:], pow_c[:], unscale[:], ALU.mult).then_inc(rstdc_ready, 1)
                    if more:
                        norm(g + 1)
                    pool.wait_ge(varx_ready, g + 1)
                    nc.gpsimd.tensor_tensor(rstd_x[:], var_x[:], mhalf[:, 0:1], ALU.pow).then_inc(rstdx_ready, 1)
                    if more:
                        low_part(g + 1 + WPB, 1 - u)

                norm(b * WPB)
                low_part((b + 1) * WPB, 0)
                with pool.Fori(0, WPB // 2 - 1) as h:
                    for u in range(2):
                        norms(2 * h + u, u, True)
                for i in range(WPB - 2, WPB):
                    norms(i, i % 2, i < WPB - 1)

        @block.vector
        def _(dve):
            dve.wait_ge(consts_in, 16)
            nc.vector.tensor_copy(ident[:], ident_f[:]).then_inc(consts, 1)

            def prep_stats(g):
                tile = xn[:, ds(g % WPB, 1), :]
                nc.vector.bn_stats(st_n[:], tile).then_inc(stn, 1)
                wait_apart(dve, stn, g + 1, passed_dve)
                nc.vector.bn_aggr(mv_n[:], st_n[:]).then_inc(mvn, 1)
                dve.wait_ge(mvn, g + 1)
                nc.vector.tensor_scalar(var_n[:], mv_n[:, 1:2], EPS, None, ALU.add).then_inc(varn_ready, 1)

            def normalise(n, u, mean, rstd):
                tile = xn[:, ds(n % WPB, 1), :]
                nc.vector.tensor_scalar(tile, tile, mean, rstd, ALU.subtract, ALU.mult).then_inc(xn_ready, 1)
                dve.wait_ge(xn_ready, n + 1)
                wait(dve, trans_done, n - 1)
                nc.vector.tensor_scalar(xn_hl[:, u, 0, :], tile, 1.0, None, ALU.mult).then_inc(xn_hi, 1)

            for n in range(WPB):
                dve.wait_ge(x_first[n * loads // WPB], 16)
                nc.vector.bn_stats(st_first[:, n, :], xn[:, n, :]).then_inc(st_first_done, 1)
            for n in range(WPB):
                dve.wait_ge(st_first_done, n + 1)
                nc.vector.bn_aggr(mv_first[:, n, :], st_first[:, n, :]).then_inc(mv_first_done, 1)
            dve.wait_ge(mv_first_done, WPB)
            nc.vector.tensor_scalar(var_first[:], mv_first[:, :, 1], EPS, None, ALU.add).then_inc(var_first_ready, 1)
            dve.wait_ge(rstd_first_ready, 1)
            for n in range(WPB):
                normalise(n, n % 2, mv_first[:, n, 0:1], rstd_first[:, n:n + 1])

            with dve.Fori(0, B) as b:
                def row_max(j):
                    g = b * WPB + j
                    u = j % 2
                    for part in range(2):
                        dve.wait_ge(scores_done, 2 * g + part + 1)
                        banks = ds(chunks * u + part * (chunks - 1), 1 if part else chunks - 1)
                        nc.vector.tensor_reduce(negmax_part[:, ds(u, 1), part], ps[:, banks, :].rearrange("p c n -> p (c n)"),
                                                AX.X, ALU.max, negate=True).then_inc(part_max, 1)
                    dve.wait_ge(part_max, 2 * g + 2)
                    nc.vector.tensor_tensor(negmax[:, ds(u, 1)], negmax_part[:, ds(u, 1), 0], negmax_part[:, ds(u, 1), 1], ALU.min).then_inc(max_ready, 1)

                def low_part(j):
                    g = b * WPB + j
                    u = j % 2
                    dve.wait_ge(e_full, e_full_start + 2 * g + 2)
                    nc.vector.tensor_scalar(colsum_s[:, ds(u, 1)], colsum[:, ds(u, 1), 0], colsum[:, ds(u, 1), 1], 1.0 / XS_SCALE,
                                            ALU.add, ALU.mult).then_inc(sum_scaled, 1)
                    nc.vector.tensor_tensor(E[:, 1, ds(j, 1), :], e32[:], E[:, 0, ds(j, 1), :], ALU.subtract).then_inc(e_lo, 1)
                    dve.wait_ge(sum_scaled, g + 1)
                    dve.wait_ge(xs_full, xs_full_start + g - 1)
                    nc.vector.reciprocal(inv_sum[:, ds(u, 1)], colsum_s[:, ds(u, 1)]).then_inc(inv_ready, 1)

                row_max(0)
                with dve.Fori(1, WPB) as j:
                    row_max(j)
                    low_part(j - 1)
                low_part(WPB - 1)
                def next_stats(i):
                    g = b * WPB + i
                    if isinstance(i, int) and i % (WPB // loads) == 0:
                        wait_apart(dve, x_loaded, x_loaded_start + 16 * (b * loads + i // (WPB // loads) + 1), passed_dve)
                    prep_stats(g)

                def next_norm(i, u):
                    g = b * WPB + i
                    dve.wait_ge(rstdn_ready, g + 1)
                    normalise(g + WPB, u, mv_n[:, 0:1], rstd_n[:])

                def finish(i, bank, more):
                    g = b * WPB + i
                    u = bank % 2
                    context = ps[:, bank, 0:D]
                    dve.wait_ge(ctx_done, g + 1)
                    nc.vector.bn_stats(st_c[:], context).then_inc(stc, 1)
                    wait_apart(dve, stc, g + 1, passed_dve)
                    nc.vector.bn_aggr(mv_c[:], st_c[:]).then_inc(mvc, 1)
                    dve.wait_ge(mvc, g + 1)
                    nc.vector.tensor_scalar(var_c[:], mv_c[:, 1:2], XS_SCALE ** -2, EPS, ALU.mult, ALU.add).then_inc(varc_ready, 1)
                    if more:
                        next_stats(i + 1)
                    dve.wait_ge(rstdc_ready, g + 1)
                    nc.vector.tensor_scalar(ln_c[:], context, mv_c[:, 0:1], rstd_c[:], ALU.subtract, ALU.mult).then_inc(ctx_free, 1)
                    dve.wait_ge(ctx_free, ctx_free_start + g + 1)
                    dve.wait_ge(res_in[u], 16 * (g // 2) + 16)
                    dve.wait_ge(x2_out[u], 16 * (g // 2) + 16)
                    nc.vector.tensor_tensor(x2[:, u, :], ln_c[:], x_res[:, u, :], ALU.add).then_inc(x2_ready, 1)
                    dve.wait_ge(x2_ready, g + 1)
                    nc.vector.bn_stats(st_x[:], x2[:, u, :]).then_inc(stx, 1)
                    wait_apart(dve, stx, g + 1, passed_dve)
                    nc.vector.bn_aggr(mv_x[:], st_x[:]).then_inc(mvx, 1)
                    dve.wait_ge(mvx, g + 1)
                    nc.vector.tensor_scalar(var_x[:], mv_x[:, 1:2], EPS, None, ALU.add).then_inc(varx_ready, 1)
                    if more:
                        next_norm(i + 1, 1 - u)
                    dve.wait_ge(rstdx_ready, g + 1)
                    dve.wait_ge(xo_out[u], 16 * (g // 2) + 16)
                    nc.vector.tensor_scalar(xo[:, u, :], x2[:, u, :], mv_x[:, 0:1], rstd_x[:], ALU.subtract, ALU.mult).then_inc(xo_ready, 1)

                next_stats(0)
                next_norm(0, 0)
                with dve.Fori(0, WPB // 4 - 1) as h:
                    for u4 in range(4):
                        if u4 == 3:
                            wait_apart(dve, x_loaded, x_loaded_start + 16 * (b * loads + h + 2), passed_dve)
                        finish(4 * h + u4, u4, True)
                for i in range(WPB - 4, WPB):
                    finish(i, i % 4, i < WPB - 1)

        @block.scalar
        def _(act):
            def keep_transposed(n, u):
                act.wait_ge(trans_done, n + 1)
                nc.scalar.copy(xnT[:, :, :, ds((n % WPB) * P, P)], ps_tr[u]).then_inc(xnT_ready, 1)

            with act.Fori(0, WPB // 2) as h:
                for u in range(2):
                    keep_transposed(2 * h + u, u)
            with act.Fori(0, B) as b:
                with act.Fori(0, WPB // 2) as h:
                    for u in range(2):
                        j = 2 * h + u
                        g = b * WPB + j
                        scores = ps[:, 4 * u:4 * u + chunks, :].rearrange("p c n -> p (c n)")
                        act.wait_ge(max_ready, g + 1)
                        nc.scalar.activation(E[:, 0, ds(j, 1), :], scores, ACT.Exp, bias=negmax[:, u:u + 1]).then_inc(e_hi, 1)
                        act.wait_ge(e_lo, e_lo_start + g)
                        for half in range(2):
                            columns = slice(half * S // 2, (half + 1) * S // 2)
                            nc.scalar.activation(e32[:, columns], scores[:, columns], ACT.Exp, bias=negmax[:, u:u + 1],
                                                 accum_out=colsum[:, u, half:half + 1]).then_inc(e_full, 1)
                with act.Fori(0, WPB // 2) as h:
                    for u in range(2):
                        keep_transposed((b + 1) * WPB + 2 * h + u, u)

        @block.tensor
        def _(pe):
            def transposes(n, u):
                pe.wait_ge(xn_lo, n + 1)
                wait(pe, xnT_ready, n - 1)
                for part in range(2):
                    for k in range(KD):
                        last = nc.tensor.transpose(ps_tr[u][:, part, k, :], xn_hl[:, u, part, k * P:(k + 1) * P], ident[:])
                last.then_inc(trans_done, 1)

            pe.wait_ge(consts, 1)
            for n in range(2):
                transposes(n, n)
            with pe.Fori(1, WPB // 2) as h:
                for u in range(2):
                    transposes(2 * h + u, u)

            with pe.Fori(0, B) as b:
                with pe.Fori(0, WPB // 2) as h:
                    for u in range(2):
                        g = b * WPB + 2 * h + u
                        rows = ds((2 * h + u) * P, P)
                        for n in range(chunks):
                            pe.wait_ge(xnT_ready, b * WPB + (n + 1) * WPB // chunks)
                            wait_apart(pe, ctx_free, b * WPB + n + 1, passed_pe)
                            pe.wait_ge(e_full, 2 * g + n // 2 + 1)
                            for k in range(KD):
                                for a, c in ((0, 0), (0, 1), (1, 0)):
                                    last = nc.tensor.matmul(ps[:, 4 * u + n, :], xnT[:, a, k, rows], xnT[:, c, k, n * 512:(n + 1) * 512],
                                                            start=(k == 0 and a == 0 and c == 0), stop=(k == KD - 1 and a == 1))
                            if n >= chunks - 2:
                                last.then_inc(scores_done, 1)

                def products(i, bank, j):
                    for a, c in ((0, 0), (0, 1), (1, 0)):
                        last = nc.tensor.matmul(ps[:, bank, 0:D], E[:, a, j, ds(i * P, P)], xs[:, c, j, :],
                                                start=(j == 0 and a == 0 and c == 0), stop=(j == WPB - 1 and a == 1))
                    if j == WPB - 1:
                        last.then_inc(ctx_done, 1)

                def context(i, bank):
                    pe.wait_ge(ctx_free, b * WPB + i + 1)
                    for j in range(WPB):
                        products(i, bank, j)

                after = (b + 1) * WPB
                wait_apart(pe, ctx_free, ctx_free_start + b * WPB, passed_pe)
                pe.wait_ge(e_full, e_full_start + 2 * (b * WPB + WPB - 1))
                for last_rows in (False, True):
                    for j in (range(WPB - 2, WPB) if last_rows else range(WPB - 2)):
                        rows_made = WPB - 2 if j == 0 else j + 1
                        if rows_made > j + 1 or last_rows:
                            wait_apart(pe, e_lo, e_lo_start + b * WPB + rows_made, passed_pe)
                            wait_apart(pe, xs_lo, xs_lo_start + b * WPB + rows_made, passed_pe)
                        for i in range(2):
                            products(i, i, j)
                transposes(after, 0)
                with pe.Fori(0, WPB // 4 - 1) as h:
                    for u4 in range(4):
                        context(4 * h + u4 + 2, (u4 + 2) % 4)
                        transposes(after + 4 * h + u4 + 1, (u4 + 1) % 2)
                for i in range(WPB - 2, WPB):
                    context(i, i % 4)
                    transposes(after + i - 1, (i - 1) % 2)
                transposes(after + WPB - 1, (WPB - 1) % 2)


def in_range(t):
    return not isinstance(t, int) or 0 <= t < NT


def slots(eng, run):
    per_layer = NW // SLOTS
    done = 0
    for l in range(LAYERS):
        first = l * per_layer + FILL_GROUPS
        end = min((l + 1) * per_layer, NT // SLOTS - 1)
        for s in range(done, first * SLOTS):
            run(s, s % SLOTS, s // 2, lambda t: t // NW)
        with eng.Fori(first, end) as i:
            for r in range(SLOTS):
                run(SLOTS * i + r, r, SLOTS // 2 * i + r // 2, lambda t: l)
        done = end * SLOTS
    for s in range(done, LAST_SLOT + 1):
        run(s, s % SLOTS, s // 2, lambda t: t // NW)


def phase_b(nc, w, consts, x2_dram, xs_dram, xp_dram, rot_dram, out):
    x2_v = x2_dram.rearrange("(w p) d -> p w d", p=P)
    out_v = out.rearrange("b (w p) d -> p (b w) d", p=P)
    xs_v = xs_dram.rearrange("(w p) d -> p w d", p=P)
    xp_v = xp_dram.rearrange("(w p) d -> p w d", p=P)
    rot_v = rot_dram.rearrange("(w p) n d -> p w (n d)", p=P)
    xs_prev = xs_dram[P - 1:-1, :].rearrange("(w p) d -> p w d", p=P)
    xp_prev = xp_dram[P - 1:-1, :].rearrange("(w p) d -> p w d", p=P)
    HALF = D // 2
    with ExitStack() as keep:
        def sb(name, shape, dt=F32):
            return keep.enter_context(nc.sbuf_tensor("b_" + name, shape, dt))

        wqkv = sb("wqkv", [P, LAYERS, 2, KD, 3 * INNER], F32R)
        w1 = sb("w1", [P, LAYERS, 2, KD, W1_BLOCKS * P], F16)
        w1_unit = sb("w1_unit", [P, LAYERS])
        b1 = sb("b1", [P, LAYERS, W1_BLOCKS])
        b1a = sb("b1a", [P, LAYERS, HC])
        w2 = sb("w2", [P, LAYERS, HC, D])
        b2 = sb("b2", [P, LAYERS, D])
        wo = sb("wo", [P, LAYERS, 2, HP, D], F32R)
        mask = sb("mask", [P, 5, 2 * P], BF16)
        ident_f, ident_h = sb("ident_f", [P, P]), sb("ident_h", [P, P], F16)
        mhalf = sb("mhalf", [P, 2 * HEADS])
        ps = keep.enter_context(nc.psum_tensor("b_ps", [P, 8, 512], F32))

        with ExitStack() as ctx:
            def sb(name, shape, dt=F32):
                return ctx.enter_context(nc.sbuf_tensor("p_" + name, shape, dt))

            def sem(name):
                return ctx.enter_context(nc.semaphore("p_" + name))

            wqkv_f = sb("wqkv_f", [P, LAYERS, KD, 3 * INNER])
            w1_f = sb("w1_f", [P, LAYERS, KD, W1_BLOCKS * P])
            b1_f = sb("b1_f", [P, LAYERS, W1_BLOCKS])
            lg, lb = sb("lg", [P, LAYERS, KD]), sb("lb", [P, LAYERS, KD])
            rot_all = sb("rot_all", [P, 4, LAYERS * WPB, DH])
            mask_f = sb("mask_f", [P, 5, 2 * P])
            wo_f = sb("wo_f", [P, LAYERS, HP, D])
            head_scale = sb("head_scale", [P, 2, 2, LAYERS, DH])
            top, top_all, top_min = sb("top", [P, LAYERS]), sb("top_all", [P, LAYERS]), sb("top_min", [P, LAYERS])
            pow2, pow2_inv, w1_scale = sb("pow2", [P, LAYERS]), sb("pow2_inv", [P, LAYERS]), sb("w1_scale", [P, LAYERS])
            cleared, loaded_ln, loaded_qkv, loaded_rot, loaded_wo, loaded = (sem(n) for n in (
                "cleared", "loaded_ln", "loaded_qkv", "loaded_rot", "loaded_wo", "loaded"))
            loaded_w1 = [sem(f"loaded_w1_{l}") for l in range(LAYERS)]
            wo_hi, rot_scaled, rot_stored = sem("wo_hi"), sem("rot_scaled"), sem("rot_stored")
            qkv_hi, bias_done, w1_gained, top_ready, top_shared = (sem(n) for n in ("qkv_hi", "bias_done", "w1_gained", "top_ready", "top_shared"))
            step, scale_ready, w1_hi, bias_added = sem("step"), sem("scale_ready"), sem("w1_hi"), sem("bias_added")
            block = ctx.enter_context(nc.Block())
            DMAS_ROT, DMAS = 4 + 6, LAYERS * 5 + 4

            @block.sync
            def _(sp):
                sp.dma_start(lb[:], w["ln_b"].rearrange("l (k p) -> p l k", p=P), allow_slow_non_contiguous=True).then_inc(loaded_ln, 16)
                sp.dma_start(lg[:], w["ln_g"].rearrange("l (k p) -> p l k", p=P), allow_slow_non_contiguous=True).then_inc(loaded_ln, 16)
                sp.wait_ge(cleared, 1)
                for l in range(LAYERS):
                    w1_rows = w["w1"][l].rearrange("(k p) n -> p k n", p=P)
                    sp.dma_start(w1_f[:, l, :, 0:HID], w1_rows[:, :, 0:HID]).then_inc(loaded_w1[l], 16)
                    sp.dma_start(w1_f[:, l, :, HC * P:W1_BLOCKS * P], w1_rows[:, :, HID:HID + FULL * P]).then_inc(loaded_w1[l], 16)
                    sp.dma_start(w1_f[:, l, :, FULL * P + SECOND_REST:FULL * P + SECOND_REST + REST],
                                 w1_rows[:, :, HID + FULL * P:2 * HID]).then_inc(loaded_w1[l], 16)
                for n in range(4):
                    sp.dma_start(rot_all[:, n, (LAYERS - 1) * WPB:LAYERS * WPB, :], consts["rot"][n].rearrange("(w p) d -> p w d", p=P)).then_inc(loaded_rot, 16)
                for n, name in enumerate(("q_scale", "k_scale")):
                    half = DH // 2
                    sp.dma_start(head_scale[:, n, 0], w[name].partition_broadcast(P)).then_inc(loaded_rot, 16)
                    sp.dma_start(head_scale[:, n, 1, :, 0:half], w[name][:, half:DH].partition_broadcast(P)).then_inc(loaded_rot, 16)
                    sp.dma_start(head_scale[:, n, 1, :, half:DH], w[name][:, 0:half].partition_broadcast(P)).then_inc(loaded_rot, 16)
                sp.dma_start(wqkv_f[:].rearrange("p l k n -> p (l k) n"), w["wqkv"].rearrange("l (k p) n -> p (l k) n", p=P)).then_inc(loaded_qkv, 16)
                sp.dma_start(wo_f[:].rearrange("p l h d -> p (l h) d"), w["wo"].rearrange("l (h p) d -> p (l h) d", p=P)).then_inc(loaded_wo, 16)
                sp.dma_start(ident_f[:], consts["ident"]).then_inc(loaded, 16)
                sp.dma_start(mask_f[:], consts["mask"].rearrange("n p j -> p n j")).then_inc(loaded, 16)
                sp.dma_start(b2[:], w["b2"].partition_broadcast(P)).then_inc(loaded, 16)
                sp.wait_ge(cleared, 3)
                for l in range(LAYERS):
                    sp.dma_start(w2[:, l, 0:FULL, :], w["w2"][l, 0:FULL * P, :].rearrange("(c p) d -> p c d", p=P)).then_inc(loaded, 16)
                    for first_block, first_row, half in ((0, 0, 0), (HC, SECOND_REST, HID)):
                        sp.dma_start(b1_f[:, l, first_block:first_block + FULL], w["b1"][l, half:half + FULL * P].rearrange("(c p) -> p c", p=P),
                                     allow_slow_non_contiguous=True).then_inc(loaded, 16)
                        sp.dma_start(b1_f[first_row:first_row + REST, l, FULL:HC], w["b1"][l, half + FULL * P:half + HID].rearrange("(p c) -> p c", c=1),
                                     allow_slow_non_contiguous=True).then_inc(loaded, 16)
                sp.dma_start(w2[0:REST, :, FULL, :], w["w2"][:, FULL * P:HID, :].rearrange("l p d -> p l d")).then_inc(loaded, 16)
                for n in range(4):
                    sp.wait_ge(rot_scaled, LAYERS * (n + 1))
                    sp.dma_start(rot_dram.rearrange("(w p) n d -> p n w d", p=P)[:, n], rot_all[:, n]).then_inc(rot_stored, 16)
                sp.wait_ge(rot_stored, 64)

            @block.gpsimd
            def _(pool):
                nc.gpsimd.memset(w1_f[:, :, :, FULL * P:HC * P], 0.0).then_inc(cleared, 1)
                nc.gpsimd.memset(b1_f[:, :, FULL:HC], 0.0).then_inc(cleared, 1)
                nc.gpsimd.memset(w2[:, :, FULL, :], 0.0).then_inc(cleared, 1)
                nc.gpsimd.memset(mhalf[:], -0.5).then_inc(cleared, 1)
                pool.wait_ge(cleared, 4)
                pool.wait_ge(loaded_rot, 16 * DMAS_ROT)
                raw = slice((LAYERS - 1) * WPB, LAYERS * WPB)
                for n in range(4):
                    for l in range(LAYERS):
                        wait(pool, rot_scaled, LAYERS * n + l)
                        nc.gpsimd.tensor_tensor(rot_all[:, n, l * WPB:(l + 1) * WPB, :], rot_all[:, n, raw, :],
                                                head_scale[:, n // 2, n % 2, l:l + 1, :].to_broadcast([P, WPB, DH]), ALU.mult).then_inc(rot_scaled, 1)
                pool.wait_ge(top_ready, LAYERS)
                nc.gpsimd.partition_all_reduce(top_all[:], top[:], P, RED_MAX).then_inc(top_shared, 1)
                pool.wait_ge(top_shared, 1)

            @block.tensor
            def _(pe):
                pe.wait_ge(loaded_ln, 32)
                pe.wait_ge(cleared, 1)
                for l in range(LAYERS):
                    pe.wait_ge(loaded_w1[l], 48)
                    for c in range(W1_BLOCKS):
                        for k in range(KD):
                            last = nc.tensor.matmul(ps[:, l, c:c + 1], w1_f[:, l, k, c * P:(c + 1) * P], lb[:, l, k:k + 1], start=(k == 0), stop=(k == KD - 1))
                    last.then_inc(bias_done, 1)

            @block.scalar
            def _(act):
                act.wait_ge(loaded_qkv, 16)
                for l in range(LAYERS):
                    nc.scalar.copy(wqkv[:, l, 0], wqkv_f[:, l]).then_inc(qkv_hi, 1)
                act.wait_ge(loaded_wo, 16)
                for l in range(LAYERS):
                    nc.scalar.copy(wo[:, l, 0], wo_f[:, l]).then_inc(wo_hi, 1)
                act.wait_ge(scale_ready, 1)
                for l in range(LAYERS):
                    nc.scalar.activation(w1[:, l, 0], w1_f[:, l], ACT.Copy, scale=w1_scale[:, l:l + 1]).then_inc(w1_hi, 1)
                act.wait_ge(loaded, 16 * DMAS)
                act.wait_ge(cleared, 4)
                for l in range(LAYERS):
                    nc.scalar.activation(w2[:, l], w2[:, l], ACT.Copy, scale=w1_unit[:, l:l + 1])

            @block.vector
            def _(dve):
                dve.wait_ge(loaded_ln, 32)
                for l in range(LAYERS):
                    dve.wait_ge(bias_done, l + 1)
                    for k in range(KD):
                        nc.vector.tensor_scalar(w1_f[:, l, k, :], w1_f[:, l, k, :], lg[:, l, k:k + 1], None, ALU.mult).then_inc(w1_gained, 1)
                    dve.wait_ge(w1_gained, KD * (l + 1))
                    nc.vector.tensor_reduce(top[:, l:l + 1], w1_f[:, l].rearrange("p k n -> p (k n)"), AX.X, ALU.max, apply_absolute_value=True).then_inc(top_ready, 1)
                dve.wait_ge(top_shared, 1)
                nc.vector.tensor_scalar(top_min[:], top_all[:], 1e-30, None, ALU.max).then_inc(step, 1)
                dve.wait_ge(step, 1)
                nc.vector.tensor_scalar(pow2[:].bitcast(I32), top_min[:].bitcast(I32), 0x7F800000, None, ALU.bitwise_and).then_inc(step, 1)
                dve.wait_ge(step, 2)
                nc.vector.reciprocal(pow2_inv[:], pow2[:]).then_inc(step, 1)
                nc.vector.tensor_scalar(w1_unit[:], pow2[:], 1.0 / W1_TOP, None, ALU.mult).then_inc(step, 1)
                dve.wait_ge(step, 4)
                nc.vector.tensor_scalar(w1_scale[:], pow2_inv[:], W1_TOP, None, ALU.mult).then_inc(scale_ready, 1)
                for l in range(LAYERS):
                    dve.wait_ge(qkv_hi, l + 1)
                    nc.vector.tensor_tensor(wqkv[:, l, 1], wqkv_f[:, l], wqkv[:, l, 0], ALU.subtract)
                    dve.wait_ge(wo_hi, l + 1)
                    nc.vector.tensor_tensor(wo[:, l, 1], wo_f[:, l], wo[:, l, 0], ALU.subtract)
                dve.wait_ge(scale_ready, 1)
                for l in range(LAYERS):
                    dve.wait_ge(w1_hi, l + 1)
                    nc.vector.scalar_tensor_tensor(w1[:, l, 1], w1_f[:, l], w1_scale[:, l:l + 1], w1[:, l, 0], ALU.mult, ALU.subtract)
                dve.wait_ge(loaded, 16 * DMAS)
                nc.vector.tensor_copy(ident_h[:], ident_f[:])
                nc.vector.tensor_copy(mask[:], mask_f[:])
                for l in range(LAYERS):
                    nc.vector.tensor_tensor(b1[:, l, :], ps[:, l, 0:W1_BLOCKS], b1_f[:, l, :], ALU.add).then_inc(bias_added, 1)
                for l in range(LAYERS):
                    dve.wait_ge(bias_added, l + 1)
                    nc.vector.tensor_scalar(b1a[:, l, :], b1[:, l, 0:HC], w1_scale[:, l:l + 1], None, ALU.mult)

        with ExitStack() as ctx:
            def sb(name, shape, dt=F32):
                return ctx.enter_context(nc.sbuf_tensor("b_" + name, shape, dt))

            def sem(name):
                return ctx.enter_context(nc.semaphore("b_" + name))

            rot = sb("rot", [P, 2, 4, DH])
            hx = sb("hx", [P, 2, D])
            xr = sb("xr", [P, 2, D])
            hT_hi, hT_lo = sb("hT_hi", [P, KD, P], F32R), sb("hT_lo", [P, KD, P], F32R)
            v = sb("v", [P, 4, INNER])
            kT = sb("kT", [P, HEADS, 2 * P], F32R)
            kT_low = sb("kT_low", [P, HEADS, 2 * P], F32R)
            sq = sb("sq", [P, 2 * HEADS, DH])
            ss_min = sb("ss_min", [P, 2 * HEADS])
            rn = sb("rn", [P, 2, 2 * HEADS])
            t1, t2 = sb("t1", [P, 2, INNER]), sb("t2", [P, 2, INNER])
            qr, kr = sb("qr", [P, INNER]), sb("kr", [P, INNER])
            qT = sb("qT", [P, HEADS, P], F32R)
            negmax = sb("negmax", [P, HEADS])
            mask_now = sb("mask_now", [P, 2 * P], BF16)
            probs = sb("probs", [P, HEADS, 2 * P])
            rowsum, rinv = sb("rowsum", [P, HEADS]), sb("rinv", [P, HEADS])
            probsT = sb("probsT", [P, HP, 512])
            oT = sb("oT", [P, 2, HP, P], F32R)
            xp = sb("xp", [P, 2, D])
            xb = sb("xb", [P, 4, D])
            h2 = sb("h2", [P, 2, D])
            st2, mv2, var2, rstd2 = sb("st2", [P, 6]), sb("mv2", [P, 2]), sb("var2", [P, 1]), sb("rstd2", [P, 1])
            xh, xh_hl = sb("xh", [P, D]), sb("xh_hl", [P, 2, D], F16)
            h2T = sb("h2T", [P, 2, KD, 2 * P], F16)
            gl = sb("gl", [P, 2, 2 * P])
            hid = sb("hid", [P, HC, 2 * P])
            xpp = sb("xpp", [P, 2, D])
            stf, mvf = sb("stf", [P, 2, 6]), sb("mvf", [P, 2, 2])
            varf, rstdf = sb("varf", [P, 2]), sb("rstdf", [P, 2])
            x2 = sb("x2", [P, 2, D])
            fin = sb("fin", [P, 2, D])

            rot_loaded, passed_dve, passed_sp = sem("rot_loaded"), sem("passed_dve"), sem("passed_sp")
            hx_loaded, xr_loaded, h2_loaded, x2_loaded = (sem(n) for n in ("hx_loaded", "xr_loaded", "h2_loaded", "x2_loaded"))
            xp_stored, xpp_stored, fin_stored = (sem(n) for n in ("xp_stored", "xpp_stored", "fin_stored"))
            hT_done, hT_hi_kept, hT_lo_kept = (sem(n) for n in ("hT_done", "hT_hi_kept", "hT_lo_kept"))
            v_done, q_done, k_done, v_kept = (sem(n) for n in ("v_done", "q_done", "k_done", "v_kept"))
            q_sq, k_sq = sem("q_sq"), sem("k_sq")
            q_terms, k_terms = sem("q_terms"), sem("k_terms")
            ss_halved, ss_ready, rn_ready = sem("ss_halved"), sem("ss_ready"), sem("rn_ready")
            qr_ready, kr_sum, kr_ready = sem("qr_ready"), sem("kr_sum"), sem("kr_ready")
            kT_done, qT_done, kT_hi, kT_lo, qT_hi, qT_lo = (sem(n) for n in (
                "kT_done", "qT_done", "kT_hi", "kT_lo", "qT_hi", "qT_lo"))
            kT_both = sem("kT_both")
            scores_done, mask_ready = sem("scores_done"), sem("mask_ready")
            scores_kept, exp_done = sem("scores_kept"), sem("exp_done")
            rinv_ready, probs_ready = sem("rinv_ready"), sem("probs_ready")
            pT_done, pT_kept = sem("pT_done"), sem("pT_kept")
            pv_done, oT_hi, oT_lo, wo_done, xp_ready, xb_ready = (sem(n) for n in ("pv_done", "oT_hi", "oT_lo", "wo_done", "xp_ready", "xb_ready"))
            st2_ready, mv2_ready, var2_ready, rstd2_ready = (sem(n) for n in ("st2_ready", "mv2_ready", "var2_ready", "rstd2_ready"))
            xh_ready, xh_hi, xh_lo, h2T_done, h2T_kept = (sem(n) for n in ("xh_ready", "xh_hi", "xh_lo", "h2T_done", "h2T_kept"))
            w1_done, gelu_done, hid_ready = sem("w1_done"), sem("gelu_done"), sem("hid_ready")
            w2_done, xpp_ready = sem("w2_done"), sem("xpp_ready")
            stf_ready, mvf_ready, varf_ready = sem("stf_ready"), sem("mvf_ready"), sem("varf_ready")
            rstdf_ready, xf_ready, fin_ready = sem("rstdf_ready"), sem("xf_ready"), sem("fin_ready")
            ps_h2T = ps[:, 7, 0:D].bitcast(F16).rearrange("p (a k n) -> p a k n", a=2, k=KD)
            vk_cleared = sem("vk_cleared")
            block = ctx.enter_context(nc.Block())

            def by_head(ap):
                return ap.rearrange("p (h d) -> p h d", d=DH)

            half_rows = [slice(h * DH, (h + 1) * DH) for h in range(2)]

            def by_pair(ap):
                return ap.rearrange("p (h n) -> p h n", h=HP)

            @block.sync
            def _(sp):
                def load_hx(t, parity):
                    n = stream_block(t)
                    sp.dma_start(hx[:, parity, 0:HALF], xs_v[:, ds(n, 1), 0:HALF]).then_inc(hx_loaded, 16)
                    sp.dma_start(hx[:, parity, HALF:D], xs_prev[:, ds(n - 1, 1), HALF:D]).then_inc(hx_loaded, 16)

                def load_rot(t, parity):
                    sp.dma_start(rot[:, parity], rot_v[:, ds((t // NW) * WPB + t % WPB, 1), :]).then_inc(rot_loaded, 16)

                load_hx(0, 0)
                load_rot(0, 0)

                def run(s, r, pairs, layer):
                    j = pairs - 3
                    f = j - NW // 2
                    if r % 2 == 0 and in_range(2 * j) and layer(2 * j) == 0:
                        wait_apart(sp, xpp_ready, 2 * j + 2, passed_sp)
                        wait(sp, xpp_stored, 16 * j)
                        sp.dma_start(xs_v[:, ds(stream_block(2 * j + NW), 2), :], xpp[:]).then_inc(xpp_stored, 16)
                    if r % 2 == 0 and in_range(2 * j - 2) and layer(2 * j - 2) == 1:
                        wait_apart(sp, fin_ready, f, passed_sp)
                        sp.dma_start(out_v[:, ds(2 * f - 2, 2), :], fin[:]).then_inc(fin_stored, 16)
                    if r % 2 == 0 and in_range(2 * j) and layer(2 * j) == 1:
                        wait(sp, x2_loaded, 16 * f)
                        sp.dma_start(x2[:], x2_v[:, ds(2 * f, 2), :]).then_inc(x2_loaded, 16)
                    if in_range(s + 1):
                        wait(sp, hT_done, s)
                        sp.wait_ge(hx_loaded, 32 * (s + 1))
                        load_hx(s + 1, (r + 1) % 2)
                        wait_apart(sp, k_terms, 3 * s, passed_sp)
                        sp.wait_ge(rot_loaded, 16 * (s + 1))
                        load_rot(s + 1, (r + 1) % 2)
                    t = s - 1
                    if in_range(t):
                        wait_apart(sp, xp_ready, t - 1, passed_sp)
                        wait(sp, xr_loaded, 16 * t)
                        sp.dma_start(xr[:, (r - 1) % 2, :], xs_v[:, ds(stream_block(t), 1), :]).then_inc(xr_loaded, 16)
                    t = s - 2
                    if in_range(t):
                        n = stream_block(t)
                        sp.wait_ge(xp_ready, t + 1)
                        sp.dma_start(xp_v[:, ds(n, 1), :], xp[:, r % 2, :]).then_inc(xp_stored, 16)
                        wait_apart(sp, xp_stored, 16 * (t + 1), passed_sp)
                        wait_apart(sp, xh_ready, t - 1, passed_sp)
                        wait(sp, h2_loaded, 32 * t)
                        sp.dma_start(h2[:, r % 2, 0:HALF], xp_v[:, ds(n, 1), 0:HALF]).then_inc(h2_loaded, 16)
                        sp.dma_start(h2[:, r % 2, HALF:D], xp_prev[:, ds(n - 1, 1), HALF:D]).then_inc(h2_loaded, 16)

                slots(sp, run)
                sp.wait_ge(xpp_stored, 16 * (NW // 2))
                sp.wait_ge(fin_stored, 16 * (NW // 2))

            @block.tensor
            def _(pe):
                def transpose_hx(t, r):
                    pe.wait_ge(hx_loaded, 32 * (t + 1))
                    wait(pe, h2T_kept, t - 3)
                    for k in range(KD):
                        last = nc.tensor.transpose(ps[:, 7, k * P:(k + 1) * P], hx[:, r % 2, k * P:(k + 1) * P], ident_f[:])
                    last.then_inc(hT_done, 1)

                def transpose_h2(t):
                    if in_range(t):
                        pe.wait_ge(xh_hi, t + 1)
                        pe.wait_ge(xh_lo, t + 1)
                        if in_range(t + 1):
                            pe.wait_ge(oT_lo, t + 2)
                        else:
                            pe.wait_ge(h2T_kept, t)
                        for part in range(2):
                            for k in range(KD):
                                last = nc.tensor.transpose(ps_h2T[:, part, k, :], xh_hl[:, part, k * P:(k + 1) * P], ident_h[:])
                        last.then_inc(h2T_done, 1)

                def run(s, r, pairs, layer):
                    t = s - 1
                    if in_range(t):
                        pe.wait_ge(qr_ready, t + 1)
                        pe.wait_ge(v_kept, t + 1)
                        wait(pe, xp_ready, s - 2)
                        for p in range(HP):
                            last = nc.tensor.transpose(ps[:, 2, p * P:(p + 1) * P], qr[:, p * P:(p + 1) * P], ident_f[:])
                        last.then_inc(qT_done, 1)
                        pe.wait_ge(kr_ready, t + 1)
                        wait(pe, scores_kept, HEADS * t)
                        if r % 2 == 1:
                            wait(pe, hid_ready, HC * (pairs - 2) + W1_BANKS.index(6) + 1)
                        for p in range(HP):
                            last = nc.tensor.transpose(ps[:, 6, p * P:(p + 1) * P], kr[:, p * P:(p + 1) * P], ident_f[:])
                        last.then_inc(kT_done, 1)
                    if in_range(s):
                        pe.wait_ge(hT_hi_kept, s + 1)
                        pe.wait_ge(hT_lo_kept, s + 1)
                        for bank, done in ((0, q_done), (1, k_done), (2, v_done)):
                            if bank == 2:
                                wait(pe, qT_lo, 2 * s)
                            else:
                                wait(pe, (q_terms, k_terms)[bank], 3 * s)
                                if r % 2 == 1:
                                    wait(pe, hid_ready, HC * (pairs - 2) + bank + 1)
                            for k in range(KD):
                                for a, hT, part in ((0, hT_hi, 0), (1, hT_hi, 1), (2, hT_lo, 0)):
                                    last = nc.tensor.matmul(ps[:, bank, :], hT[:, k, :],
                                                            wqkv[:, ds(layer(s), 1), part, k, bank * INNER:(bank + 1) * INNER],
                                                            start=(k == 0 and a == 0), stop=(k == KD - 1 and a == 2))
                            last.then_inc(done, 1)
                    t = s - 2
                    if in_range(t):
                        if r % 2 == 0:
                            wait(pe, xpp_ready, s - 4)
                        else:
                            wait(pe, hid_ready, HC * (pairs - 1))
                        for p in range(HP):
                            if p == HP - 1 and in_range(s - 1):
                                pe.wait_ge(kT_lo, 2 * s)
                            pe.wait_ge(probs_ready, HEADS * t + 2 * p + 2)
                            for n in range(4):
                                last = nc.tensor.transpose(ps[:, 3 + p, n * P:(n + 1) * P],
                                                           probs[:, 2 * p + n // 2, (n % 2) * P:(n % 2 + 1) * P], ident_f[:])
                            last.then_inc(pT_done, 1)
                        pe.wait_ge(v_kept, t + 1)
                        if not in_range(s):
                            pe.wait_ge(h2T_kept, s - 3)
                        for p in range(HP):
                            pe.wait_ge(pT_kept, HP * t + p + 1)
                            for c in range(2):
                                window = (r - 2 - (r + c) % 2) % 4
                                for h in range(2):
                                    last = nc.tensor.matmul(ps[h * DH:(h + 1) * DH, 7, p * P:(p + 1) * P],
                                                            v[:, window, (2 * p + h) * DH:(2 * p + h + 1) * DH],
                                                            probsT[:, p, (2 * h + c) * P:(2 * h + c + 1) * P],
                                                            start=(c == 0), stop=(c == 1))
                        last.then_inc(pv_done, 1)
                    t = s - 1
                    if in_range(t):
                        pe.wait_ge(kT_lo, 2 * (t + 1))
                        pe.wait_ge(kT_both, 2 * (t + 1))
                        pe.wait_ge(qT_lo, 2 * (t + 1))
                        for p in range(HP):
                            for h in range(2):
                                scores = ps[:, 3 + p, h * 2 * P:(h + 1) * 2 * P]
                                nc.tensor.matmul(scores, qT[:, 2 * p + h, :], kT[:, 2 * p + h, :], start=True, stop=False)
                                last = nc.tensor.matmul(scores, qT[:, 2 * p + h, :], kT_low[:, 2 * p + h, :], start=False, stop=True)
                            last.then_inc(scores_done, 1)
                    transpose_h2(s - 3)
                    t = s - 2
                    if in_range(t):
                        pe.wait_ge(oT_lo, t + 1)
                        if in_range(s):
                            pe.wait_ge(v_kept, s + 1)
                        else:
                            pe.wait_ge(xp_ready, s - 2)
                        for p in range(HP):
                            for a, (op, wp) in enumerate(PARTS):
                                last = nc.tensor.matmul(ps[:, 2, 0:D], oT[:, op, p, :], wo[:, ds(layer(t), 1), wp, p, :],
                                                        start=(p == 0 and a == 0), stop=(p == HP - 1 and a == 2))
                        last.then_inc(wo_done, 1)
                    if in_range(s + 1):
                        transpose_hx(s + 1, r + 1)
                    j = pairs - 2
                    if r % 2 == 0 and in_range(2 * j):
                        pe.wait_ge(h2T_kept, 2 * j + 2)
                        if not in_range(s - 2):
                            pe.wait_ge(xpp_ready, s - 4)
                        for c, bank in enumerate(W1_BANKS):
                            if bank < 2 and in_range(s):
                                pe.wait_ge((q_terms, k_terms)[bank], 3 * (s + 1))
                            if bank > 2 and in_range(s - 1):
                                pe.wait_ge(scores_kept, HEADS * (s - 1) + 2 * (bank - 3) + 2)
                            for half in range(1 if c == FULL else 2):
                                for k in range(KD):
                                    for a, (wp, hp) in enumerate(PARTS):
                                        first = (half * HC + c) * P
                                        last = nc.tensor.matmul(ps[:, bank, half * 2 * P:(half + 1) * 2 * P],
                                                                w1[:, ds(layer(2 * j), 1), wp, k, first:first + P], h2T[:, hp, k, :],
                                                                start=(k == 0 and a == 0), stop=(k == KD - 1 and a == 2))
                            last.then_inc(w1_done, 1)
                    if r % 2 == 1 and in_range(2 * j):
                        pe.wait_ge(hid_ready, HC * (j + 1))
                        if in_range(s - 1):
                            pe.wait_ge(scores_kept, HEADS * (s - 1) + 2)
                        for n in range(2):
                            for c in range(HC):
                                last = nc.tensor.matmul(ps[:, 3, n * D:(n + 1) * D], hid[:, c, n * P:(n + 1) * P], w2[:, ds(layer(2 * j), 1), c, :],
                                                        start=(c == 0), stop=(c == HC - 1))
                        last.then_inc(w2_done, 1)

                transpose_hx(0, 0)
                slots(pe, run)

            @block.scalar
            def _(act):
                def keep_hT(t):
                    act.wait_ge(hT_done, t + 1)
                    wait(act, k_done, t)
                    nc.scalar.copy(hT_hi[:], ps[:, 7, 0:D].rearrange("p (k n) -> p k n", k=KD)).then_inc(hT_hi_kept, 1)

                def keep_h2T(t, r, pairs):
                    if in_range(t):
                        act.wait_ge(h2T_done, t + 1)
                        if r % 2 == 1:
                            wait(act, w1_done, HC * (pairs - 1))
                        n = (r - 3) % 2
                        nc.scalar.copy(h2T[:, :, :, n * P:(n + 1) * P], ps_h2T).then_inc(h2T_kept, 1)

                def run(s, r, pairs, layer):
                    t = s - 1
                    if in_range(t):
                        act.wait_ge(qT_done, t + 1)
                        wait(act, scores_done, HP * t)
                        for h, rows in enumerate(half_rows):
                            nc.scalar.copy(qT[rows, h::2, :], by_pair(ps[rows, 2, :])).then_inc(qT_hi, 1)
                        act.wait_ge(kT_done, t + 1)
                        par = (r - 1) % 2
                        for h, rows in enumerate(half_rows):
                            nc.scalar.copy(kT[rows, h::2, par * P:(par + 1) * P], by_pair(ps[rows, 6, :])).then_inc(kT_hi, 1)
                        for h, rows in enumerate(half_rows):
                            act.wait_ge(kT_hi, 2 * t + h + 1)
                            nc.scalar.copy(kT[half_rows[1 - h], h::2, par * P:(par + 1) * P], kT[rows, h::2, par * P:(par + 1) * P]).then_inc(kT_both, 1)
                    if in_range(s):
                        wait(act, ss_ready, s)
                        act.wait_ge(q_done, s + 1)
                        nc.scalar.activation(sq[:, 0:HEADS, :], by_head(ps[:, 0, :]), ACT.Square).then_inc(q_sq, 1)
                        act.wait_ge(k_done, s + 1)
                        nc.scalar.activation(sq[:, HEADS:2 * HEADS, :], by_head(ps[:, 1, :]), ACT.Square).then_inc(k_sq, 1)
                        act.wait_ge(v_done, s + 1)
                        wait(act, pv_done, s - 2)
                        nc.scalar.copy(v[:, r, :], ps[:, 2, :]).then_inc(v_kept, 1)
                    t = s - 2
                    if in_range(t):
                        wait(act, pv_done, t)
                        for p in range(HP):
                            act.wait_ge(pT_done, HP * t + p + 1)
                            nc.scalar.copy(probsT[:, p, :], ps[:, 3 + p, :]).then_inc(pT_kept, 1)
                        act.wait_ge(pv_done, t + 1)
                        wait(act, wo_done, t)
                        nc.scalar.copy(oT[:, 0], by_pair(ps[:, 7, :])).then_inc(oT_hi, 1)
                    t = s - 1
                    if in_range(t):
                        for p in range(HP):
                            if p == H2T_AT:
                                keep_h2T(s - 3, r, pairs)
                            for h in range(2 * p, 2 * p + 2):
                                act.wait_ge(scores_kept, HEADS * t + h + 1)
                                nc.scalar.activation(probs[:, h, :], probs[:, h, :], ACT.Exp, bias=negmax[:, h:h + 1], scale=-1.0,
                                                     accum_out=rowsum[:, h:h + 1]).then_inc(exp_done, 1)
                    else:
                        keep_h2T(s - 3, r, pairs)
                    if in_range(s + 1):
                        keep_hT(s + 1)
                    j = pairs - 2
                    if r % 2 == 0 and in_range(2 * j):
                        for c, bank in enumerate(W1_BANKS):
                            wait(act, hid_ready, HC * j + c - 1)
                            act.wait_ge(w1_done, HC * j + c + 1)
                            if c < FULL:
                                rows, kept, block, columns = slice(0, P), slice(0, P), HC + c, slice(2 * P, 4 * P)
                            else:
                                rows, kept, block, columns = slice(SECOND_REST, SECOND_REST + REST), slice(0, REST), FULL, slice(0, 2 * P)
                            nc.scalar.activation(gl[kept, c % 2, :], ps[rows, bank, columns], ACT.Gelu,
                                                 bias=b1[rows, ds(layer(2 * j), 1), block], scale=w1_unit[rows, ds(layer(2 * j), 1)]).then_inc(gelu_done, 1)

                keep_hT(0)
                act.wait_ge(vk_cleared, 4)
                slots(act, run)

            @block.vector
            def _(dve):
                def keep_hT(t):
                    dve.wait_ge(hT_hi_kept, t + 1)
                    nc.vector.tensor_tensor(hT_lo[:], ps[:, 7, 0:D].rearrange("p (k n) -> p k n", k=KD), hT_hi[:], ALU.subtract).then_inc(hT_lo_kept, 1)

                def rotate(s, r, n, squared, terms, used):
                    if in_range(s):
                        dve.wait_ge(rot_loaded, 16 * (s + 1))
                        dve.wait_ge(squared, s + 1)
                        wait(dve, used, s)
                        x = by_head(ps[:, n, :])
                        half = DH // 2

                        def factor(which, lo, hi):
                            return rot[:, r % 2, which:which + 1, lo:hi].to_broadcast([P, HEADS, hi - lo])

                        t2_h = by_head(t2[:, n, :])
                        nc.vector.tensor_tensor(by_head(t1[:, n, :]), x, factor(2 * n, 0, DH), ALU.mult).then_inc(terms, 1)
                        nc.vector.tensor_tensor(t2_h[:, :, 0:half], x[:, :, half:DH], factor(2 * n + 1, 0, half), ALU.mult).then_inc(terms, 1)
                        nc.vector.tensor_tensor(t2_h[:, :, half:DH], x[:, :, 0:half], factor(2 * n + 1, half, DH), ALU.mult).then_inc(terms, 1)

                def floor_norms(s):
                    if in_range(s):
                        dve.wait_ge(ss_halved, HALVINGS * (s + 1))
                        wait(dve, rn_ready, s)
                        nc.vector.tensor_scalar(ss_min[:], sq[:, :, 0], 1e-24, None, ALU.max).then_inc(ss_ready, 1)

                def layer_output(j, r, layer):
                    if r % 2 == 0 and in_range(2 * j):
                        dve.wait_ge(w2_done, j + 1)
                        if layer(2 * j) == 0:
                            wait(dve, xpp_stored, 16 * j)
                        else:
                            dve.wait_ge(xpp_stored, 16 * (NW // 2))
                            wait(dve, xf_ready, 2 * (j - NW // 2))
                        for n in range(2):
                            dve.wait_ge(xb_ready, 2 * j + n + 1)
                            nc.vector.tensor_tensor(xpp[:, n, :], ps[:, 3, n * D:(n + 1) * D], xb[:, (r - 6 + n) % 4, :], ALU.add).then_inc(xpp_ready, 1)

                def output_stats(j, r, layer):
                    f = j - NW // 2
                    if r % 2 == 1 and in_range(2 * j) and layer(2 * j) == 1:
                        for n in range(2):
                            dve.wait_ge(xpp_ready, 2 * j + n + 1)
                            nc.vector.bn_stats(stf[:, n, :], xpp[:, n, :]).then_inc(stf_ready, 1)
                        for n in range(2):
                            wait_apart(dve, stf_ready, 2 * f + n + 1, passed_dve)
                            nc.vector.bn_aggr(mvf[:, n, :], stf[:, n, :]).then_inc(mvf_ready, 1)
                        dve.wait_ge(mvf_ready, 2 * f + 2)
                        nc.vector.tensor_scalar(varf[:], mvf[:, :, 1], EPS, None, ALU.add).then_inc(varf_ready, 1)

                def output_norm(j, r, layer):
                    f = j - NW // 2
                    if r % 2 == 1 and in_range(2 * j) and layer(2 * j) == 1:
                        dve.wait_ge(rstdf_ready, f + 1)
                        wait(dve, fin_stored, 16 * f)
                        for n in range(2):
                            nc.vector.tensor_scalar(fin[:, n, :], xpp[:, n, :], mvf[:, n, 0:1], rstdf[:, n:n + 1],
                                                    ALU.subtract, ALU.mult).then_inc(xf_ready, 1)

                def oT_low(t):
                    if in_range(t):
                        dve.wait_ge(oT_hi, t + 1)
                        nc.vector.tensor_tensor(oT[:, 1], by_pair(ps[:, 7, :]), oT[:, 0], ALU.subtract).then_inc(oT_lo, 1)

                def run(s, r, pairs, layer):
                    t = s - 1
                    if in_range(t):
                        par = (r - 1) % 2
                        for h, rows in enumerate(half_rows):
                            dve.wait_ge(qT_hi, 2 * t + h + 1)
                            nc.vector.tensor_tensor(qT[half_rows[1 - h], h::2, :], by_pair(ps[rows, 2, :]), qT[rows, h::2, :], ALU.subtract).then_inc(qT_lo, 1)
                        for h, rows in enumerate(half_rows):
                            dve.wait_ge(kT_hi, 2 * t + h + 1)
                            nc.vector.tensor_tensor(kT_low[rows, h::2, par * P:(par + 1) * P], by_pair(ps[rows, 6, :]), kT[rows, h::2, par * P:(par + 1) * P],
                                                    ALU.subtract).then_inc(kT_lo, 1)
                    layer_output(pairs - 3, r, layer)
                    t = s - 3
                    if in_range(t):
                        dve.wait_ge(h2_loaded, 32 * (t + 1))
                        nc.vector.bn_stats(st2[:], h2[:, (r - 3) % 2, :]).then_inc(st2_ready, 1)
                        wait_apart(dve, st2_ready, t + 1, passed_dve)
                        nc.vector.bn_aggr(mv2[:], st2[:]).then_inc(mv2_ready, 1)
                        dve.wait_ge(mv2_ready, t + 1)
                        nc.vector.tensor_scalar(var2[:], mv2[:, 1:2], EPS, None, ALU.add).then_inc(var2_ready, 1)
                    rotate(s, r, 0, q_sq, q_terms, qr_ready)
                    t = s - 3
                    if in_range(t):
                        dve.wait_ge(rstd2_ready, t + 1)
                        wait(dve, xh_lo, t)
                        nc.vector.tensor_scalar(xh[:], h2[:, (r - 3) % 2, :], mv2[:, 0:1], rstd2[:], ALU.subtract, ALU.mult).then_inc(xh_ready, 1)
                        dve.wait_ge(xh_ready, t + 1)
                        wait(dve, h2T_done, t)
                        nc.vector.tensor_copy(xh_hl[:, 0, :], xh[:]).then_inc(xh_hi, 1)
                    rotate(s, r, 1, k_sq, k_terms, kr_ready)
                    output_stats(pairs - 3, r, layer)
                    oT_low(s - 2)
                    t = s - 1
                    if in_range(t):
                        dve.wait_ge(rn_ready, t + 1)
                        which = mask_now[:] if r == 1 else mask[:, EVEN_MASK if r == 3 else ODD_MASK, :]
                        if r == 1:
                            dve.wait_ge(mask_ready, t // SLOTS + 1)
                        wait(dve, pT_done, HP * t)
                        for p in range(HP):
                            if p == HP - 1:
                                floor_norms(s)
                            wait_apart(dve, scores_done, HP * t + p + 1, passed_dve)
                            for h in range(2 * p, 2 * p + 2):
                                nc.vector.tensor_tensor_reduce(probs[:, h, :], ps[:, 3 + p, (h % 2) * 2 * P:(h % 2 + 1) * 2 * P], which,
                                                               rn[:, (r - 1) % 2, h:h + 1], ABOVE_ALL, ALU.add, ALU.min,
                                                               negmax[:, h:h + 1]).then_inc(scores_kept, 1)
                    else:
                        floor_norms(s)

                    def normalise(p):
                        t = s - 1
                        if in_range(t):
                            dve.wait_ge(exp_done, HEADS * t + 2 * p + 2)
                            nc.vector.reciprocal(rinv[:, 2 * p:2 * p + 2], rowsum[:, 2 * p:2 * p + 2]).then_inc(rinv_ready, 1)
                            dve.wait_ge(rinv_ready, HP * t + p + 1)
                            for h in range(2 * p, 2 * p + 2):
                                nc.vector.tensor_scalar(probs[:, h, :], probs[:, h, :], rinv[:, h:h + 1], None, ALU.mult).then_inc(probs_ready, 1)

                    normalise(0)
                    normalise(1)
                    t = s - 2
                    if in_range(t):
                        dve.wait_ge(wo_done, t + 1)
                        dve.wait_ge(xr_loaded, 16 * (t + 1))
                        wait(dve, xp_stored, 16 * (t - 1))
                        wait(dve, xb_ready, t - 1)
                        nc.vector.tensor_tensor(xp[:, r % 2, :], ps[:, 2, 0:D], xr[:, r % 2, :], ALU.add).then_inc(xp_ready, 1)
                    normalise(2)
                    if in_range(s + 1):
                        keep_hT(s + 1)
                    normalise(3)
                    output_norm(pairs - 3, r, layer)
                    j = pairs - 2
                    if r % 2 == 0 and in_range(2 * j):
                        wait(dve, w2_done, j)
                        for c, bank in enumerate(W1_BANKS):
                            dve.wait_ge(gelu_done, HC * j + c + 1)
                            rows = slice(0, P if c < FULL else REST)
                            nc.vector.scalar_tensor_tensor(hid[rows, c, :], ps[rows, bank, 0:2 * P], b1a[rows, ds(layer(2 * j), 1), c], gl[rows, c % 2, :],
                                                           ALU.add, ALU.mult).then_inc(hid_ready, 1)

                keep_hT(0)
                slots(dve, run)

            @block.gpsimd
            def _(pool):
                def run(s, r, pairs, layer):
                    if r == 0 and in_range(s):
                        wait(pool, scores_kept, HEADS * (s - 3))
                        nc.gpsimd.tensor_copy(mask_now[:], mask[:, ds((s // SLOTS) % (WPB // SLOTS), 1), :]).then_inc(mask_ready, 1)
                    t = s - 3
                    if in_range(t):
                        pool.wait_ge(var2_ready, t + 1)
                        nc.gpsimd.tensor_tensor(rstd2[:], var2[:], mhalf[:, 0:1], ALU.pow).then_inc(rstd2_ready, 1)
                        pool.wait_ge(xh_hi, t + 1)
                        nc.gpsimd.tensor_tensor(xh_hl[:, 1, :], xh[:], xh_hl[:, 0, :], ALU.subtract).then_inc(xh_lo, 1)
                    if in_range(s):
                        pool.wait_ge(q_terms, 3 * (s + 1))
                        wait(pool, qT_done, s)
                        nc.gpsimd.tensor_tensor(qr[:], t1[:, 0, :], t2[:, 0, :], ALU.add).then_inc(qr_ready, 1)
                        pool.wait_ge(k_sq, s + 1)
                        for n in range(HALVINGS):
                            width = DH >> (n + 1)
                            target = sq[:, :, 0:width]
                            wait(pool, ss_halved, HALVINGS * s + n)
                            nc.gpsimd.tensor_tensor(target, target, sq[:, :, width:2 * width], ALU.add).then_inc(ss_halved, 1)
                        pool.wait_ge(k_terms, 3 * (s + 1))
                        nc.gpsimd.tensor_tensor(t1[:, 1, :], t1[:, 1, :], t2[:, 1, :], ALU.add).then_inc(kr_sum, 1)
                        pool.wait_ge(ss_ready, s + 1)
                        wait(pool, scores_kept, HEADS * (s - 1))
                        nc.gpsimd.tensor_tensor(rn[:, r % 2, :], ss_min[:], mhalf[:], ALU.pow).then_inc(rn_ready, 1)
                    j = pairs - 3
                    f = j - NW // 2
                    if r % 2 == 1 and in_range(2 * j) and layer(2 * j) == 1:
                        pool.wait_ge(varf_ready, f + 1)
                        nc.gpsimd.tensor_tensor(rstdf[:], varf[:], mhalf[:, 0:2], ALU.pow).then_inc(rstdf_ready, 1)
                    if in_range(s):
                        pool.wait_ge(rn_ready, s + 1)
                        pool.wait_ge(kr_sum, s + 1)
                        wait(pool, kT_done, s)
                        nc.gpsimd.tensor_tensor(by_head(kr[:]), by_head(t1[:, 1, :]),
                                                rn[:, r % 2, HEADS:2 * HEADS].unsqueeze(2).to_broadcast([P, HEADS, DH]), ALU.mult).then_inc(kr_ready, 1)
                    t = s - 2
                    if in_range(t):
                        pool.wait_ge(xp_ready, t + 1)
                        wait(pool, xpp_ready, t - 3)
                        nc.gpsimd.tensor_tensor(xb[:, (r - 2) % 4, :], xp[:, r % 2, :], b2[:, ds(layer(t), 1), :], ALU.add).then_inc(xb_ready, 1)
                    j = pairs - 3
                    f = j - NW // 2
                    if r % 2 == 1 and in_range(2 * j) and layer(2 * j) == 1:
                        pool.wait_ge(xf_ready, 2 * f + 2)
                        pool.wait_ge(x2_loaded, 16 * (f + 1))
                        nc.gpsimd.tensor_tensor(fin[:], fin[:], x2[:], ALU.add).then_inc(fin_ready, 1)

                nc.gpsimd.memset(v[:], 0.0).then_inc(vk_cleared, 1)
                nc.gpsimd.memset(kT[:].bitcast(F32), 0.0).then_inc(vk_cleared, 1)
                nc.gpsimd.memset(kT_low[:].bitcast(F32), 0.0).then_inc(vk_cleared, 1)
                nc.gpsimd.memset(hid[:, FULL, :], 0.0).then_inc(vk_cleared, 1)
                slots(pool, run)


def build(nc, x, wqkv, q_scale, k_scale, wo, ln_g, ln_b, w1, b1, w2, b2, ident, rot, mask, out):
    x2_dram = nc.dram_tensor("x2_dram", [NW * P, D], F32).ap()
    xs_dram = nc.dram_tensor("xs_dram", [STREAM_BLOCKS * P, D], F32).ap()
    xp_dram = nc.dram_tensor("xp_dram", [STREAM_BLOCKS * P, D], F32).ap()
    rot_dram = nc.dram_tensor("rot_dram", [LAYERS * S, 4, DH], F32).ap()
    phase_a(nc, x, ident, x2_dram, xs_dram, xp_dram)
    weights = dict(wqkv=wqkv, q_scale=q_scale, k_scale=k_scale, wo=wo, ln_g=ln_g, ln_b=ln_b, w1=w1, b1=b1, w2=w2, b2=b2)
    phase_b(nc, weights, dict(ident=ident, rot=rot, mask=mask), x2_dram, xs_dram, xp_dram, rot_dram, out)


def rotary_tables():
    f = np.float32
    half = np.arange(0, DH, 2, dtype=f)
    inv_freq = f(1) / np.power(10000.0, (half / f(DH)).astype(np.float64)).astype(f)
    t = np.arange(S, dtype=f)
    freqs = t[:, None] * inv_freq[None, :]
    base = (half + f(0.4 * DH)) / f(1.4 * DH)
    power = (t - f(S // 2)) / f(P // 2)
    scale = np.power(base[None, :].astype(np.float64), power[:, None].astype(np.float64))
    cos, sin = np.cos(freqs.astype(np.float64)), np.sin(freqs.astype(np.float64))
    both = lambda lo, hi: np.concatenate([lo, hi], axis=1)
    tables = [both(cos, cos) * both(scale, scale) * -QK_SCALE, both(-sin, sin) * both(scale, scale) * -QK_SCALE,
              both(cos, cos) / both(scale, scale), both(-sin, sin) / both(scale, scale)]
    return np.stack(tables).astype(f)


def window_masks():
    i, j = np.arange(P)[:, None], np.arange(P)[None, :]
    own, before = np.where(j <= i, 0.0, MASKED), np.where(j >= i, 0.0, MASKED)
    none = np.full((P, P), MASKED)
    kinds = [(own, none)] + (WPB // SLOTS - 1) * [(own, before)] + [(before, own)]
    return np.stack([np.concatenate(kind, axis=1) for kind in kinds]).astype(np.float32)


_INS = ["L0_attn_x", "L0_ffn_wqkv", "L0_ffn_q_scale", "L0_ffn_k_scale", "L0_ffn_wo", "L0_ffn_ln_g", "L0_ffn_ln_b", "L0_ffn_w1", "L0_ffn_b1",
        "L0_ffn_w2", "L0_ffn_b2"]


def kernel(**inputs):
    import concourse.bacc as bacc
    from concourse.bass_utils import run_bass_kernel_spmd

    nc = bacc.Bacc("TRN2", target_bir_lowering=False, num_devices=1)
    arrays = {f"in_{name}_dram": np.ascontiguousarray(inputs[name]) for name in _INS}
    arrays["in_ident_dram"] = np.eye(P, dtype=np.float32)
    arrays["in_rot_dram"] = rotary_tables()
    arrays["in_mask_dram"] = window_masks()
    args = [nc.dram_tensor(name, a.shape, mybir.dt.from_np(a.dtype), kind="ExternalInput").ap() for name, a in arrays.items()]
    out = nc.dram_tensor("out_0_dram", (B, S, D), F32, kind="ExternalOutput").ap()
    build(nc, *args, out)
    r = run_bass_kernel_spmd(nc, [arrays], core_ids=[0])
    return r.results[0]["out_0_dram"]
```
